# Optimizing a Trainium2 kernel written in Bass

```python
import numpy as np
import jax
import jax.numpy as jnp

def _softmax(x, axis=-1):
    return jax.nn.softmax(x, axis=axis)

def _gelu(x):
    return jax.nn.gelu(x, approximate=True)

def _silu(x):
    return jax.nn.silu(x)

def _sigmoid(x):
    return jax.nn.sigmoid(x)

def _layernorm(x, axis=-1, eps=1e-05):
    m = jnp.mean(x, axis=axis, keepdims=True)
    v = jnp.var(x, axis=axis, keepdims=True)
    return (x - m) / jnp.sqrt(v + eps)

def _scatter_add(tgt, idx, src, axis=0):
    return tgt.at[idx].add(src)

def _segment_sum(src, seg, n):
    return jax.ops.segment_sum(src, seg, n)
kernel_name = 'mk_adaln_attn_ffn_d1_seqx_r4_075c28'

def setup_inputs(seed: int=0):
    np.random.seed(seed)
    _w = jnp.asarray

    def _rec_inputs():
        import jax
        import jax.numpy as jnp
        _rk = jax.random.key(seed)
        x = -0.0002928 + 1 * jax.random.normal(jax.random.fold_in(_rk, 1), (2, 1024, 256), jnp.float32)
        _lenS = 1024 - jax.random.randint(jax.random.fold_in(_rk, 7), (2,), 0, max(1, 1024 // 4) + 1, jnp.int32)
        _lenS2 = 1024 - jax.random.randint(jax.random.fold_in(_rk, 8), (2,), 0, max(1, 1024 // 4) + 1, jnp.int32)
        cond_1024 = 0.0061147 + 1.02565 * jax.random.normal(jax.random.fold_in(_rk, 11), (2, 256), jnp.float32)
        return (x, cond_1024)
    x, cond_1024 = _rec_inputs()

    def _L0_cond_setup():
        import jax, jax.numpy as jnp
        import numpy as np
        D, HS, HE, E, K = (256, 512, 256, 8, 2)
        B, T = (4, 256)
        N_SHARED = 1
        key = jax.random.key(seed)
        ks = jax.random.split(key, 9)
        g = lambda k, shape, s: jax.random.normal(k, shape, jnp.float32) * s
        return {'x': g(ks[0], (B, T, D), 1.0), 't_emb': g(ks[1], (B, D), 1.0), 'router_W': g(ks[2], (2 * D, E), 0.01), 'router_bias': jnp.zeros((E,), jnp.float32), 'w1': g(ks[3], (D, HS), 0.02), 'w3': g(ks[4], (D, HS), 0.02), 'w2': g(ks[5], (HS, D), 0.02), 'W1e': g(ks[6], (E, D, HE), 0.02), 'W2e': g(ks[7], (E, HE, D), 0.02)}
    _L0_cond_all = _L0_cond_setup()
    _L0_cond_in = {k: v for k, v in _L0_cond_all.items() if k in ('router_W', 'router_bias', 'w1', 'w3', 'w2', 'W1e', 'W2e')}
    del _L0_cond_all

    def _L0_attn_setup():
        import jax, jax.numpy as jnp
        import numpy as np
        B, T, C = (4, 256, 256)
        HEAD = 64
        H = C // HEAD
        LORA_MIX = 32
        LORA_DECAY = 64
        LN_EPS = 0.00064

        def _wkv6(r, k, v, w, u):
            rT = jnp.moveaxis(r, 1, 0)
            kT = jnp.moveaxis(k, 1, 0)
            vT = jnp.moveaxis(v, 1, 0)
            wT = jnp.moveaxis(w, 1, 0)

            def step(S, inputs):
                rt, kt, vt, wt = inputs
                kv = kt[..., :, None] * vt[..., None, :]
                y = jnp.einsum('bhi,bhij->bhj', rt, S + u[None, :, :, None] * kv)
                S = wt[..., :, None] * S + kv
                return (S, y)
            S0 = jnp.zeros((r.shape[0], H, HEAD, HEAD), r.dtype)
            _, yT = jax.lax.scan(step, S0, (rT, kT, vT, wT))
            return jnp.moveaxis(yT, 0, 1)

        def _tmix_forward(x, time_maa_x, time_maa_w, time_maa_k, time_maa_v, time_maa_r, time_maa_w1, time_maa_w2, time_decay, time_decay_w1, time_decay_w2, time_faaaa, W_r, W_k, W_v, W_o, ln_w, ln_b):
            b, t, c = x.shape
            xshift = jnp.pad(x, ((0, 0), (1, 0), (0, 0)))[:, :t]
            xx = xshift - x
            xxx = x + xx * time_maa_x
            m = jnp.tanh(xxx @ time_maa_w1).reshape(b, t, 4, LORA_MIX)
            m = jnp.einsum('btfl,flc->fbtc', m, time_maa_w2)
            mw, mk, mv, mr = (m[0], m[1], m[2], m[3])
            xw = x + xx * (time_maa_w + mw)
            xk = x + xx * (time_maa_k + mk)
            xv = x + xx * (time_maa_v + mv)
            xr = x + xx * (time_maa_r + mr)
            r = (xr @ W_r).reshape(b, t, H, HEAD)
            k = (xk @ W_k).reshape(b, t, H, HEAD)
            v = (xv @ W_v).reshape(b, t, H, HEAD)
            ww = time_decay + jnp.tanh(xw @ time_decay_w1) @ time_decay_w2
            w = jnp.exp(-jnp.exp(ww)).reshape(b, t, H, HEAD)
            y = _wkv6(r, k, v, w, time_faaaa)
            mean = y.mean(-1, keepdims=True)
            var = y.var(-1, keepdims=True)
            yn = ((y - mean) * jax.lax.rsqrt(var + LN_EPS)).reshape(b, t, c)
            yn = yn * ln_w + ln_b
            return yn @ W_o
        key0 = jax.random.key(seed)
        ks = jax.random.split(key0, 24)
        rn = lambda k, shape, s: jax.random.normal(k, shape, jnp.float32) * s
        inp = {'query': jax.random.normal(ks[0], (B, T, C), jnp.float32), 'key': jax.random.normal(ks[1], (B, T, C), jnp.float32), 'value': jax.random.normal(ks[2], (B, T, C), jnp.float32), 'time_maa_x': rn(ks[3], (C,), 0.1) + 0.5, 'time_maa_w': rn(ks[4], (C,), 0.1) + 0.5, 'time_maa_k': rn(ks[5], (C,), 0.1) + 0.5, 'time_maa_v': rn(ks[6], (C,), 0.1) + 0.5, 'time_maa_r': rn(ks[7], (C,), 0.1) + 0.5, 'time_maa_w1': rn(ks[8], (C, 4 * LORA_MIX), 0.02), 'time_maa_w2': rn(ks[9], (4, LORA_MIX, C), 0.02), 'time_decay': rn(ks[10], (C,), 0.5) - 5.0, 'time_decay_w1': rn(ks[11], (C, LORA_DECAY), 0.02), 'time_decay_w2': rn(ks[12], (LORA_DECAY, C), 0.02), 'time_faaaa': rn(ks[13], (H, HEAD), 0.5), 'W_r': rn(ks[14], (C, C), 0.02), 'W_k': rn(ks[15], (C, C), 0.02), 'W_v': rn(ks[16], (C, C), 0.02), 'W_o': rn(ks[17], (C, C), 0.02), 'ln_w': jnp.ones((C,), jnp.float32), 'ln_b': jnp.zeros((C,), jnp.float32)}
        return inp
    _L0_attn_all = _L0_attn_setup()
    _L0_attn_in = {k: v for k, v in _L0_attn_all.items() if k in ('key', 'value', 'time_maa_x', 'time_maa_w', 'time_maa_k', 'time_maa_v', 'time_maa_r', 'time_maa_w1', 'time_maa_w2', 'time_decay', 'time_decay_w1', 'time_decay_w2', 'time_faaaa', 'W_r', 'W_k', 'W_v', 'W_o', 'ln_w', 'ln_b')}
    del _L0_attn_all

    def _L0_cond2_setup():
        import jax, jax.numpy as jnp
        import numpy as np
        B, N, D, C = (32, 64, 256, 256)
        key = jax.random.key(seed)
        k1, k2, k3, k4 = jax.random.split(key, 4)
        scale = 1.0 / np.sqrt(D)
        return {'encoded_utterance': jax.random.normal(k1, (B, D), dtype=jnp.float32), 'element_embeddings': jax.random.normal(k2, (B, N, D), dtype=jnp.float32), 'weight_matrix': jax.random.normal(k3, (2 * D, C), dtype=jnp.float32) * scale, 'W_proj': jax.random.normal(k4, (D, D), dtype=jnp.float32) * scale, 'b_proj': jnp.zeros((D,), dtype=jnp.float32)}
    _L0_cond2_all = _L0_cond2_setup()
    _L0_cond2_in = {k: v for k, v in _L0_cond2_all.items() if k in ('weight_matrix', 'W_proj', 'b_proj')}
    del _L0_cond2_all

    def _L0_ffn_setup():
        import jax, jax.numpy as jnp
        import numpy as np
        D_MODEL = 256
        D_HIDDEN = 1024
        NUM_BANKS = 16
        NUM_SELECTED = 2
        key = jax.random.key(seed)
        ks = jax.random.split(key, 7)
        s = 0.02
        return {'tensor': jax.random.normal(ks[0], (4, 256, D_MODEL), dtype=jnp.float32), 'Wr': jax.random.normal(ks[1], (D_MODEL, NUM_BANKS), dtype=jnp.float32) * s, 'br': jnp.zeros((NUM_BANKS,), dtype=jnp.float32), 'W1': jax.random.normal(ks[2], (NUM_BANKS, D_MODEL, D_HIDDEN), dtype=jnp.float32) * s, 'b1': jnp.zeros((NUM_BANKS, D_HIDDEN), dtype=jnp.float32), 'W2': jax.random.normal(ks[3], (NUM_BANKS, D_HIDDEN, D_MODEL), dtype=jnp.float32) * s, 'b2': jnp.zeros((NUM_BANKS, D_MODEL), dtype=jnp.float32)}
    _L0_ffn_all = _L0_ffn_setup()
    _L0_ffn_in = {k: v for k, v in _L0_ffn_all.items() if k in ('Wr', 'br', 'W1', 'b1', 'W2', 'b2')}
    del _L0_ffn_all
    return {'x': x, 'cond_1024': cond_1024, 'L0_cond_router_W': _L0_cond_in['router_W'], 'L0_cond_router_bias': _L0_cond_in['router_bias'], 'L0_cond_w1': _L0_cond_in['w1'], 'L0_cond_w3': _L0_cond_in['w3'], 'L0_cond_w2': _L0_cond_in['w2'], 'L0_cond_W1e': _L0_cond_in['W1e'], 'L0_cond_W2e': _L0_cond_in['W2e'], 'L0_attn_key': _L0_attn_in['key'], 'L0_attn_value': _L0_attn_in['value'], 'L0_attn_time_maa_x': _L0_attn_in['time_maa_x'], 'L0_attn_time_maa_w': _L0_attn_in['time_maa_w'], 'L0_attn_time_maa_k': _L0_attn_in['time_maa_k'], 'L0_attn_time_maa_v': _L0_attn_in['time_maa_v'], 'L0_attn_time_maa_r': _L0_attn_in['time_maa_r'], 'L0_attn_time_maa_w1': _L0_attn_in['time_maa_w1'], 'L0_attn_time_maa_w2': _L0_attn_in['time_maa_w2'], 'L0_attn_time_decay': _L0_attn_in['time_decay'], 'L0_attn_time_decay_w1': _L0_attn_in['time_decay_w1'], 'L0_attn_time_decay_w2': _L0_attn_in['time_decay_w2'], 'L0_attn_time_faaaa': _L0_attn_in['time_faaaa'], 'L0_attn_W_r': _L0_attn_in['W_r'], 'L0_attn_W_k': _L0_attn_in['W_k'], 'L0_attn_W_v': _L0_attn_in['W_v'], 'L0_attn_W_o': _L0_attn_in['W_o'], 'L0_attn_ln_w': _L0_attn_in['ln_w'], 'L0_attn_ln_b': _L0_attn_in['ln_b'], 'L0_cond2_weight_matrix': _L0_cond2_in['weight_matrix'], 'L0_cond2_W_proj': _L0_cond2_in['W_proj'], 'L0_cond2_b_proj': _L0_cond2_in['b_proj'], 'L0_ffn_Wr': _L0_ffn_in['Wr'], 'L0_ffn_br': _L0_ffn_in['br'], 'L0_ffn_W1': _L0_ffn_in['W1'], 'L0_ffn_b1': _L0_ffn_in['b1'], 'L0_ffn_W2': _L0_ffn_in['W2'], 'L0_ffn_b2': _L0_ffn_in['b2']}

def reference(x, cond_1024, L0_cond_router_W, L0_cond_router_bias, L0_cond_w1, L0_cond_w3, L0_cond_w2, L0_cond_W1e, L0_cond_W2e, L0_attn_key, L0_attn_value, L0_attn_time_maa_x, L0_attn_time_maa_w, L0_attn_time_maa_k, L0_attn_time_maa_v, L0_attn_time_maa_r, L0_attn_time_maa_w1, L0_attn_time_maa_w2, L0_attn_time_decay, L0_attn_time_decay_w1, L0_attn_time_decay_w2, L0_attn_time_faaaa, L0_attn_W_r, L0_attn_W_k, L0_attn_W_v, L0_attn_W_o, L0_attn_ln_w, L0_attn_ln_b, L0_cond2_weight_matrix, L0_cond2_W_proj, L0_cond2_b_proj, L0_ffn_Wr, L0_ffn_br, L0_ffn_W1, L0_ffn_b1, L0_ffn_W2, L0_ffn_b2):
    import jax
    import jax.numpy as jnp

    def _L0_cond_ref(x, t_emb, router_W, router_bias, w1, w3, w2, W1e, W2e):
        import jax, jax.numpy as jnp
        import numpy as np
        D, HS, HE, E, K = (256, 512, 256, 8, 2)
        B, T = (4, 256)
        N_SHARED = 1
        Bb, Tt, C = x.shape
        xf = x.reshape(-1, C)
        tf = jnp.broadcast_to(t_emb[:, None, :], (Bb, Tt, C)).reshape(-1, C)
        N = xf.shape[0]
        shared = jax.nn.silu(xf @ w1) * (xf @ w3) @ w2
        s = jax.nn.sigmoid((jnp.concatenate([xf, tf], axis=-1) @ router_W).astype(jnp.float32))
        sel_scores = s + router_bias
        _, topk_idx = jax.lax.top_k(sel_scores, K)
        s_sel = jnp.take_along_axis(s, topk_idx, axis=1)
        denom = s_sel.sum(axis=1, keepdims=True)
        gates = jnp.where(denom > 1e-09, s_sel / (denom + 1e-09), 1.0 / K).astype(x.dtype)
        combine = jnp.zeros((N, E), x.dtype).at[jnp.arange(N)[:, None], topk_idx].add(gates)
        h = jax.nn.gelu(jnp.einsum('nc,ech->enh', xf, W1e), approximate=False)
        y = jnp.einsum('enh,ehc->enc', h, W2e)
        routed = jnp.einsum('ne,enc->nc', combine, y)
        return ((shared + routed) / (N_SHARED + K)).reshape(Bb, Tt, C)

    def _L0_attn_ref(query, key, value, time_maa_x, time_maa_w, time_maa_k, time_maa_v, time_maa_r, time_maa_w1, time_maa_w2, time_decay, time_decay_w1, time_decay_w2, time_faaaa, W_r, W_k, W_v, W_o, ln_w, ln_b):
        import jax, jax.numpy as jnp
        import numpy as np
        B, T, C = (4, 256, 256)
        HEAD = 64
        H = C // HEAD
        LORA_MIX = 32
        LORA_DECAY = 64
        LN_EPS = 0.00064

        def _wkv6(r, k, v, w, u):
            rT = jnp.moveaxis(r, 1, 0)
            kT = jnp.moveaxis(k, 1, 0)
            vT = jnp.moveaxis(v, 1, 0)
            wT = jnp.moveaxis(w, 1, 0)

            def step(S, inputs):
                rt, kt, vt, wt = inputs
                kv = kt[..., :, None] * vt[..., None, :]
                y = jnp.einsum('bhi,bhij->bhj', rt, S + u[None, :, :, None] * kv)
                S = wt[..., :, None] * S + kv
                return (S, y)
            S0 = jnp.zeros((r.shape[0], H, HEAD, HEAD), r.dtype)
            _, yT = jax.lax.scan(step, S0, (rT, kT, vT, wT))
            return jnp.moveaxis(yT, 0, 1)

        def _tmix_forward(x, time_maa_x, time_maa_w, time_maa_k, time_maa_v, time_maa_r, time_maa_w1, time_maa_w2, time_decay, time_decay_w1, time_decay_w2, time_faaaa, W_r, W_k, W_v, W_o, ln_w, ln_b):
            b, t, c = x.shape
            xshift = jnp.pad(x, ((0, 0), (1, 0), (0, 0)))[:, :t]
            xx = xshift - x
            xxx = x + xx * time_maa_x
            m = jnp.tanh(xxx @ time_maa_w1).reshape(b, t, 4, LORA_MIX)
            m = jnp.einsum('btfl,flc->fbtc', m, time_maa_w2)
            mw, mk, mv, mr = (m[0], m[1], m[2], m[3])
            xw = x + xx * (time_maa_w + mw)
            xk = x + xx * (time_maa_k + mk)
            xv = x + xx * (time_maa_v + mv)
            xr = x + xx * (time_maa_r + mr)
            r = (xr @ W_r).reshape(b, t, H, HEAD)
            k = (xk @ W_k).reshape(b, t, H, HEAD)
            v = (xv @ W_v).reshape(b, t, H, HEAD)
            ww = time_decay + jnp.tanh(xw @ time_decay_w1) @ time_decay_w2
            w = jnp.exp(-jnp.exp(ww)).reshape(b, t, H, HEAD)
            y = _wkv6(r, k, v, w, time_faaaa)
            mean = y.mean(-1, keepdims=True)
            var = y.var(-1, keepdims=True)
            yn = ((y - mean) * jax.lax.rsqrt(var + LN_EPS)).reshape(b, t, c)
            yn = yn * ln_w + ln_b
            return yn @ W_o
        return _tmix_forward(query, time_maa_x, time_maa_w, time_maa_k, time_maa_v, time_maa_r, time_maa_w1, time_maa_w2, time_decay, time_decay_w1, time_decay_w2, time_faaaa, W_r, W_k, W_v, W_o, ln_w, ln_b)

    def _L0_cond2_ref(encoded_utterance, element_embeddings, weight_matrix, W_proj, b_proj):
        import jax, jax.numpy as jnp
        import numpy as np
        B, N, D, C = (32, 64, 256, 256)
        u = jax.nn.gelu(encoded_utterance @ W_proj + b_proj, approximate=False)
        W_u, W_e = (weight_matrix[:D], weight_matrix[D:])
        logits = (u @ W_u)[:, None, :] + jnp.einsum('bnd,dc->bnc', element_embeddings, W_e)
        return logits

    def _L0_ffn_ref(tensor, Wr, br, W1, b1, W2, b2):
        import jax, jax.numpy as jnp
        import numpy as np
        D_MODEL = 256
        D_HIDDEN = 1024
        NUM_BANKS = 16
        NUM_SELECTED = 2
        logits = jnp.einsum('bsd,de->bse', tensor, Wr) + br
        probs = jax.nn.softmax(logits, axis=-1)
        topv, topi = jax.lax.top_k(probs, NUM_SELECTED)
        gate = jnp.sum(jax.nn.one_hot(topi, NUM_BANKS, dtype=tensor.dtype) * topv[..., None], axis=-2)
        h = jax.nn.relu(jnp.einsum('bsd,edh->bseh', tensor, W1) + b1)
        y = jnp.einsum('bseh,ehm->bsem', h, W2) + b2
        out = jnp.einsum('bse,bsem->bsm', gate, y)
        return out
    x = x + _L0_attn_ref(_L0_cond_ref(x, cond_1024, L0_cond_router_W, L0_cond_router_bias, L0_cond_w1, L0_cond_w3, L0_cond_w2, L0_cond_W1e, L0_cond_W2e), L0_attn_key, L0_attn_value, L0_attn_time_maa_x, L0_attn_time_maa_w, L0_attn_time_maa_k, L0_attn_time_maa_v, L0_attn_time_maa_r, L0_attn_time_maa_w1, L0_attn_time_maa_w2, L0_attn_time_decay, L0_attn_time_decay_w1, L0_attn_time_decay_w2, L0_attn_time_faaaa, L0_attn_W_r, L0_attn_W_k, L0_attn_W_v, L0_attn_W_o, L0_attn_ln_w, L0_attn_ln_b)
    x = x + _L0_ffn_ref(_L0_cond2_ref(cond_1024, x, L0_cond2_weight_matrix, L0_cond2_W_proj, L0_cond2_b_proj), L0_ffn_Wr, L0_ffn_br, L0_ffn_W1, L0_ffn_b1, L0_ffn_W2, L0_ffn_b2)
    return x

_drawn_inputs = setup_inputs


def setup_inputs(seed=0):
    import zlib

    import numpy as np

    out = dict(_drawn_inputs(seed))
    spreads = {'L0_cond_router_bias': (0.0, 0.8),
     'L0_attn_ln_w': (1.0, 0.6),
     'L0_attn_ln_b': (0.0, 0.1),
     'L0_cond2_b_proj': (0.0, 0.8),
     'L0_ffn_br': (0.0, 0.45),
     'L0_ffn_b1': (0.0, 0.8),
     'L0_ffn_b2': (0.0, 0.495)}
    factors = {'L0_cond_router_W': 8.0,
     'L0_cond_w1': 8.0,
     'L0_cond_w3': 8.0,
     'L0_cond_w2': 8.0,
     'L0_cond_W1e': 8.0,
     'L0_cond_W2e': 8.0,
     'L0_attn_time_maa_x': 8.0,
     'L0_attn_time_maa_w': 8.0,
     'L0_attn_time_maa_k': 8.0,
     'L0_attn_time_maa_v': 8.0,
     'L0_attn_time_maa_r': 8.0,
     'L0_attn_time_maa_w1': 8.0,
     'L0_attn_time_maa_w2': 8.0,
     'L0_attn_time_decay': 8.0,
     'L0_attn_time_decay_w1': 8.0,
     'L0_attn_time_decay_w2': 8.0,
     'L0_attn_time_faaaa': 8.0,
     'L0_attn_W_r': 8.0,
     'L0_attn_W_k': 8.0,
     'L0_attn_W_v': 8.0}
    for name, (base, spread) in spreads.items():
        noise = np.random.default_rng([zlib.crc32(name.encode()), seed]).standard_normal(out[name].shape)
        drawn = base * np.exp(spread * noise) if base else spread * noise
        out[name] = jnp.asarray(drawn.astype(out[name].dtype))
    for name, factor in factors.items():
        out[name] = (out[name] * factor).astype(out[name].dtype)
    return out
```

```python
from contextlib import ExitStack

import concourse.bass as bass
from concourse import mybir

F32 = mybir.dt.float32
I32 = mybir.dt.int32
U32 = mybir.dt.uint32
ALU = mybir.AluOpType
ACT = mybir.ActivationFunctionType
AX = mybir.AxisListType

P = 128
B, SEQ, D = 2, 1024, 256
N = B * SEQ
NT = N // P
KC = D // P
GT = 4
NG = NT // GT
HS = 512
E1, H1 = 8, 256
E2, H2 = 16, 1024
RING = 4
HEADS, HD = 4, 64
MIX, DEC = 32, 64
CH = 128
LEVELS = 7
LN_EPS = 0.00064
STOP = "end"


def slots_for(experts):
    return 2 * N // P + experts - 1


S1, S2 = slots_for(E1), slots_for(E2)


def dense_front(nc, d, t):
    with ExitStack() as ctx:
        def sb(name, shape, dt=F32):
            return ctx.enter_context(nc.sbuf_tensor(name, shape, dt))

        def ps(name, shape, dt=F32):
            return ctx.enter_context(nc.psum_tensor(name, shape, dt))

        def sem(name):
            return ctx.enter_context(nc.semaphore(name))

        w1, w3 = sb("w1", [P, KC, HS]), sb("w3", [P, KC, HS])
        w2 = sb("w2", [P, HS // P, D])
        rw = sb("rw", [P, 2 * KC, E1])
        cond_col = sb("cond_col", [P, KC, B])
        cond_rep = sb("cond_rep", [P, KC, B, P])
        bias_rep = sb("bias_rep", [P, E1])
        zero = sb("zero", [P, D])
        xs = sb("xs", [P, GT, D])
        xT = sb("xT", [P, KC, GT * P])
        sig = sb("sig", [P, 2, GT * P])
        gate = sb("gate", [P, 2, GT * P])
        hT = sb("hT", [P, HS // P, GT * P])
        tp = ps("tp", [P, KC, GT * P])
        hp = ps("hp", [P, 2, GT * P])
        gp = ps("gp", [P, 2, GT * P])
        yp = ps("yp", [P, 2, D])
        rp = ps("rp", [P, 512])
        rp_l = rp[:, 0:GT * E1].rearrange("p (t e) -> p t e", e=E1)
        rp_c = rp[:, 0:B * E1].rearrange("p (b e) -> p b e", e=E1)
        cond_part = sb("cond_part", [P, B, E1])
        logits = sb("logits", [P, NT, E1])

        weights_in, x_in, zeroed, cond_in, cond_ready, rows_cleared = (
            sem("weights_in"), sem("x_in"), sem("zeroed"), sem("cond_in"), sem("cond_ready"), sem("rows_cleared"))
        x_turned, xT_ready, h_ready, sig_ready, gate_ready, hT_ready, y_ready, y_out = (
            sem("x_turned"), sem("xT_ready"), sem("h_ready"), sem("sig_ready"), sem("gate_ready"), sem("hT_ready"),
            sem("y_ready"), sem("y_out"))
        logits_ready, scores_ready, logits_out = (
            sem("logits_ready"), sem("scores_ready"), sem("logits_out"))
        block = ctx.enter_context(nc.Block())
        x_rows = d["x"].rearrange("b (t p) c -> p (b t) c", p=P)

        @block.sync
        def _(sp):
            sp.dma_start(w1[:], d["w1"].rearrange("(k p) n -> p k n", p=P)).then_inc(weights_in, 16)
            sp.dma_start(w3[:], d["w3"].rearrange("(k p) n -> p k n", p=P)).then_inc(weights_in, 16)
            sp.dma_start(w2[:], d["w2"].rearrange("(k p) n -> p k n", p=P)).then_inc(weights_in, 16)
            sp.dma_start(rw[:], d["router_W"].rearrange("(k p) n -> p k n", p=P)).then_inc(weights_in, 16)
            sp.dma_start(bias_rep[:], d["router_bias"].unsqueeze(0).to_broadcast([P, E1])).then_inc(weights_in, 16)
            sp.dma_start(t["x_tok"][:], x_rows).then_inc(weights_in, 16)
            sp.wait_ge(zeroed, 1)
            sp.dma_start(d["rows1"].rearrange("(s p) c -> p s c", p=P),
                         zero[:].unsqueeze(1).to_broadcast([P, S1, D])).then_inc(rows_cleared, 16)
            sp.dma_start(d["rows2"].rearrange("(s p) c -> p s c", p=P),
                         zero[:].unsqueeze(1).to_broadcast([P, S2, D])).then_inc(rows_cleared, 16)
            sp.wait_ge(rows_cleared, 32)
            sp.wait_ge(weights_in, 96)

        @block.gpsimd
        def _(pool):
            with nc.allow_non_contiguous_dma(reason="512 condition values, once"):
                for b in range(B):
                    pool.dma_start(cond_col[:, :, b], d["cond"][b].rearrange("(k p) -> p k", p=P)).then_inc(cond_in, 16)
            with pool.Fori(0, NG) as g:
                pool.wait_ge(x_turned, 1 + g)
                pool.dma_start(xs[:], x_rows[:, bass.ds(g * GT, GT), :]).then_inc(x_in, 16)
            pool.wait_ge(x_in, 16 * NG)

        @block.scalar
        def _(act):
            act.wait_ge(cond_in, 32)
            for k in range(KC):
                for b in range(B):
                    last = nc.scalar.activation(cond_rep[:, k, b, :], cond_col[:, k, b:b + 1].to_broadcast([P, P]),
                                                ACT.Copy)
            last.then_inc(cond_ready, 1)
            with act.Fori(0, NG) as g:
                for k in range(KC):
                    act.wait_ge(x_turned, 1 + g + 1)
                    last = nc.scalar.activation(xT[:, k, :], tp[:, k, :], ACT.Copy)
                last.then_inc(xT_ready, 1)
                for c in range(HS // P):
                    act.wait_ge(h_ready, g * (HS // P) + c + 1)
                    if c >= 2:
                        act.wait_ge(hT_ready, 1 + g * (HS // P) + c - 1)
                    else:
                        act.wait_ge(hT_ready, 1 + g * (HS // P))
                    nc.scalar.activation(sig[:, c % 2, :], hp[:, c % 2, :], ACT.Sigmoid).then_inc(sig_ready, 1)
            act.wait_ge(scores_ready, 1)
            nc.scalar.activation(t["score1"][:], logits[:], ACT.Sigmoid).then_inc(scores_ready, 1)

        @block.vector
        def _(dve):
            for primed in (x_turned, hT_ready, xT_ready, y_out):
                dve.sem_inc(primed, 1)
            nc.vector.memset(zero[:], 0.0).then_inc(zeroed, 1)
            dve.wait_ge(logits_ready, 1)
            nc.vector.tensor_copy(cond_part[:], rp_c).then_inc(logits_out, 1)
            with dve.Fori(0, NG) as g:
                for c in range(HS // P):
                    dve.wait_ge(sig_ready, g * (HS // P) + c + 1)
                    nc.vector.tensor_tensor(gate[:, c % 2, :], sig[:, c % 2, :], hp[:, c % 2, :],
                                            ALU.mult).then_inc(gate_ready, 1)
                    dve.wait_ge(gate_ready, g * (HS // P) + c + 1)
                    if c == 0:
                        dve.wait_ge(y_ready, g * 2)
                    nc.vector.tensor_tensor(hT[:, c, :], gate[:, c % 2, :], gp[:, c % 2, :],
                                            ALU.mult).then_inc(hT_ready, 1)
                dve.wait_ge(logits_ready, g + 2)
                nc.vector.tensor_copy(logits[:, bass.ds(g * GT, GT), :], rp_l).then_inc(logits_out, 1)
                for h in range(2):
                    dve.wait_ge(y_ready, g * 2 + h + 1)
                    nc.vector.tensor_copy(t["acc"][:, bass.ds(g * GT + 2 * h, 2), :], yp[:]).then_inc(y_out, 1)
            dve.wait_ge(logits_out, NG + 1)
            for b in range(B):
                last = nc.vector.tensor_tensor(logits[:, b * NT // B:(b + 1) * NT // B, :],
                                               logits[:, b * NT // B:(b + 1) * NT // B, :],
                                               cond_part[:, b:b + 1, :].to_broadcast([P, NT // B, E1]), ALU.add)
            last.then_inc(scores_ready, 1)
            dve.wait_ge(scores_ready, 2)
            dve.wait_ge(weights_in, 96)
            nc.vector.tensor_tensor(t["sel1"][:], t["score1"][:], bias_rep[:].unsqueeze(1).to_broadcast([P, NT, E1]),
                                    ALU.add)

        @block.tensor
        def _(pe):
            pe.wait_ge(cond_ready, 1)
            pe.wait_ge(weights_in, 96)
            for b in range(B):
                for k in range(KC):
                    last = nc.tensor.matmul(rp_c[:, b, :], cond_rep[:, k, b, :], rw[:, KC + k, :],
                                            start=(k == 0), stop=(k == KC - 1))
            last.then_inc(logits_ready, 1)
            with pe.Fori(0, NG) as g:
                pe.wait_ge(x_in, g * 16 + 16)
                pe.wait_ge(xT_ready, 1 + g)
                for tt in range(GT):
                    for k in range(KC):
                        last = nc.tensor.transpose(tp[:, k, tt * P:(tt + 1) * P], xs[:, tt, k * P:(k + 1) * P],
                                                   t["ident"][:])
                last.then_inc(x_turned, 1)
                pe.wait_ge(xT_ready, 1 + g + 1)
                for c in range(HS // P):
                    if c >= 2:
                        pe.wait_ge(hT_ready, 1 + g * (HS // P) + c - 1)
                    else:
                        pe.wait_ge(hT_ready, 1 + g * (HS // P))
                    for w, o in ((w1, hp), (w3, gp)):
                        for k in range(KC):
                            last = nc.tensor.matmul(o[:, c % 2, :], w[:, k, c * P:(c + 1) * P], xT[:, k, :],
                                                    start=(k == 0), stop=(k == KC - 1))
                    last.then_inc(h_ready, 1)
                pe.wait_ge(logits_out, g + 1)
                for tt in range(GT):
                    for k in range(KC):
                        last = nc.tensor.matmul(rp_l[:, tt, :], xT[:, k, tt * P:(tt + 1) * P], rw[:, k, :],
                                                start=(k == 0), stop=(k == KC - 1))
                last.then_inc(logits_ready, 1)
                for h in range(2):
                    pe.wait_ge(hT_ready, 1 + (g + 1) * (HS // P))
                    pe.wait_ge(y_out, 1 + g * 2 + h)
                    for tt in range(2):
                        for c in range(HS // P):
                            last = nc.tensor.matmul(yp[:, tt, :], hT[:, c, (2 * h + tt) * P:(2 * h + tt + 1) * P],
                                                    w2[:, c, :], start=(c == 0), stop=(c == HS // P - 1))
                    last.then_inc(y_ready, 1)


def route(nc, t, experts, slots, sel, val, first, tag):
    with ExitStack() as ctx:
        def sb(name, shape, dt=F32):
            return ctx.enter_context(nc.sbuf_tensor(tag + name, shape, dt))

        cand, onehot = sb("cand", [P, NT, experts]), sb("onehot", [P, 2, NT, experts])
        best, order = sb("best", [P, NT]), sb("order", [P, NT])
        both, rank = sb("both", [P, NT, experts]), sb("rank", [P, NT, experts])
        run = sb("run", [P, 2, NT, experts])
        count_i = sb("count_i", [P, experts], I32)
        tiles = sb("tiles", [P, experts])
        ends = sb("ends", [P, 2, experts])
        prod, picked = sb("prod", [P, NT, experts]), sb("picked", [P, NT])
        over = sb("over", [P, slots, experts])
        ends_f = sb("ends_f", [P, slots])
        cp = ctx.enter_context(nc.psum_tensor(tag + "cp", [P, 2, 512], F32))
        counts_ready = ctx.enter_context(nc.semaphore(tag + "counts_ready"))
        both_ready = ctx.enter_context(nc.semaphore(tag + "both_ready"))
        step_done = ctx.enter_context(nc.semaphore(tag + "step_done"))
        block = ctx.enter_context(nc.Block())
        width = NT * experts
        full = [P, NT, experts]

        @block.tensor
        def _(pe):
            pe.wait_ge(both_ready, 1)
            flat = both[:].rearrange("p t e -> p (t e)")
            nc.tensor.matmul(cp[:, 0, 0:width], t["before"][:], flat, start=True, stop=True)
            nc.tensor.matmul(cp[:, 1, 0:width], t["ones"][:], flat, start=True, stop=True).then_inc(counts_ready, 1)

        @block.vector
        def _(dve):
            steps = [0]

            def link(ins):
                steps[0] += 1
                ins.then_inc(step_done, 1)
                dve.wait_ge(step_done, steps[0])

            for k in range(2):
                link(nc.vector.tensor_reduce(best[:], sel[:], AX.X, ALU.max))
                link(nc.vector.tensor_tensor(cand[:], sel[:], best[:].unsqueeze(2).to_broadcast(full), ALU.is_equal))
                link(nc.vector.tensor_tensor(cand[:], cand[:], first[:], ALU.mult))
                link(nc.vector.tensor_reduce(order[:], cand[:], AX.X, ALU.max))
                link(nc.vector.tensor_tensor(onehot[:, k], cand[:], order[:].unsqueeze(2).to_broadcast(full),
                                             ALU.is_equal))
                link(nc.vector.tensor_tensor(prod[:], onehot[:, k], val[:], ALU.mult))
                link(nc.vector.tensor_reduce(t[tag + "gate"][:, k, :], prod[:], AX.X, ALU.add))
                if k == 0:
                    link(nc.vector.scalar_tensor_tensor(sel[:], onehot[:, 0], -3.0e38, sel[:], ALU.mult, ALU.add))
            nc.vector.tensor_tensor(both[:], onehot[:, 0], onehot[:, 1], ALU.add).then_inc(both_ready, 1)
            dve.wait_ge(counts_ready, 1)
            total = cp[:, 1, 0:width].rearrange("p (t e) -> p t e", e=experts)
            link(nc.vector.tensor_copy(run[:, 0], total))
            now, d = 0, 1
            while d < NT:
                link(nc.vector.tensor_copy(run[:, 1 - now, 0:d], run[:, now, 0:d]))
                link(nc.vector.tensor_tensor(run[:, 1 - now, d:NT], run[:, now, d:NT], run[:, now, 0:NT - d], ALU.add))
                now, d = 1 - now, 2 * d
            link(nc.vector.tensor_scalar(count_i[:], run[:, now, NT - 1], float(P - 1), None, ALU.add))
            link(nc.vector.tensor_scalar(count_i[:], count_i[:], 7, None, ALU.arith_shift_right))
            link(nc.vector.tensor_copy(tiles[:], count_i[:]))
            link(nc.vector.tensor_copy(ends[:, 0], tiles[:]))
            at, d = 0, 1
            while d < experts:
                link(nc.vector.tensor_copy(ends[:, 1 - at, 0:d], ends[:, at, 0:d]))
                link(nc.vector.tensor_tensor(ends[:, 1 - at, d:experts], ends[:, at, d:experts],
                                             ends[:, at, 0:experts - d], ALU.add))
                at, d = 1 - at, 2 * d
            link(nc.vector.tensor_tensor(rank[:], run[:, now], total, ALU.subtract))
            link(nc.vector.tensor_tensor(rank[:], rank[:],
                                         cp[:, 0, 0:width].rearrange("p (t e) -> p t e", e=experts), ALU.add))
            link(nc.vector.tensor_tensor(tiles[:], ends[:, at], tiles[:], ALU.subtract))
            link(nc.vector.tensor_scalar(tiles[:], tiles[:], float(P), None, ALU.mult))
            link(nc.vector.tensor_tensor(rank[:], rank[:], tiles[:].unsqueeze(1).to_broadcast(full), ALU.add))
            for k in range(2):
                link(nc.vector.tensor_tensor(prod[:], onehot[:, k], rank[:], ALU.mult))
                link(nc.vector.tensor_reduce(picked[:], prod[:], AX.X, ALU.add))
                link(nc.vector.tensor_copy(t[tag + "row"][:, k, :], picked[:]))
            link(nc.vector.tensor_tensor(over[:], ends[:, at].unsqueeze(1).to_broadcast([P, slots, experts]),
                                         t["slot_no"][:, 0:slots, 0:experts], ALU.is_le))
            link(nc.vector.tensor_reduce(ends_f[:], over[:], AX.X, ALU.add))
            link(nc.vector.tensor_scalar(t[tag + "owner"][:], ends_f[:], float(experts - 1), None, ALU.min))
            if tag == "a_":
                g = t["a_gate"]
                link(nc.vector.tensor_tensor(best[:], g[:, 0, :], g[:, 1, :], ALU.add))
                link(nc.vector.tensor_scalar(order[:], best[:], 1e-9, None, ALU.is_gt))
                link(nc.vector.tensor_scalar(best[:], best[:], 1e-9, None, ALU.add))
                link(nc.vector.reciprocal(best[:], best[:]))
                link(nc.vector.tensor_tensor(best[:], best[:], order[:], ALU.mult))
                link(nc.vector.tensor_scalar(order[:], order[:], -0.5, 0.5, ALU.mult, ALU.add))
                link(nc.vector.tensor_tensor(g[:], g[:], best[:].unsqueeze(1).to_broadcast([P, 2, NT]), ALU.mult))
                link(nc.vector.tensor_tensor(g[:], g[:], order[:].unsqueeze(1).to_broadcast([P, 2, NT]), ALU.add))


def dispatch(nc, t, src, row, rows):
    with nc.semaphore("rows_out") as rows_out, nc.Block() as block:
        @block.gpsimd
        def _(pool):
            for tt in range(NT):
                for k in range(2):
                    pool.indirect_dma_start(rows, bass.IndirectOffsetOnAxis(row[:, k, tt:tt + 1], 0),
                                            src[:, tt, :], None).then_inc(rows_out, 16)
            pool.wait_ge(rows_out, 32 * NT)


def expert_slots(nc, d, t, tag, experts, hidden, slots, rows, outs, W1, b1, W2, b2):
    C = hidden // P
    with ExitStack() as ctx:
        def sb(name, shape, dt=F32):
            return ctx.enter_context(nc.sbuf_tensor(tag + name, shape, dt))

        def ps(name, shape, dt=F32):
            return ctx.enter_context(nc.psum_tensor(tag + name, shape, dt))

        def ring(name):
            return [ctx.enter_context(nc.semaphore(f"{tag}{name}{b}")) for b in range(RING)]

        def sem(name):
            return ctx.enter_context(nc.semaphore(tag + name))

        wa = [sb(f"wa{b}", [P, KC, hidden]) for b in range(RING)]
        wb = [sb(f"wb{b}", [P, C, D]) for b in range(RING)]
        ba = [sb(f"ba{b}", [P, C]) for b in range(RING)]
        bb = [sb(f"bb{b}", [P, D]) for b in range(RING)]
        xr = [sb(f"xr{b}", [P, D]) for b in range(RING)]
        xT = [sb(f"xT{b}", [P, KC, P]) for b in range(RING)]
        hT = [sb(f"hT{b}", [P, C, P]) for b in range(RING)]
        yo = [sb(f"yo{b}", [P, D]) for b in range(RING)]
        HB = 2 if C > 4 else 1
        tp = [ps(f"tp{b}", [P, 512]) for b in range(1)]
        hp = [ps(f"hp{b}", [P, HB, 4, P]) for b in range(2)]
        yp = [ps(f"yp{b}", [P, 512]) for b in range(2)]
        loaded, freed, stored = ring("loaded"), ring("freed"), ring("stored")
        x_turned, xT_ready, h_ready, hT_ready, y_ready = (
            sem("x_turned"), sem("xT_ready"), sem("h_ready"), sem("hT_ready"), sem("y_ready"))
        block = ctx.enter_context(nc.Block())
        loads = 5 if b1 is not None else 3
        whole, rest = slots // RING, slots % RING

        def each_slot(eng, slot):
            with eng.Fori(0, whole) as i:
                for j in range(RING):
                    slot(i * RING + j, j, i)
            for j in range(rest):
                slot(whole * RING + j, j, whole)

        @block.sync
        def _(sp):
            def load(s, b, use):
                sp.wait_ge(freed[b], 1 + use)
                e = sp.value_load(t[tag + "owner"][0:1, bass.ds(s, 1)], min_val=0, max_val=experts - 1)
                sp.dma_start(xr[b][:], rows[bass.ds(s, 1), :, :].rearrange("s p c -> (s p) c")).then_inc(loaded[b], 16)
                sp.dma_start(wa[b][:], W1[bass.ds(e, 1), :, :].rearrange("e (k p) n -> p (e k) n", p=P)).then_inc(loaded[b], 16)
                sp.dma_start(wb[b][:], W2[bass.ds(e, 1), :, :].rearrange("e (p c) n -> p (e c) n", p=P)).then_inc(loaded[b], 16)
                if b1 is not None:
                    sp.dma_start(ba[b][:], b1[bass.ds(e, 1), :].rearrange("e (p c) -> p (e c)", p=P)).then_inc(loaded[b], 16)
                    sp.dma_start(bb[b][:], b2[bass.ds(e, 1), :].to_broadcast([P, D])).then_inc(loaded[b], 16)
            each_slot(sp, load)

        @block.tensor
        def _(pe):
            def turn(s, b, use):
                pe.wait_ge(loaded[b], use * (16 * loads) + 16 * loads)
                pe.wait_ge(xT_ready, s)
                for k in range(KC):
                    last = nc.tensor.transpose(tp[0][:, k * P:(k + 1) * P], xr[b][:, k * P:(k + 1) * P], t["ident"][:])
                last.then_inc(x_turned, 1)

            def up(s, b, q):
                pe.wait_ge(xT_ready, s + 1)
                if q is not None:
                    pe.wait_ge(hT_ready, 1 + q)
                for c in range(C):
                    for k in range(KC):
                        last = nc.tensor.matmul(hp[b % 2][:, c // 4, c % 4, :], wa[b][:, k, c:hidden:C], xT[b][:, k, :],
                                                start=(k == 0), stop=(k == KC - 1))
                last.then_inc(h_ready, 1)

            def down(s, b, use):
                pe.wait_ge(hT_ready, 1 + s + 1)
                pe.wait_ge(freed[(b + 2) % RING], 1 + use + (1 if b >= 2 else 0))
                for c in range(C):
                    last = nc.tensor.matmul(yp[b % 2][:, 0:D], hT[b][:, c, :], wb[b][:, c, :],
                                            start=(c == 0), stop=(c == C - 1))
                last.then_inc(y_ready, 1)

            turn(0, 0, 0)
            up(0, 0, None)
            turn(1, 1, 0)
            steps = (slots - 2) // RING
            with pe.Fori(0, steps) as i:
                for j in range(RING):
                    s, b = i * RING + j + 1, (j + 1) % RING
                    up(s, b, i * RING + j)
                    turn(i * RING + j + 2, (j + 2) % RING, i + (j + 2) // RING)
                    down(i * RING + j, j, i)
            for s in range(steps * RING + 1, slots):
                up(s, s % RING, s - 1)
                if s + 1 < slots:
                    turn(s + 1, (s + 1) % RING, (s + 1) // RING)
                down(s - 1, (s - 1) % RING, (s - 1) // RING)
            down(slots - 1, (slots - 1) % RING, (slots - 1) // RING)

        @block.scalar
        def _(act):
            def hidden_values(s, b, use):
                act.wait_ge(h_ready, s + 1)
                act.wait_ge(freed[b], 1 + use)
                if b1 is None:
                    last = nc.scalar.activation(hT[b][:], hp[b % 2][:, 0, 0:C, :], ACT.Gelu)
                else:
                    for c in range(C):
                        last = nc.scalar.activation(hT[b][:, c, :], hp[b % 2][:, c // 4, c % 4, :], ACT.Relu,
                                                    bias=ba[b][:, c:c + 1])
                last.then_inc(hT_ready, 1)
            each_slot(act, hidden_values)

        @block.vector
        def _(dve):
            for primed in (*freed, hT_ready):
                dve.sem_inc(primed, 1)
            def turned(s, b, use):
                dve.wait_ge(x_turned, s + 1)
                nc.vector.tensor_copy(xT[b][:].rearrange("p k n -> p (k n)"), tp[0][:, 0:D]).then_inc(xT_ready, 1)

            def result(s, b, use):
                dve.wait_ge(y_ready, s + 1)
                if use is not None:
                    dve.wait_ge(stored[b], 16 * use)
                if b2 is None:
                    ins = nc.vector.tensor_copy(yo[b][:], yp[b % 2][:, 0:D])
                else:
                    ins = nc.vector.tensor_tensor(yo[b][:], yp[b % 2][:, 0:D], bb[b][:], ALU.add)
                ins.then_inc(freed[b], 1)

            turned(0, 0, 0)
            turned(1, 1, 0)
            steps = (slots - 2) // RING
            for j in range(RING):
                turned(j + 2, (j + 2) % RING, None)
                result(j, j, None)
            with dve.Fori(1, steps) as i:
                for j in range(RING):
                    turned(i * RING + j + 2, (j + 2) % RING, None)
                    result(i * RING + j, j, i)
            for s in range(steps * RING, slots):
                if s + 2 < slots:
                    turned(s + 2, (s + 2) % RING, None)
                result(s, s % RING, s // RING)

        @block.gpsimd
        def _(pool):
            def store(s, b, use):
                pool.wait_ge(freed[b], 1 + use + 1)
                pool.dma_start(outs[bass.ds(s, 1), :, :].rearrange("s p c -> (s p) c"), yo[b][:]).then_inc(stored[b], 16)
            each_slot(pool, store)
            for b in range(RING):
                pool.wait_ge(stored[b], 16 * (whole + (b < rest)))


def combine(nc, t, tag, base, outs, finish):
    GB = 4
    with ExitStack() as ctx:
        gb = [ctx.enter_context(nc.sbuf_tensor(f"{tag}gb{b}", [P, 2, D], F32)) for b in range(GB)]
        part = [ctx.enter_context(nc.sbuf_tensor(f"{tag}part{b}", [P, D], F32)) for b in range(GB)]
        res = [ctx.enter_context(nc.sbuf_tensor(f"{tag}res{b}", [P, D], F32)) for b in range(GB)]
        tp = [ctx.enter_context(nc.psum_tensor(f"{tag}ctp{b}", [P, 4, P], F32)) for b in range(2)]
        got = [ctx.enter_context(nc.semaphore(f"{tag}got{b}")) for b in range(GB)]
        part_ready = ctx.enter_context(nc.semaphore(tag + "part_ready"))
        res_ready = ctx.enter_context(nc.semaphore(tag + "res_ready"))
        turned = ctx.enter_context(nc.semaphore(tag + "turned"))
        taken = ctx.enter_context(nc.semaphore(tag + "taken"))
        sent = [ctx.enter_context(nc.semaphore(f"{tag}sent{b}")) for b in range(GB)]
        block = ctx.enter_context(nc.Block())
        row, gate = t[tag + "row"], t[tag + "gate"]

        @block.gpsimd
        def _(pool):
            for tt in range(NT):
                if tt >= GB:
                    pool.wait_ge(res_ready, tt - GB + 1)
                for k in range(2):
                    pool.indirect_dma_start(gb[tt % GB][:, k, :], None, outs,
                                            bass.IndirectOffsetOnAxis(row[:, k, tt:tt + 1], 0)).then_inc(got[tt % GB], 16)

        @block.vector
        def _(dve):
            for tt in range(NT):
                dve.wait_ge(got[tt % GB], 32 * (tt // GB + 1))
                nc.vector.scalar_tensor_tensor(part[tt % GB][:], gb[tt % GB][:, 0, :], gate[:, 0, tt:tt + 1],
                                               base[:, tt, :], ALU.mult, ALU.add).then_inc(part_ready, 1)
                dve.wait_ge(part_ready, tt + 1)
                if tt >= GB:
                    if finish is None:
                        dve.wait_ge(turned, tt - GB + 1)
                    else:
                        dve.wait_ge(sent[tt % GB], 16 * (tt // GB))
                nc.vector.scalar_tensor_tensor(res[tt % GB][:], gb[tt % GB][:, 1, :], gate[:, 1, tt:tt + 1],
                                               part[tt % GB][:], ALU.mult, ALU.add).then_inc(res_ready, 1)

        if finish is None:
            @block.tensor
            def _(pe):
                for tt in range(NT):
                    pe.wait_ge(res_ready, tt + 1)
                    if tt >= 2:
                        pe.wait_ge(taken, tt - 1)
                    for k in range(KC):
                        last = nc.tensor.transpose(tp[tt % 2][:, k, :], res[tt % GB][:, k * P:(k + 1) * P], t["ident"][:])
                    last.then_inc(turned, 1)

            @block.scalar
            def _(act):
                for tt in range(NT):
                    act.wait_ge(turned, tt + 1)
                    b, at = tt // (NT // B), (tt % (NT // B)) * P
                    nc.scalar.activation(t["qT"][:, :, b, 1 + at:1 + at + P], tp[tt % 2][:, 0:KC, :], ACT.Copy,
                                         scale=1.0 / 3.0).then_inc(taken, 1)
        else:
            @block.sync
            def _(sp):
                for tt in range(NT):
                    sp.wait_ge(res_ready, tt + 1)
                    sp.dma_start(finish[:, tt, :], res[tt % GB][:]).then_inc(sent[tt % GB], 16)
                for b in range(GB):
                    sp.wait_ge(sent[b], 16 * (NT // GB))


def qcols(t, i, width, at):
    return t["qT"][:, :, :, bass.ds(i * width + at, width)].rearrange("p k b w -> p (k b) w")


def recurrence(nc, d, t):
    NI = 4
    W = SEQ // NI
    CW = W // CH
    COLS = B * W
    with ExitStack() as ctx:
        def sb(name, shape, dt=F32):
            return ctx.enter_context(nc.sbuf_tensor(name, shape, dt))

        def ps(name, shape, dt=F32):
            return ctx.enter_context(nc.psum_tensor(name, shape, dt))

        def sem(name):
            return ctx.enter_context(nc.semaphore(name))

        maa1, maa2 = sb("maa1", [P, KC, P]), sb("maa2", [P, D])
        dw1, dw2 = sb("dw1", [P, KC, DEC]), sb("dw2", [DEC, D])
        wr, wk, wv, wo = (sb(n, [P, KC, D]) for n in ("wr", "wk", "wv", "wo"))
        NV = 9
        vec_rows, vec = sb("vec_rows", [NV * KC, P]), sb("vec", [P, NV * KC])
        bonus_sel = sb("bonus_sel", [P, KC, HEADS])
        cur, xx, xxx = (sb(n, [P, KC, B, W]) for n in ("cur", "xx", "xxx"))
        mix = sb("mix", [P, COLS])
        shifted = [sb(f"shifted{i}", [P, KC, B, W]) for i in range(4)]
        dlow = sb("dlow", [DEC, COLS])
        r, k, w, ew = (sb(n, [P, KC * COLS]) for n in ("r", "k", "w", "ew"))
        v = sb("v", [P, B * CW, D])
        pre, suf = sb("pre", [P, KC * COLS]), sb("suf", [P, KC * COLS])
        tot = [w] + [sb(f"tot{l}", [P, (KC * COLS) >> l]) for l in range(1, LEVELS + 1)]
        rp = [None] + [sb(f"rp{l}", [P, KC * COLS // 2]) for l in range(1, LEVELS)]
        kq = [k] + [sb(f"kq{l}", [P, KC * COLS]) for l in range(1, LEVELS)]
        rfull, kfull, rk = (sb(n, [P, KC * COLS]) for n in ("rfull", "kfull", "rk"))
        pick = sb("pick", [P, LEVELS, CH // 2])
        A = [sb(f"A{i}", [P, 2, CH]) for i in range(2)]
        kt = sb("kt", [P, P])
        state = sb("state", [P, B, KC, 2 * HD])
        y1, y2, yn = sb("y1", [P, D]), sb("y2", [P, D]), sb("yn", [P, D])
        mean, rinv, var, rstd, power = sb("mean", [P, HEADS]), sb("rinv", [P, HEADS]), sb("var", [P, HEADS]), sb("rstd", [P, HEADS]), sb("power", [P, HEADS])
        ynT = sb("ynT", [P, KC, P])

        pw = [ps(f"pw{i}", [P, 512]) for i in range(2)]
        pa = [ps(f"pa{i}", [P, 2, 512]) for i in range(2)]
        py = ps("py", [P, 512])
        pm = ps("pm", [P, 512])

        ld, vec_in, vec_turned, vec_ready = sem("ld"), sem("vec_in"), sem("vec_turned"), sem("vec_ready")
        consts = sem("pick_ready")
        pairs_seen, tot_seen, zeroed = sem("pairs_seen"), sem("tot_seen"), sem("wkv_zeroed")
        dve_step, pool_step, act_step = sem("dve_step"), sem("pool_step"), sem("act_step")
        xxx_ready, mix_ready, moved, shifted_ready = sem("xxx_ready"), sem("mix_ready"), sem("moved"), sem("shifted_ready")
        wide_done = [sem(f"wide_done{i}") for i in range(2)]
        wide_free = [sem(f"wide_free{i}") for i in range(2)]
        dlow_ready, rkw_ready, tot_ready = sem("dlow_ready"), sem("rkw_ready"), sem("tot_ready")
        left_ready, right_ready, v_ready = sem("left_ready"), sem("right_ready"), sem("v_ready")
        pairs_done, picked, kt_turned, kt_ready, state_inc, state_ready = (
            sem("pairs_done"), sem("picked"), sem("kt_turned"), sem("kt_ready"), sem("state_inc"), sem("state_ready"))
        var_ready, rstd_ready = sem("var_ready"), sem("rstd_ready")
        y_done, y_taken, yn_ready, yn_turned, ynT_ready, o_done, o_taken, step_over = (
            sem("y_done"), sem("y_taken"), sem("yn_ready"), sem("yn_turned"), sem("ynT_ready"), sem("o_done"),
            sem("o_taken"), sem("step_over"))
        block = ctx.enter_context(nc.Block())

        W_JOBS = 18
        F_MIX, F_SHIFT, F_R, F_K, F_LOW, F_DEC, F_V = 0, 1, 9, 11, 13, 14, 16
        vecs = ["maa_x", "maa_w", "maa_k", "maa_v", "maa_r", "decay", "ln_w", "ln_b", "faaaa"]
        PAIRS = CW * B * KC
        TILES = CW * B

        def col(name, c):
            return vec[:, vecs.index(name) * KC + c:vecs.index(name) * KC + c + 1]

        def half(ap, m, side, width=KC * COLS):
            return ap.rearrange("p (n s m) -> p n s m", s=2, m=m)[:, :, side, :]

        def tall(ap, l, side):
            return ap.rearrange("p (n s) -> p n s", s=2)[:, :, side]

        def take(eng, i, job):
            eng.wait_ge(wide_done[job % 2], i * (W_JOBS // 2) + job // 2 + 1)

        @block.sync
        def _(sp):
            for n, (name, cols) in enumerate((("W_r", wr), ("W_k", wk), ("W_v", wv), ("W_o", wo), ("maa_w1", maa1),
                                              ("decay_w1", dw1))):
                sp.dma_start(cols[:], d[name].rearrange("(k p) n -> p k n", p=P)).then_inc(ld, 16)
            sp.dma_start(maa2[:], d["maa_w2"].rearrange("f l c -> (f l) c")).then_inc(ld, 16)
            sp.dma_start(dw2[:], d["decay_w2"]).then_inc(ld, 16)
            for n, name in enumerate(vecs):
                src = d[name].rearrange("h i -> (h i)") if name == "faaaa" else d[name]
                sp.dma_start(vec_rows[n * KC:(n + 1) * KC, :], src.rearrange("(k p) -> k p", p=P)).then_inc(vec_in, 16)

        @block.tensor
        def _(pe):
            pe.wait_ge(vec_in, 16 * NV)
            nc.tensor.transpose(py[:, 0:NV * KC], vec_rows[:], t["ident"][0:NV * KC, 0:NV * KC]).then_inc(vec_turned, 1)
            pe.wait_ge(ld, 16 * 8)
            pe.wait_ge(vec_ready, 1)
            with pe.Fori(0, NI) as i:
                def give(job):
                    pe.wait_ge(wide_free[job % 2], 1 + i * (W_JOBS // 2) + job // 2)
                    return pw[job % 2]

                pe.wait_ge(xxx_ready, i + 1)
                o = give(F_MIX)
                for c in range(KC):
                    last = nc.tensor.matmul(o[:], maa1[:, c, :], xxx[:, c].rearrange("p b w -> p (b w)"),
                                            start=(c == 0), stop=(c == KC - 1))
                last.then_inc(wide_done[F_MIX % 2], 1)
                pe.wait_ge(mix_ready, i + 1)
                for f in range(4):
                    for c in range(KC):
                        job = F_SHIFT + f * KC + c
                        o = give(job)
                        nc.tensor.matmul(o[:], maa2[32 * f:32 * f + 32, c * P:(c + 1) * P], mix[32 * f:32 * f + 32, :],
                                         start=True, stop=True, tile_position=(32 * f, 0)).then_inc(wide_done[job % 2], 1)
                for job0, wt, f in ((F_R, wr, 3), (F_K, wk, 1)):
                    pe.wait_ge(shifted_ready, i * 4 + 4)
                    for c in range(KC):
                        o = give(job0 + c)
                        for kk in range(KC):
                            last = nc.tensor.matmul(o[:], wt[:, kk, c * P:(c + 1) * P],
                                                    shifted[f][:, kk].rearrange("p b w -> p (b w)"),
                                                    start=(kk == 0), stop=(kk == KC - 1))
                        last.then_inc(wide_done[(job0 + c) % 2], 1)
                o = give(F_LOW)
                for kk in range(KC):
                    last = nc.tensor.matmul(o[0:DEC, :], dw1[:, kk, :], shifted[0][:, kk].rearrange("p b w -> p (b w)"),
                                            start=(kk == 0), stop=(kk == KC - 1))
                last.then_inc(wide_done[F_LOW % 2], 1)
                pe.wait_ge(dlow_ready, i + 1)
                for c in range(KC):
                    o = give(F_DEC + c)
                    nc.tensor.matmul(o[:], dw2[:, c * P:(c + 1) * P], dlow[:], start=True,
                                     stop=True).then_inc(wide_done[(F_DEC + c) % 2], 1)
                for h in range(2):
                    o = give(F_V + h)
                    for q in range(2):
                        tile = 2 * h + q
                        for kk in range(KC):
                            last = nc.tensor.matmul(o[:, q * D:(q + 1) * D],
                                                    shifted[2][:, kk, tile // CW, (tile % CW) * CH:(tile % CW + 1) * CH],
                                                    wv[:, kk, :], start=(kk == 0), stop=(kk == KC - 1))
                    last.then_inc(wide_done[(F_V + h) % 2], 1)

                pe.wait_ge(left_ready, i + 1)
                pe.wait_ge(right_ready, i + 1)
                pe.wait_ge(v_ready, i * 2 + 2)

                def pairs(u):
                    ck, b, c = u // (B * KC), u // KC % B, u % KC
                    first = c * COLS + b * W + ck * CH
                    if u >= 2:
                        pe.wait_ge(picked, 1 + i * PAIRS + u - 1)
                    else:
                        pe.wait_ge(picked, 1 + i * PAIRS)
                    for h in range(2):
                        hs = slice(HD * h, HD * h + HD)
                        for l in range(LEVELS):
                            if l == 0:
                                rhs = tall(r[hs, first:first + CH], 0, 1)
                            else:
                                rhs = rp[l][hs, first // 2:first // 2 + CH // 2]
                            last = nc.tensor.matmul(pa[u % 2][:, h, l * CH // 2:(l + 1) * CH // 2],
                                                    kq[l][hs, first:first + CH], rhs, start=True, stop=True)
                    last.then_inc(pairs_done, 1)

                def outputs(u):
                    ck, b, c = u // (B * KC), u // KC % B, u % KC
                    first, tile = c * COLS + b * W + ck * CH, b * CW + ck
                    n = u // KC
                    if c == 0 and n > 0:
                        pe.wait_ge(o_taken, 1 + i * TILES + n)
                    elif c == 0:
                        pe.wait_ge(o_taken, 1 + i * TILES)
                    else:
                        pe.wait_ge(state_ready, 1 + i * PAIRS + u)
                    nc.tensor.transpose(pm[:, 0:P], kfull[:, first:first + CH], t["ident"][:]).then_inc(kt_turned, 1)
                    if c == 0:
                        pe.wait_ge(y_taken, 1 + i * TILES + n)
                    pe.wait_ge(picked, 1 + i * PAIRS + u + 1)
                    pe.wait_ge(state_ready, 1 + i * PAIRS + (u - B * KC + 1 if ck > 0 else 0))
                    nc.tensor.matmul(py[:, c * P:(c + 1) * P], rfull[:, first:first + CH], state[:, b, c, :],
                                     start=True, stop=True)
                    for h in range(2):
                        o = py[:, (2 * c + h) * HD:(2 * c + h + 1) * HD]
                        nc.tensor.matmul(o, A[u % 2][:, h, :], v[:, tile, (2 * c + h) * HD:(2 * c + h + 1) * HD],
                                         start=False, stop=True, skip_group_check=True)
                    pe.wait_ge(kt_ready, i * PAIRS + u + 1)
                    nc.tensor.matmul(pm[:, P:2 * P], kt[:], v[:, tile, c * P:(c + 1) * P], start=True,
                                     stop=True).then_inc(state_inc, 1)
                    if c == KC - 1:
                        for kk in range(KC):
                            f0 = kk * COLS + b * W + ck * CH
                            last = nc.tensor.matmul(py[:, D:D + HEADS], rk[:, f0:f0 + CH], bonus_sel[:, kk, :],
                                                    start=(kk == 0), stop=(kk == KC - 1))
                        last.then_inc(y_done, 1)

                def project(n):
                    pe.wait_ge(yn_ready, i * TILES + n + 1)
                    pe.wait_ge(state_ready, 1 + i * PAIRS + KC * (n + 1))
                    for kk in range(KC):
                        last = nc.tensor.transpose(pm[:, kk * P:(kk + 1) * P], yn[:, kk * P:(kk + 1) * P], t["ident"][:])
                    last.then_inc(yn_turned, 1)
                    pe.wait_ge(ynT_ready, i * TILES + n + 1)
                    for kk in range(KC):
                        last = nc.tensor.matmul(pm[:, D:2 * D], ynT[:, kk, :], wo[:, kk, :], start=(kk == 0), stop=(kk == KC - 1))
                    last.then_inc(o_done, 1)

                pairs(0)
                for u in range(PAIRS):
                    if u + 1 < PAIRS:
                        pairs(u + 1)
                    outputs(u)
                    if u % KC == KC - 1:
                        project(u // KC)

        @block.scalar
        def _(act):
            act.wait_ge(vec_turned, 1)
            nc.scalar.activation(vec[:], py[:, 0:NV * KC], ACT.Copy).then_inc(vec_ready, 1)
            act.wait_ge(vec_ready, 1)
            with act.Fori(0, NI) as i:
                take(act, i, F_MIX)
                nc.scalar.activation(mix[:], pw[F_MIX % 2][:], ACT.Tanh).then_inc(mix_ready, 1)
                act.wait_ge(mix_ready, i + 1)
                act.sem_inc(wide_free[F_MIX % 2], 1)
                for job, dst in ((F_R, r), (F_K, k)):
                    for c in range(KC):
                        take(act, i, job + c)
                        nc.scalar.activation(dst[:, c * COLS:(c + 1) * COLS], pw[(job + c) % 2][:],
                                             ACT.Copy).then_inc(wide_free[(job + c) % 2], 1)
                take(act, i, F_LOW)
                nc.scalar.activation(dlow[:], pw[F_LOW % 2][0:DEC, :], ACT.Tanh).then_inc(dlow_ready, 1)
                act.wait_ge(dlow_ready, i + 1)
                act.sem_inc(wide_free[F_LOW % 2], 1)
                for c in range(KC):
                    take(act, i, F_DEC + c)
                    nc.scalar.activation(ew[:, c * COLS:(c + 1) * COLS], pw[(F_DEC + c) % 2][:], ACT.Exp,
                                         bias=col("decay", c)).then_inc(wide_free[(F_DEC + c) % 2], 1)
                act.wait_ge(wide_free[(F_DEC + 1) % 2], 1 + i * (W_JOBS // 2) + (F_DEC + 1) // 2 + 1)
                act.wait_ge(wide_free[F_DEC % 2], 1 + i * (W_JOBS // 2) + F_DEC // 2 + 1)
                nc.scalar.activation(w[:], ew[:], ACT.Exp, scale=-1.0).then_inc(rkw_ready, 1)
                for u in range(PAIRS):
                    act.wait_ge(kt_turned, i * PAIRS + u + 1)
                    nc.scalar.activation(kt[:], pm[:, 0:P], ACT.Copy).then_inc(kt_ready, 1)
                    if u % KC == KC - 1:
                        n = u // KC
                        act.wait_ge(yn_turned, i * TILES + n + 1)
                        for kk in range(KC):
                            last = nc.scalar.activation(ynT[:, kk, :], pm[:, kk * P:(kk + 1) * P], ACT.Identity,
                                                        scale=col("ln_w", kk), bias=col("ln_b", kk))
                        last.then_inc(ynT_ready, 1)

        @block.gpsimd
        def _(pool):
            steps = [0]

            nc.gpsimd.memset(power[:], -0.5)
            nc.gpsimd.memset(pick[:], 1.0).then_inc(pool_step, 1)
            steps[0] = 1
            for l in range(LEVELS):
                m = 1 << l
                view = pick[:, l, :].rearrange("p (n m) -> p n m", m=m)
                for mult, pat, base in ((1, -2 * m, 0), (-1, 2 * m, m - 1)):
                    pool.wait_ge(pool_step, steps[0])
                    nc.gpsimd.affine_select(out=view, in_=view, compare_op=ALU.is_ge, fill=0.0, base=base,
                                            pattern=[[pat, CH // 2 // m], [0, m]],
                                            channel_multiplier=mult).then_inc(pool_step, 1)
                    steps[0] += 1
            nc.gpsimd.memset(bonus_sel[:], 0.0).then_inc(pool_step, 1)
            steps[0] += 1
            pool.wait_ge(pool_step, steps[0])
            pool.wait_ge(vec_ready, 1)
            for c in range(KC):
                for h in range(2):
                    hs = slice(HD * h, HD * h + HD)
                    nc.gpsimd.tensor_copy(bonus_sel[hs, c, 2 * c + h:2 * c + h + 1],
                                          vec[hs, vecs.index("faaaa") * KC + c:vecs.index("faaaa") * KC + c + 1]).then_inc(pool_step, 1)
                    steps[0] += 1
                    pool.wait_ge(pool_step, steps[0])
            pool.sem_inc(consts, 1)
            pool.wait_ge(zeroed, 1)
            with pool.Fori(0, NI) as i:
                pool.sem_clear(pool_step)
                done = [0]

                def link(ins):
                    done[0] += 1
                    ins.then_inc(pool_step, 1)
                    pool.wait_ge(pool_step, done[0])

                for f in range(4):
                    pool.wait_ge(moved, i * 4 + f + 1)
                    link(nc.gpsimd.tensor_tensor(shifted[f][:], shifted[f][:], cur[:], ALU.add))
                    pool.sem_inc(shifted_ready, 1)
                pool.wait_ge(rkw_ready, i + 1)
                link(nc.gpsimd.tensor_tensor(rk[:], r[:], k[:], ALU.mult))
                pool.wait_ge(tot_ready, i + 1)
                pool.sem_inc(tot_seen, 1)
                nc.gpsimd.memset(half(suf[:], 1, 1), 1.0)
                link(nc.gpsimd.tensor_copy(half(suf[:], 1, 0), half(w[:], 1, 1)))
                for l in range(1, LEVELS):
                    m = 1 << l
                    link(nc.gpsimd.tensor_tensor(half(kq[l][:], m, 0), half(k[:], m, 0), half(suf[:], m, 0), ALU.mult))
                    link(nc.gpsimd.tensor_tensor(half(suf[:], m, 0), half(suf[:], m, 0),
                                                 tall(tot[l][:], l, 1).unsqueeze(2).to_broadcast([P, (KC * COLS) // (2 * m), m]),
                                                 ALU.mult))
                link(nc.gpsimd.tensor_tensor(kfull[:], k[:], suf[:], ALU.mult))
                pool.sem_inc(left_ready, 1)
                for n in range(TILES):
                    pool.wait_ge(var_ready, i * TILES + n + 1)
                    nc.gpsimd.tensor_tensor(rinv[:], rstd[:], power[:], ALU.pow).then_inc(rstd_ready, 1)

        @block.vector
        def _(dve):
            for primed in (*wide_free, picked, o_taken, state_ready, y_taken):
                dve.sem_inc(primed, 1)
            nc.vector.memset(state[:], 0.0)
            nc.vector.memset(A[0][:], 0.0)
            nc.vector.memset(A[1][:], 0.0)
            for l in range(1, LEVELS):
                nc.vector.memset(kq[l][:], 0.0)
            nc.vector.memset(t["qT"][:, :, :, 0:1], 0.0).then_inc(zeroed, 1)
            dve.wait_ge(zeroed, 1)
            dve.wait_ge(vec_ready, 1)
            dve.wait_ge(consts, 1)
            with dve.Fori(0, NI) as i:
                dve.sem_clear(dve_step)
                done = [0]

                def link(ins):
                    done[0] += 1
                    ins.then_inc(dve_step, 1)
                    dve.wait_ge(dve_step, done[0])

                nc.vector.tensor_copy(cur[:].rearrange("p k b w -> p (k b) w"), qcols(t, i, W, 1))
                link(nc.vector.tensor_tensor(xx[:].rearrange("p k b w -> p (k b) w"), qcols(t, i, W, 0), qcols(t, i, W, 1),
                                             ALU.subtract))
                for c in range(KC):
                    last = nc.vector.scalar_tensor_tensor(xxx[:, c], xx[:, c], col("maa_x", c), cur[:, c], ALU.mult, ALU.add)
                last.then_inc(xxx_ready, 1)
                for f in range(4):
                    for c in range(KC):
                        job = F_SHIFT + f * KC + c
                        take(dve, i, job)
                        nc.vector.scalar_tensor_tensor(shifted[f][:, c].rearrange("p b w -> p (b w)"), pw[job % 2][:],
                                                       col(vecs[1 + f], c), xx[:, c].rearrange("p b w -> p (b w)"),
                                                       ALU.add, ALU.mult).then_inc(wide_free[job % 2], 1)
                    dve.wait_ge(wide_free[job % 2], 1 + i * (W_JOBS // 2) + job // 2 + 1)
                    dve.wait_ge(wide_free[(job - 1) % 2], 1 + i * (W_JOBS // 2) + (job - 1) // 2 + 1)
                    dve.sem_inc(moved, 1)
                dve.wait_ge(rkw_ready, i + 1)
                for l in range(LEVELS):
                    link(nc.vector.tensor_tensor(tot[l + 1][:], tall(tot[l][:], l, 0), tall(tot[l][:], l, 1), ALU.mult))
                dve.sem_inc(tot_ready, 1)
                for h in range(2):
                    take(dve, i, F_V + h)
                    nc.vector.tensor_copy(v[:, 2 * h:2 * h + 2, :].rearrange("p t c -> p (t c)"),
                                          pw[(F_V + h) % 2][:]).then_inc(wide_free[(F_V + h) % 2], 1)
                dve.wait_ge(wide_free[(F_V + 1) % 2], 1 + i * (W_JOBS // 2) + (F_V + 1) // 2 + 1)
                dve.sem_inc(v_ready, 2)
                nc.vector.memset(half(pre[:], 1, 0), 1.0)
                link(nc.vector.tensor_copy(half(pre[:], 1, 1), half(w[:], 1, 0)))
                for l in range(1, LEVELS):
                    m = 1 << l
                    link(nc.vector.tensor_tensor(rp[l][:].rearrange("p (n m) -> p n m", m=m), half(r[:], m, 1),
                                                 half(pre[:], m, 1), ALU.mult))
                    link(nc.vector.tensor_tensor(half(pre[:], m, 1), half(pre[:], m, 1),
                                                 tall(tot[l][:], l, 0).unsqueeze(2).to_broadcast([P, (KC * COLS) // (2 * m), m]),
                                                 ALU.mult))
                link(nc.vector.tensor_tensor(rfull[:], r[:], pre[:], ALU.mult))
                dve.sem_inc(right_ready, 1)

                def choose(u):
                    dve.wait_ge(pairs_done, i * PAIRS + u + 1)
                    dve.sem_inc(pairs_seen, 1)
                    for l in range(LEVELS):
                        m = 1 << l
                        shape = [P, 2, CH // 2 // m, m]
                        link(nc.vector.copy_predicated(
                            A[u % 2][:].rearrange("p h (n s m) -> p h n s m", s=2, m=m)[:, :, :, 1, :],
                            pick[:, l, :].bitcast(I32).rearrange("p (n m) -> p n m", m=m).unsqueeze(1).to_broadcast(shape),
                            pa[u % 2][:, :, l * CH // 2:(l + 1) * CH // 2].rearrange("p h (n m) -> p h n m", m=m)))
                    dve.sem_inc(picked, 1)

                def advance(u):
                    ck, b, c = u // (B * KC), u // KC % B, u % KC
                    dve.wait_ge(state_inc, i * PAIRS + u + 1)
                    if ck > 0:
                        dve.wait_ge(state_ready, 1 + i * PAIRS + u - B * KC + 1)
                    tb = (c * COLS + b * W) // CH + ck
                    for h in range(2):
                        hs = slice(HD * h, HD * h + HD)
                        own = state[hs, b, c, HD * h:HD * h + HD]
                        last = nc.vector.scalar_tensor_tensor(own, own,
                                                              tot[LEVELS][hs, tb:tb + 1],
                                                              pm[hs, P + HD * h:P + HD * h + HD], ALU.mult, ALU.add)
                    last.then_inc(state_ready, 1)

                def normalise(n):
                    ck, b = n // B, n % B
                    tile = b * CW + ck
                    dve.wait_ge(y_done, i * TILES + n + 1)
                    heads = [P, HEADS, HD]
                    y1v, y2v, ynv = (a[:].rearrange("p (h j) -> p h j", j=HD) for a in (y1, y2, yn))
                    vv = v[:, tile, :].rearrange("p (h j) -> p h j", j=HD)
                    link(nc.vector.tensor_tensor(y1v, vv, py[:, D:D + HEADS].unsqueeze(2).to_broadcast(heads), ALU.mult))
                    link(nc.vector.tensor_tensor(y1[:], y1[:], py[:, 0:D], ALU.add))
                    dve.sem_inc(y_taken, 1)
                    link(nc.vector.tensor_reduce(mean[:], y1v, AX.X, ALU.add))
                    link(nc.vector.tensor_scalar(mean[:], mean[:], 1.0 / HD, None, ALU.mult))
                    link(nc.vector.tensor_tensor(y1v, y1v, mean[:].unsqueeze(2).to_broadcast(heads), ALU.subtract))
                    link(nc.vector.tensor_tensor(y2[:], y1[:], y1[:], ALU.mult))
                    link(nc.vector.tensor_reduce(var[:], y2v, AX.X, ALU.add))
                    link(nc.vector.tensor_scalar(rstd[:], var[:], 1.0 / HD, LN_EPS, ALU.mult, ALU.add))
                    dve.sem_inc(var_ready, 1)
                    dve.wait_ge(rstd_ready, i * TILES + n + 1)
                    link(nc.vector.tensor_tensor(ynv, y1v, rinv[:].unsqueeze(2).to_broadcast(heads), ALU.mult))
                    dve.sem_inc(yn_ready, 1)

                def residual(n):
                    ck, b = n // B, n % B
                    dve.wait_ge(o_done, i * TILES + n + 1)
                    at = t["x_tok"][:, bass.ds(i * CW + (b * (NT // B) + ck), 1), :].rearrange("p t c -> p (t c)")
                    nc.vector.tensor_tensor(at, at, pm[:, D:2 * D], ALU.add).then_inc(o_taken, 1)

                choose(0)
                for u in range(PAIRS):
                    if u + 1 < PAIRS:
                        choose(u + 1)
                    advance(u)
                    if u % KC == KC - 1:
                        normalise(u // KC)
                        residual(u // KC)


def condition(nc, d, t):
    with ExitStack() as ctx:
        def sb(name, shape, dt=F32):
            return ctx.enter_context(nc.sbuf_tensor("c_" + name, shape, dt))

        def ps(name, shape, dt=F32):
            return ctx.enter_context(nc.psum_tensor("c_" + name, shape, dt))

        def sem(name):
            return ctx.enter_context(nc.semaphore("c_" + name))

        wp, wm = sb("wp", [P, KC, D]), sb("wm", [P, 2 * KC, D])
        wr = sb("wr", [P, KC, E2])
        cond_col, bp_col = sb("cond_col", [P, KC, B]), sb("bp_col", [P, KC])
        u_col, u_rep, u_row = sb("u_col", [P, KC, B]), sb("u_rep", [P, KC, B, P]), sb("u_row", [P, B, D])
        br = sb("br", [P, E2])
        xg = sb("xg", [P, GT, D])
        xT, hT = sb("xT", [P, KC, GT * P]), sb("hT", [P, KC, GT * P])
        hg = sb("hg", [P, GT, D])
        logits, top, total = sb("logits", [P, NT, E2]), sb("top", [P, NT]), sb("total", [P, NT])
        tp = ps("tp", [P, KC, GT * P])
        hp = ps("hp", [P, GT, D])
        rp = ps("rp", [P, 512])
        up = ps("up", [P, 512])
        weights_in, cols_in, u_sum, u_ready, rep_ready, urow_done, urow_ready = (
            sem("weights_in"), sem("cols_in"), sem("u_sum"), sem("u_ready"), sem("rep_ready"), sem("urow_done"),
            sem("urow_ready"))
        h_kept = sem("h_kept")
        xg_ready, x_turned, xT_ready, h_done, h_ready, h_turned, hT_ready, r_done, r_ready, step_done, exp_done = (
            sem("xg_ready"), sem("x_turned"), sem("xT_ready"), sem("h_done"), sem("h_ready"), sem("h_turned"),
            sem("hT_ready"), sem("r_done"), sem("r_ready"), sem("step_done"), sem("exp_done"))
        block = ctx.enter_context(nc.Block())

        @block.sync
        def _(sp):
            sp.dma_start(wp[:], d["W_proj"].rearrange("(k p) n -> p k n", p=P)).then_inc(weights_in, 16)
            sp.dma_start(wm[:], d["weight_matrix"].rearrange("(k p) n -> p k n", p=P)).then_inc(weights_in, 16)
            sp.dma_start(wr[:], d["Wr"].rearrange("(k p) n -> p k n", p=P)).then_inc(weights_in, 16)
            sp.dma_start(br[:], d["br"].unsqueeze(0).to_broadcast([P, E2])).then_inc(weights_in, 16)

        @block.gpsimd
        def _(pool):
            with nc.allow_non_contiguous_dma(reason="768 values, once"):
                for b in range(B):
                    pool.dma_start(cond_col[:, :, b], d["cond"][b].rearrange("(k p) -> p k", p=P)).then_inc(cols_in, 16)
                pool.dma_start(bp_col[:], d["b_proj"].rearrange("(k p) -> p k", p=P)).then_inc(cols_in, 16)
            with pool.Fori(0, NG) as g:
                pool.wait_ge(x_turned, 1 + g)
                nc.gpsimd.tensor_copy(xg[:], t["x_tok"][:, bass.ds(g * GT, GT), :]).then_inc(xg_ready, 1)
                pool.wait_ge(h_ready, 1 + g + 1)
                nc.gpsimd.tensor_copy(t["acc"][:, bass.ds(g * GT, GT), :], hg[:]).then_inc(h_kept, 1)

        @block.tensor
        def _(pe):
            pe.wait_ge(weights_in, 64)
            pe.wait_ge(cols_in, 48)
            for c in range(KC):
                for k in range(KC):
                    last = nc.tensor.matmul(up[:, c * B:(c + 1) * B], wp[:, k, c * P:(c + 1) * P], cond_col[:, k, :],
                                            start=(k == 0), stop=(k == KC - 1))
            last.then_inc(u_sum, 1)
            pe.wait_ge(rep_ready, 1)
            for b in range(B):
                for k in range(KC):
                    last = nc.tensor.matmul(up[:, b * D:(b + 1) * D], u_rep[:, k, b, :], wm[:, k, :],
                                            start=(k == 0), stop=(k == KC - 1))
            last.then_inc(urow_done, 1)
            with pe.Fori(0, NG) as g:
                pe.wait_ge(xg_ready, g + 1)
                pe.wait_ge(hT_ready, 1 + g)
                for tt in range(GT):
                    for k in range(KC):
                        last = nc.tensor.transpose(tp[:, k, tt * P:(tt + 1) * P], xg[:, tt, k * P:(k + 1) * P], t["ident"][:])
                last.then_inc(x_turned, 1)
                pe.wait_ge(xT_ready, g + 1)
                pe.wait_ge(h_ready, 1 + g)
                for tt in range(GT):
                    for k in range(KC):
                        last = nc.tensor.matmul(hp[:, tt, :], xT[:, k, tt * P:(tt + 1) * P], wm[:, KC + k, :],
                                                start=(k == 0), stop=(k == KC - 1))
                last.then_inc(h_done, 1)
                pe.wait_ge(h_ready, 1 + g + 1)
                for tt in range(GT):
                    for k in range(KC):
                        last = nc.tensor.transpose(tp[:, k, tt * P:(tt + 1) * P], hg[:, tt, k * P:(k + 1) * P], t["ident"][:])
                last.then_inc(h_turned, 1)
                pe.wait_ge(hT_ready, 1 + g + 1)
                pe.wait_ge(r_ready, 1 + g)
                for tt in range(GT):
                    for k in range(KC):
                        last = nc.tensor.matmul(rp[:, tt * E2:(tt + 1) * E2], hT[:, k, tt * P:(tt + 1) * P], wr[:, k, :],
                                                start=(k == 0), stop=(k == KC - 1))
                last.then_inc(r_done, 1)

        @block.scalar
        def _(act):
            act.wait_ge(u_sum, 1)
            act.wait_ge(cols_in, 48)
            for c in range(KC):
                last = nc.scalar.activation(u_col[:, c, :], up[:, c * B:(c + 1) * B], ACT.Gelu, bias=bp_col[:, c:c + 1])
            last.then_inc(u_ready, 1)
            act.wait_ge(u_ready, 1)
            for k in range(KC):
                for b in range(B):
                    last = nc.scalar.activation(u_rep[:, k, b, :], u_col[:, k, b:b + 1].to_broadcast([P, P]), ACT.Copy)
            last.then_inc(rep_ready, 1)
            with act.Fori(0, NG) as g:
                act.wait_ge(x_turned, 1 + g + 1)
                for k in range(KC):
                    last = nc.scalar.activation(xT[:, k, :], tp[:, k, :], ACT.Copy)
                last.then_inc(xT_ready, 1)
                act.wait_ge(h_turned, g + 1)
                for k in range(KC):
                    last = nc.scalar.activation(hT[:, k, :], tp[:, k, :], ACT.Copy)
                last.then_inc(hT_ready, 1)
            act.wait_ge(step_done, 3)
            nc.scalar.activation(logits[:], logits[:], ACT.Exp).then_inc(exp_done, 1)

        @block.vector
        def _(dve):
            for primed in (x_turned, hT_ready, h_ready, r_ready, h_kept):
                dve.sem_inc(primed, 1)
            dve.wait_ge(urow_done, 1)
            nc.vector.tensor_copy(u_row[:].rearrange("p b c -> p (b c)"), up[:]).then_inc(urow_ready, 1)
            dve.wait_ge(urow_ready, 1)
            dve.wait_ge(weights_in, 64)
            for b in range(B):
                with dve.Fori(b * NG // B, (b + 1) * NG // B) as g:
                    dve.wait_ge(h_done, g + 1)
                    dve.wait_ge(h_kept, 1 + g)
                    nc.vector.tensor_tensor(hg[:], hp[:], u_row[:, b:b + 1, :].to_broadcast([P, GT, D]),
                                            ALU.add).then_inc(h_ready, 1)
                    dve.wait_ge(r_done, g + 1)
                    nc.vector.tensor_tensor(logits[:, bass.ds(g * GT, GT), :],
                                            rp[:, 0:GT * E2].rearrange("p (t e) -> p t e", e=E2),
                                            br[:].unsqueeze(1).to_broadcast([P, GT, E2]), ALU.add).then_inc(r_ready, 1)
            dve.wait_ge(r_ready, 1 + NG)
            wide = [P, NT, E2]
            nc.vector.tensor_reduce(top[:], logits[:], AX.X, ALU.max).then_inc(step_done, 1)
            dve.wait_ge(step_done, 1)
            nc.vector.tensor_tensor(logits[:], logits[:], top[:].unsqueeze(2).to_broadcast(wide),
                                    ALU.subtract).then_inc(step_done, 2)
            dve.wait_ge(exp_done, 1)
            nc.vector.tensor_reduce(total[:], logits[:], AX.X, ALU.add).then_inc(step_done, 1)
            dve.wait_ge(step_done, 4)
            nc.vector.reciprocal(total[:], total[:]).then_inc(step_done, 1)
            dve.wait_ge(step_done, 5)
            nc.vector.tensor_tensor(t["score2"][:], logits[:], total[:].unsqueeze(2).to_broadcast(wide),
                                    ALU.mult).then_inc(step_done, 1)
            dve.wait_ge(step_done, 6)
            nc.vector.tensor_copy(t["sel2"][:], t["score2"][:])


def constants(nc, t):
    with nc.semaphore("filled") as filled, nc.semaphore("shaped") as shaped, nc.Block() as block:
        @block.gpsimd
        def _(pool):
            nc.gpsimd.memset(t["ident"][:], 0.0)
            nc.gpsimd.memset(t["ones"][:], 1.0)
            nc.gpsimd.memset(t["before"][:], 1.0).then_inc(filled, 1)
            nc.gpsimd.iota(t["first1"][:], [[0, NT], [-1, E1]], base=E1, channel_multiplier=0,
                           allow_small_or_imprecise_dtypes=True)
            nc.gpsimd.iota(t["first2"][:], [[0, NT], [-1, E2]], base=E2, channel_multiplier=0,
                           allow_small_or_imprecise_dtypes=True)
            nc.gpsimd.iota(t["slot_no"][:], [[1, S2], [0, E2]], base=0, channel_multiplier=0,
                           allow_small_or_imprecise_dtypes=True)
            pool.wait_ge(filled, 1)
            nc.gpsimd.affine_select(out=t["ident"][:], in_=t["ident"][:], compare_op=ALU.not_equal, fill=1.0, base=0,
                                    pattern=[[-1, P]], channel_multiplier=1)
            nc.gpsimd.affine_select(out=t["before"][:], in_=t["before"][:], compare_op=ALU.is_ge, fill=0.0, base=-1,
                                    pattern=[[1, P]], channel_multiplier=-1)


def program(nc, d, out):
    with ExitStack() as ctx:
        def sb(name, shape, dt=F32):
            return ctx.enter_context(nc.sbuf_tensor(name, shape, dt))

        rows1 = nc.dram_tensor("rows1", [S1, P, D], F32, kind="Internal").ap()
        outs1 = nc.dram_tensor("outs1", [S1, P, D], F32, kind="Internal").ap()
        rows2 = nc.dram_tensor("rows2", [S2, P, D], F32, kind="Internal").ap()
        outs2 = nc.dram_tensor("outs2", [S2, P, D], F32, kind="Internal").ap()
        flat = lambda a: a.rearrange("s p c -> (s p) c")
        d["rows1"], d["rows2"] = flat(rows1), flat(rows2)
        out_tiles = out.rearrange("b (t p) c -> p (b t) c", p=P)
        t = {
            "ident": sb("ident", [P, P]), "ones": sb("ones", [P, P]), "before": sb("before", [P, P]),
            "first1": sb("first1", [P, NT, E1]), "first2": sb("first2", [P, NT, E2]),
            "slot_no": sb("slot_no", [P, S2, E2]),
            "score1": sb("score1", [P, NT, E1]), "sel1": sb("sel1", [P, NT, E1]),
            "score2": sb("score2", [P, NT, E2]), "sel2": sb("sel2", [P, NT, E2]),
            "a_gate": sb("a_gate", [P, 2, NT]), "a_row": sb("a_row", [P, 2, NT], U32), "a_owner": sb("a_owner", [P, S1], I32),
            "b_gate": sb("b_gate", [P, 2, NT]), "b_row": sb("b_row", [P, 2, NT], U32), "b_owner": sb("b_owner", [P, S2], I32),
            "x_tok": sb("x_tok", [P, NT, D]), "acc": sb("acc", [P, NT, D]),
        }

        def dump(src):
            with nc.semaphore("dumped") as s, nc.Block() as block:
                @block.sync
                def _(sp):
                    sp.dma_start(out_tiles, src).then_inc(s, 16)
                    sp.wait_ge(s, 16)

        constants(nc, t)
        dense_front(nc, d, t)
        if STOP == "front":
            return dump(t["acc"][:])
        route(nc, t, E1, S1, t["sel1"], t["score1"], t["first1"], "a_")
        dispatch(nc, t, t["x_tok"], t["a_row"], flat(rows1))
        expert_slots(nc, d, t, "a_", E1, H1, S1, rows1, outs1, d["W1e"], None, d["W2e"], None)
        with nc.sbuf_tensor("qT", [P, KC, B, 1 + SEQ], F32) as qT:
            t["qT"] = qT
            if STOP == "moe":
                combine(nc, t, "a_", t["acc"], flat(outs1), out_tiles)
                return
            combine(nc, t, "a_", t["acc"], flat(outs1), None)
            recurrence(nc, d, t)
        if STOP == "wkv":
            return dump(t["x_tok"][:])
        condition(nc, d, t)
        if STOP == "cond":
            return dump(t["acc"][:])
        route(nc, t, E2, S2, t["sel2"], t["score2"], t["first2"], "b_")
        dispatch(nc, t, t["acc"], t["b_row"], flat(rows2))
        expert_slots(nc, d, t, "b_", E2, H2, S2, rows2, outs2, d["W1"], d["b1"], d["W2"], d["b2"])
        combine(nc, t, "b_", t["x_tok"], flat(outs2), out_tiles)


_NAMES = {
    "x": "x", "cond": "cond_1024", "router_W": "L0_cond_router_W", "router_bias": "L0_cond_router_bias",
    "w1": "L0_cond_w1", "w3": "L0_cond_w3", "w2": "L0_cond_w2", "W1e": "L0_cond_W1e", "W2e": "L0_cond_W2e",
    "maa_x": "L0_attn_time_maa_x", "maa_w": "L0_attn_time_maa_w", "maa_k": "L0_attn_time_maa_k",
    "maa_v": "L0_attn_time_maa_v", "maa_r": "L0_attn_time_maa_r", "maa_w1": "L0_attn_time_maa_w1",
    "maa_w2": "L0_attn_time_maa_w2", "decay": "L0_attn_time_decay", "decay_w1": "L0_attn_time_decay_w1",
    "decay_w2": "L0_attn_time_decay_w2", "faaaa": "L0_attn_time_faaaa", "W_r": "L0_attn_W_r", "W_k": "L0_attn_W_k",
    "W_v": "L0_attn_W_v", "W_o": "L0_attn_W_o", "ln_w": "L0_attn_ln_w", "ln_b": "L0_attn_ln_b",
    "weight_matrix": "L0_cond2_weight_matrix", "W_proj": "L0_cond2_W_proj", "b_proj": "L0_cond2_b_proj",
    "Wr": "L0_ffn_Wr", "br": "L0_ffn_br", "W1": "L0_ffn_W1", "b1": "L0_ffn_b1", "W2": "L0_ffn_W2", "b2": "L0_ffn_b2",
}


def kernel(**inputs):
    import numpy as np
    import concourse.bacc as bacc
    from concourse.bass_utils import run_bass_kernel_spmd

    nc = bacc.Bacc("TRN2", target_bir_lowering=False, num_devices=1)
    arrays, dram = {}, {}
    for short, name in _NAMES.items():
        a = np.ascontiguousarray(inputs[name])
        arrays[f"in_{short}"] = a
        dram[short] = nc.dram_tensor(f"in_{short}", a.shape, mybir.dt.from_np(a.dtype), kind="ExternalInput").ap()
    out = nc.dram_tensor("out_0", (B, SEQ, D), F32, kind="ExternalOutput").ap()
    program(nc, dram, out)
    r = run_bass_kernel_spmd(nc, [arrays], core_ids=[0])
    return r.results[0]["out_0"]
```

```python
from contextlib import ExitStack

import concourse.bass as bass
from concourse import mybir

F32 = mybir.dt.float32
I32 = mybir.dt.int32
U32 = mybir.dt.uint32
ALU = mybir.AluOpType
ACT = mybir.ActivationFunctionType
AX = mybir.AxisListType

P = 128
B, SEQ, D = 2, 1024, 256
N = B * SEQ
NT = N // P
KC = D // P
GT = 4
NG = NT // GT
HS = 512
E1, H1 = 8, 256
E2, H2 = 16, 1024
RING = 4
HEADS, HD = 4, 64
MIX, DEC = 32, 64
CH = 128
LEVELS = 7
LN_EPS = 0.00064
STOP = "end"


def slots_for(experts):
    return 2 * N // P + experts - 1


S1, S2 = slots_for(E1), slots_for(E2)


def router_front(nc, d, t):
    with ExitStack() as ctx:
        def sb(name, shape, dt=F32):
            return ctx.enter_context(nc.sbuf_tensor(name, shape, dt))

        def ps(name, shape, dt=F32):
            return ctx.enter_context(nc.psum_tensor(name, shape, dt))

        def sem(name):
            t["used"].append(ctx.enter_context(nc.semaphore(name)))
            return t["used"][-1]

        rw = sb("rw", [P, 2 * KC, E1])
        cond_col, cond_rep = sb("cond_col", [P, KC, B]), sb("cond_rep", [P, KC, B, P])
        bias_rep = sb("bias_rep", [P, E1])
        cond_part, logits = sb("cond_part", [P, B, E1]), sb("logits", [P, NT, E1])
        tp = [ps(f"tp{i}", [P, KC, GT * P]) for i in range(2)]
        rp, cp = ps("rp", [P, 512]), ps("cp", [P, 512])
        rp_t = rp[:, 0:NT * E1].rearrange("p (t e) -> p t e", e=E1)
        cp_b = cp[:, 0:B * E1].rearrange("p (b e) -> p b e", e=E1)
        x_in = [sem(f"x_in{g}") for g in range(NG)]
        zeroed = sem("zeroed")
        rw_in, cond_in, cond_ready, x_turned, xT_ready, c_done, c_taken, logits_done, summed, scores_ready = (
            sem("rw_in"), sem("cond_in"), sem("cond_ready"), sem("x_turned"), sem("xT_ready"), sem("c_done"),
            sem("c_taken"), sem("logits_done"), sem("summed"), sem("scores_ready"))
        block = ctx.enter_context(nc.Block())
        x_rows = d["x"].rearrange("b (t p) c -> p (b t) c", p=P)

        @block.sync
        def _(sp):
            for g in range(NG):
                sp.dma_start(t["x_tok"][:, g * GT:(g + 1) * GT, :], x_rows[:, g * GT:(g + 1) * GT, :]).then_inc(x_in[g], 16)
            sp.dma_start(rw[:], d["router_W"].rearrange("(k p) n -> p k n", p=P)).then_inc(rw_in, 16)
            sp.dma_start(bias_rep[:], d["router_bias"].unsqueeze(0).to_broadcast([P, E1])).then_inc(rw_in, 16)
            for name in ("w1", "w3", "w2"):
                sp.dma_start(t[name][:], d[name].rearrange("(k p) n -> p k n", p=P)).then_inc(t["weights_in"], 16)
            sp.wait_ge(zeroed, 1)
            sp.dma_start(d["rows1"].rearrange("(s p) c -> p s c", p=P),
                         t["zero"][:].unsqueeze(1).to_broadcast([P, S1, D])).then_inc(t["rows_cleared"], 16)

        @block.gpsimd
        def _(pool):
            nc.gpsimd.memset(t["zero"][:], 0.0).then_inc(zeroed, 1)
            with nc.allow_non_contiguous_dma(reason="512 condition values, once"):
                for b in range(B):
                    pool.dma_start(cond_col[:, :, b], d["cond"][b].rearrange("(k p) -> p k", p=P)).then_inc(cond_in, 16)

        @block.tensor
        def _(pe):
            for g in range(NG):
                pe.wait_ge(x_in[g], 16)
                if g >= 2:
                    pe.wait_ge(xT_ready, g - 1)
                for tt in range(GT):
                    for k in range(KC):
                        last = nc.tensor.transpose(tp[g % 2][:, k, tt * P:(tt + 1) * P],
                                                   t["x_tok"][:, g * GT + tt, k * P:(k + 1) * P], t["ident"][:])
                last.then_inc(x_turned, 1)
            pe.wait_ge(rw_in, 32)
            pe.wait_ge(cond_ready, 1)
            for b in range(B):
                for k in range(KC):
                    last = nc.tensor.matmul(cp_b[:, b, :], cond_rep[:, k, b, :], rw[:, KC + k, :],
                                            start=(k == 0), stop=(k == KC - 1))
            last.then_inc(c_done, 1)
            for g in range(NG):
                pe.wait_ge(xT_ready, g + 1)
                for tt in range(g * GT, (g + 1) * GT):
                    for k in range(KC):
                        last = nc.tensor.matmul(rp_t[:, tt, :], t["xT"][:, k, tt * P:(tt + 1) * P], rw[:, k, :],
                                                start=(k == 0), stop=(k == KC - 1))
            last.then_inc(logits_done, 1)

        @block.scalar
        def _(act):
            act.wait_ge(cond_in, 32)
            for k in range(KC):
                for b in range(B):
                    last = nc.scalar.activation(cond_rep[:, k, b, :], cond_col[:, k, b:b + 1].to_broadcast([P, P]),
                                                ACT.Copy)
            last.then_inc(cond_ready, 1)
            for g in range(NG):
                act.wait_ge(x_turned, g + 1)
                for k in range(KC):
                    last = nc.scalar.activation(t["xT"][:, k, g * GT * P:(g + 1) * GT * P], tp[g % 2][:, k, :], ACT.Copy)
                last.then_inc(xT_ready, 1)
            act.wait_ge(summed, 1)
            nc.scalar.activation(t["score1"][:], logits[:], ACT.Sigmoid).then_inc(scores_ready, 1)

        @block.vector
        def _(dve):
            dve.wait_ge(c_done, 1)
            nc.vector.tensor_copy(cond_part[:], cp_b).then_inc(c_taken, 1)
            dve.wait_ge(c_taken, 1)
            dve.wait_ge(logits_done, 1)
            for b in range(B):
                own = slice(b * NT // B, (b + 1) * NT // B)
                last = nc.vector.tensor_tensor(logits[:, own, :], rp_t[:, own, :],
                                               cond_part[:, b:b + 1, :].to_broadcast([P, NT // B, E1]), ALU.add)
            last.then_inc(summed, 1)
            dve.wait_ge(scores_ready, 1)
            dve.wait_ge(rw_in, 32)
            nc.vector.tensor_tensor(t["sel1"][:], t["score1"][:], bias_rep[:].unsqueeze(1).to_broadcast([P, NT, E1]),
                                    ALU.add)


def shared_expert(nc, d, t):
    with ExitStack() as ctx:
        def sb(name, shape, dt=F32):
            return ctx.enter_context(nc.sbuf_tensor(name, shape, dt))

        def ps(name, shape, dt=F32):
            return ctx.enter_context(nc.psum_tensor(name, shape, dt))

        def sem(name):
            t["used"].append(ctx.enter_context(nc.semaphore(name)))
            return t["used"][-1]

        C = HS // P
        w1, w3, w2 = t["w1"], t["w3"], t["w2"]
        sig, gate = sb("sig", [P, 2, GT * P]), sb("gate", [P, 2, GT * P])
        hT = sb("hT", [P, C, GT * P])
        hp, gp, yp = ps("hp", [P, 2, GT * P]), ps("gp", [P, 2, GT * P]), ps("yp", [P, GT, 512])
        mask_step = sem("mask_step")
        h_ready, sig_ready, gate_ready, hT_ready, y_ready, y_out, rows_out = (
            sem("h_ready"), sem("sig_ready"), sem("gate_ready"), sem("hT_ready"), sem("y_ready"), sem("y_out"),
            sem("rows_out"))
        block = ctx.enter_context(nc.Block())

        @block.gpsimd
        def _(pool):
            pool.wait_ge(t["rows_cleared"], 16)
            for tt in range(NT):
                for k in range(2):
                    pool.indirect_dma_start(d["rows1"], bass.IndirectOffsetOnAxis(t["a_row"][:, k, tt:tt + 1], 0),
                                            t["x_tok"][:, tt, :], None).then_inc(rows_out, 16)
            nc.gpsimd.memset(t["pick"][:], 1.0).then_inc(mask_step, 1)
            for l in range(LEVELS):
                m = 1 << l
                view = t["pick"][:, l, :].rearrange("p (n m) -> p n m", m=m)
                for q, (mult, pat, base) in enumerate(((1, -2 * m, 0), (-1, 2 * m, m - 1))):
                    pool.wait_ge(mask_step, 2 * l + q + 1)
                    nc.gpsimd.affine_select(out=view, in_=view, compare_op=ALU.is_ge, fill=0.0, base=base,
                                            pattern=[[pat, CH // 2 // m], [0, m]],
                                            channel_multiplier=mult).then_inc(mask_step, 1)
            pool.wait_ge(rows_out, 32 * NT)

        @block.tensor
        def _(pe):
            pe.wait_ge(t["weights_in"], 48)
            with pe.Fori(0, NG) as g:
                for c in range(C):
                    pe.wait_ge(hT_ready, 1 + g * C + (c - 1 if c >= 2 else 0))
                    for w, o in ((w1, hp), (w3, gp)):
                        for k in range(KC):
                            last = nc.tensor.matmul(o[:, c % 2, :], w[:, k, c * P:(c + 1) * P],
                                                    t["xT"][:, k, bass.ds(g * (GT * P), GT * P)],
                                                    start=(k == 0), stop=(k == KC - 1))
                    last.then_inc(h_ready, 1)
                pe.wait_ge(y_out, 1 + g)
                for c in range(C):
                    pe.wait_ge(hT_ready, 1 + g * C + c + 1)
                    for tt in range(GT):
                        last = nc.tensor.matmul(yp[:, tt, 0:D], hT[:, c, tt * P:(tt + 1) * P], w2[:, c, :],
                                                start=(c == 0), stop=(c == C - 1))
                last.then_inc(y_ready, 1)

        @block.scalar
        def _(act):
            with act.Fori(0, NG) as g:
                for c in range(C):
                    act.wait_ge(h_ready, g * C + c + 1)
                    act.wait_ge(hT_ready, 1 + g * C + (c - 1 if c >= 2 else 0))
                    nc.scalar.activation(sig[:, c % 2, :], hp[:, c % 2, :], ACT.Sigmoid).then_inc(sig_ready, 1)

        @block.vector
        def _(dve):
            for primed in (hT_ready, y_out, y_ready):
                dve.sem_inc(primed, 1)
            with dve.Fori(0, NG) as g:
                for c in range(C):
                    dve.wait_ge(sig_ready, g * C + c + 1)
                    nc.vector.tensor_tensor(gate[:, c % 2, :], sig[:, c % 2, :], hp[:, c % 2, :],
                                            ALU.mult).then_inc(gate_ready, 1)
                    dve.wait_ge(gate_ready, g * C + c + 1)
                    if c == 0:
                        dve.wait_ge(y_ready, 1 + g)
                    nc.vector.tensor_tensor(hT[:, c, :], gate[:, c % 2, :], gp[:, c % 2, :],
                                            ALU.mult).then_inc(hT_ready, 1)
                dve.wait_ge(y_ready, 1 + g + 1)
                nc.vector.tensor_copy(t["acc"][:, bass.ds(g * GT, GT), :], yp[:, :, 0:D]).then_inc(y_out, 1)


def route(nc, t, experts, slots, sel, val, first, tag):
    with ExitStack() as ctx:
        def sb(name, shape, dt=F32):
            return ctx.enter_context(nc.sbuf_tensor(tag + name, shape, dt))

        cand, onehot = sb("cand", [P, NT, experts]), sb("onehot", [P, 2, NT, experts])
        best, order = sb("best", [P, NT]), sb("order", [P, NT])
        both, rank = sb("both", [P, NT, experts]), sb("rank", [P, NT, experts])
        run = sb("run", [P, 2, NT, experts])
        count_i = sb("count_i", [P, experts], I32)
        tiles = sb("tiles", [P, experts])
        ends = sb("ends", [P, 2, experts])
        prod, picked = sb("prod", [P, NT, experts]), sb("picked", [P, NT])
        over = sb("over", [P, slots, experts])
        ends_f = sb("ends_f", [P, slots])
        cp = ctx.enter_context(nc.psum_tensor(tag + "cp", [P, 2, 512], F32))
        if tag == "b_":
            QUARTER = 2 * NT // 4
            place, place_i, place_slot = sb("place", [P, 2 * NT]), sb("place_i", [P, 2 * NT], I32), sb("place_slot", [P, 2 * NT])
            in_row, in_slot = sb("in_row", [P, 2 * NT, P]), sb("in_slot", [P, 2 * NT, slots])
            tk = ctx.enter_context(nc.psum_tensor(tag + "tk", [P, 512], F32))
            row_ready, table_done = (ctx.enter_context(nc.semaphore(tag + n)) for n in ("row_ready", "table_done"))
        counts_ready = ctx.enter_context(nc.semaphore(tag + "counts_ready"))
        both_ready = ctx.enter_context(nc.semaphore(tag + "both_ready"))
        step_done = ctx.enter_context(nc.semaphore(tag + "step_done"))
        block = ctx.enter_context(nc.Block())
        width = NT * experts
        full = [P, NT, experts]

        @block.tensor
        def _(pe):
            pe.wait_ge(both_ready, 1)
            flat = both[:].rearrange("p t e -> p (t e)")
            nc.tensor.matmul(cp[:, 0, 0:width], t["before"][:], flat, start=True, stop=True)
            nc.tensor.matmul(cp[:, 1, 0:width], t["ones"][:], flat, start=True, stop=True).then_inc(counts_ready, 1)
            if tag == "b_":
                for q in range(2 * NT):
                    if q % QUARTER == 0:
                        pe.wait_ge(row_ready, q // QUARTER + 1)
                    last = nc.tensor.matmul(tk[:, 0:slots], in_row[:, q, :], in_slot[:, q, :], start=(q == 0),
                                            stop=(q == 2 * NT - 1))
                last.then_inc(table_done, 1)

        @block.vector
        def _(dve):
            steps = [0]

            def link(ins):
                steps[0] += 1
                ins.then_inc(step_done, 1)
                dve.wait_ge(step_done, steps[0])

            for k in range(2):
                link(nc.vector.tensor_reduce(best[:], sel[:], AX.X, ALU.max))
                link(nc.vector.tensor_tensor(cand[:], sel[:], best[:].unsqueeze(2).to_broadcast(full), ALU.is_equal))
                link(nc.vector.tensor_tensor(cand[:], cand[:], first[:], ALU.mult))
                link(nc.vector.tensor_reduce(order[:], cand[:], AX.X, ALU.max))
                link(nc.vector.tensor_tensor(onehot[:, k], cand[:], order[:].unsqueeze(2).to_broadcast(full),
                                             ALU.is_equal))
                link(nc.vector.tensor_tensor(prod[:], onehot[:, k], val[:], ALU.mult))
                link(nc.vector.tensor_reduce(t[tag + "gate"][:, k, :], prod[:], AX.X, ALU.add))
                if k == 0:
                    link(nc.vector.scalar_tensor_tensor(sel[:], onehot[:, 0], -3.0e38, sel[:], ALU.mult, ALU.add))
            nc.vector.tensor_tensor(both[:], onehot[:, 0], onehot[:, 1], ALU.add).then_inc(both_ready, 1)
            dve.wait_ge(counts_ready, 1)
            total = cp[:, 1, 0:width].rearrange("p (t e) -> p t e", e=experts)
            link(nc.vector.tensor_copy(run[:, 0], total))
            now, d = 0, 1
            while d < NT:
                link(nc.vector.tensor_copy(run[:, 1 - now, 0:d], run[:, now, 0:d]))
                link(nc.vector.tensor_tensor(run[:, 1 - now, d:NT], run[:, now, d:NT], run[:, now, 0:NT - d], ALU.add))
                now, d = 1 - now, 2 * d
            link(nc.vector.tensor_scalar(count_i[:], run[:, now, NT - 1], float(P - 1), None, ALU.add))
            link(nc.vector.tensor_scalar(count_i[:], count_i[:], 7, None, ALU.arith_shift_right))
            link(nc.vector.tensor_copy(tiles[:], count_i[:]))
            link(nc.vector.tensor_copy(ends[:, 0], tiles[:]))
            at, d = 0, 1
            while d < experts:
                link(nc.vector.tensor_copy(ends[:, 1 - at, 0:d], ends[:, at, 0:d]))
                link(nc.vector.tensor_tensor(ends[:, 1 - at, d:experts], ends[:, at, d:experts],
                                             ends[:, at, 0:experts - d], ALU.add))
                at, d = 1 - at, 2 * d
            link(nc.vector.tensor_tensor(rank[:], run[:, now], total, ALU.subtract))
            link(nc.vector.tensor_tensor(rank[:], rank[:],
                                         cp[:, 0, 0:width].rearrange("p (t e) -> p t e", e=experts), ALU.add))
            link(nc.vector.tensor_tensor(tiles[:], ends[:, at], tiles[:], ALU.subtract))
            link(nc.vector.tensor_scalar(tiles[:], tiles[:], float(P), None, ALU.mult))
            link(nc.vector.tensor_tensor(rank[:], rank[:], tiles[:].unsqueeze(1).to_broadcast(full), ALU.add))
            for k in range(2):
                link(nc.vector.tensor_tensor(prod[:], onehot[:, k], rank[:], ALU.mult))
                link(nc.vector.tensor_reduce(picked[:], prod[:], AX.X, ALU.add))
                link(nc.vector.tensor_copy(t[tag + "row"][:, k, :], picked[:]))
                if tag == "b_":
                    link(nc.vector.tensor_copy(place[:, k * NT:(k + 1) * NT], picked[:]))
            if tag == "b_":
                link(nc.vector.memset(t["b_token"][:], 0))
                link(nc.vector.tensor_copy(place_i[:], place[:]))
                link(nc.vector.tensor_scalar(place_i[:], place_i[:], 7, None, ALU.arith_shift_right))
                link(nc.vector.tensor_copy(place_slot[:], place_i[:]))
                link(nc.vector.scalar_tensor_tensor(place[:], place_slot[:], -float(P), place[:], ALU.mult, ALU.add))
                link(nc.vector.tensor_tensor(in_slot[:], place_slot[:].unsqueeze(2).to_broadcast([P, 2 * NT, slots]),
                                             t["slot_no"][:, 0:slots, 0].unsqueeze(1).to_broadcast([P, 2 * NT, slots]),
                                             ALU.is_equal))
                for k in range(2):
                    mine = in_slot[:, k * NT:(k + 1) * NT, :]
                    link(nc.vector.tensor_tensor(mine, mine, t["token_no"][:].unsqueeze(2).to_broadcast([P, NT, slots]),
                                                 ALU.mult))
                for q in range(4):
                    own = slice(q * QUARTER, (q + 1) * QUARTER)
                    nc.vector.tensor_tensor(in_row[:, own, :], place[:, own].unsqueeze(2).to_broadcast([P, QUARTER, P]),
                                            t["row_no"][:].unsqueeze(1).to_broadcast([P, QUARTER, P]),
                                            ALU.is_equal).then_inc(row_ready, 1)
                dve.wait_ge(table_done, 1)
                link(nc.vector.tensor_copy(t["b_token"][:, 0:slots], tk[:, 0:slots]))
            link(nc.vector.tensor_tensor(over[:], ends[:, at].unsqueeze(1).to_broadcast([P, slots, experts]),
                                         t["slot_no"][:, 0:slots, 0:experts], ALU.is_le))
            link(nc.vector.tensor_reduce(ends_f[:], over[:], AX.X, ALU.add))
            link(nc.vector.tensor_scalar(t[tag + "owner"][:], ends_f[:], float(experts - 1), None, ALU.min))
            if tag == "a_":
                g = t["a_gate"]
                link(nc.vector.tensor_tensor(best[:], g[:, 0, :], g[:, 1, :], ALU.add))
                link(nc.vector.tensor_scalar(order[:], best[:], 1e-9, None, ALU.is_gt))
                link(nc.vector.tensor_scalar(best[:], best[:], 1e-9, None, ALU.add))
                link(nc.vector.reciprocal(best[:], best[:]))
                link(nc.vector.tensor_tensor(best[:], best[:], order[:], ALU.mult))
                link(nc.vector.tensor_scalar(order[:], order[:], -0.5, 0.5, ALU.mult, ALU.add))
                link(nc.vector.tensor_tensor(g[:], g[:], best[:].unsqueeze(1).to_broadcast([P, 2, NT]), ALU.mult))
                link(nc.vector.tensor_tensor(g[:], g[:], order[:].unsqueeze(1).to_broadcast([P, 2, NT]), ALU.add))


def expert_slots(nc, d, t, tag, experts, hidden, slots, rows, outs, W1, b1, W2, b2):
    C = hidden // P
    with ExitStack() as ctx:
        def sb(name, shape, dt=F32):
            return ctx.enter_context(nc.sbuf_tensor(tag + name, shape, dt))

        def ps(name, shape, dt=F32):
            return ctx.enter_context(nc.psum_tensor(tag + name, shape, dt))

        def ring(name):
            return [ctx.enter_context(nc.semaphore(f"{tag}{name}{b}")) for b in range(RING)]

        def sem(name):
            return ctx.enter_context(nc.semaphore(tag + name))

        wa = [sb(f"wa{b}", [P, KC, hidden]) for b in range(RING)]
        wb = [sb(f"wb{b}", [P, C, D]) for b in range(RING)]
        ba = [sb(f"ba{b}", [P, C]) for b in range(RING)]
        bb = [sb(f"bb{b}", [P, D]) for b in range(RING)]
        xr = [sb(f"xr{b}", [P, D]) for b in range(RING)]
        xT = [sb(f"xT{b}", [P, KC, P]) for b in range(RING)]
        hT = [sb(f"hT{b}", [P, C, P]) for b in range(RING)]
        yo = [sb(f"yo{b}", [P, D]) for b in range(RING)]
        HB = 2 if C > 4 else 1
        tp = [ps(f"tp{b}", [P, 512]) for b in range(1)]
        hp = [ps(f"hp{b}", [P, HB, 4, P]) for b in range(2)]
        yp = [ps(f"yp{b}", [P, 512]) for b in range(2)]
        loaded, freed, stored = ring("loaded"), ring("freed"), ring("stored")
        x_turned, xT_ready, h_ready, hT_ready, y_ready = (
            sem("x_turned"), sem("xT_ready"), sem("h_ready"), sem("hT_ready"), sem("y_ready"))
        block = ctx.enter_context(nc.Block())
        rows_in, token_ready, token_seen = ring("rows_in"), sem("token_ready"), sem("token_seen")
        loads = 4 if b1 is not None else 2
        gathered = rows is None
        token = [sb(f"token{b}", [P, 1], U32) for b in range(RING)]
        whole, rest = slots // RING, slots % RING

        def each_slot(eng, slot):
            with eng.Fori(0, whole) as i:
                for j in range(RING):
                    slot(i * RING + j, j, i)
            for j in range(rest):
                slot(whole * RING + j, j, whole)

        @block.sync
        def _(sp):
            def load(s, b, use):
                sp.wait_ge(freed[b], 1 + use)
                e = sp.value_load(t[tag + "owner"][0:1, bass.ds(s, 1)], min_val=0, max_val=experts - 1)
                if not gathered:
                    sp.dma_start(xr[b][:], rows[bass.ds(s, 1), :, :].rearrange("s p c -> (s p) c")).then_inc(rows_in[b], 16)
                sp.dma_start(wa[b][:], W1[bass.ds(e, 1), :, :].rearrange("e (k p) n -> p (e k) n", p=P)).then_inc(loaded[b], 16)
                sp.dma_start(wb[b][:], W2[bass.ds(e, 1), :, :].rearrange("e (p c) n -> p (e c) n", p=P)).then_inc(loaded[b], 16)
                if b1 is not None:
                    sp.dma_start(ba[b][:], b1[bass.ds(e, 1), :].rearrange("e (p c) -> p (e c)", p=P)).then_inc(loaded[b], 16)
                    sp.dma_start(bb[b][:], b2[bass.ds(e, 1), :].to_broadcast([P, D])).then_inc(loaded[b], 16)
            each_slot(sp, load)

        @block.tensor
        def _(pe):
            def turn(s, b, use):
                pe.wait_ge(rows_in[b], use * 16 + 16)
                pe.wait_ge(xT_ready, s)
                for k in range(KC):
                    last = nc.tensor.transpose(tp[0][:, k * P:(k + 1) * P], xr[b][:, k * P:(k + 1) * P], t["ident"][:])
                last.then_inc(x_turned, 1)

            def up(s, b, use, q):
                pe.wait_ge(loaded[b], use * (16 * loads) + 16 * loads)
                pe.wait_ge(xT_ready, s + 1)
                if q is not None:
                    pe.wait_ge(hT_ready, 1 + q)
                for c in range(C):
                    for k in range(KC):
                        last = nc.tensor.matmul(hp[b % 2][:, c // 4, c % 4, :], wa[b][:, k, c:hidden:C], xT[b][:, k, :],
                                                start=(k == 0), stop=(k == KC - 1))
                last.then_inc(h_ready, 1)

            def down(s, b, use):
                pe.wait_ge(hT_ready, 1 + s + 1)
                pe.wait_ge(freed[(b + 2) % RING], 1 + use + (1 if b >= 2 else 0))
                for c in range(C):
                    last = nc.tensor.matmul(yp[b % 2][:, 0:D], hT[b][:, c, :], wb[b][:, c, :],
                                            start=(c == 0), stop=(c == C - 1))
                last.then_inc(y_ready, 1)

            turn(0, 0, 0)
            up(0, 0, 0, None)
            turn(1, 1, 0)
            steps = (slots - 2) // RING
            with pe.Fori(0, steps) as i:
                for j in range(RING):
                    s, b = i * RING + j + 1, (j + 1) % RING
                    up(s, b, i + (j + 1) // RING, i * RING + j)
                    turn(i * RING + j + 2, (j + 2) % RING, i + (j + 2) // RING)
                    down(i * RING + j, j, i)
            for s in range(steps * RING + 1, slots):
                up(s, s % RING, s // RING, s - 1)
                if s + 1 < slots:
                    turn(s + 1, (s + 1) % RING, (s + 1) // RING)
                down(s - 1, (s - 1) % RING, (s - 1) // RING)
            down(slots - 1, (slots - 1) % RING, (slots - 1) // RING)

        @block.scalar
        def _(act):
            def hidden_values(s, b, use):
                act.wait_ge(h_ready, s + 1)
                act.wait_ge(freed[b], 1 + use)
                if b1 is None:
                    last = nc.scalar.activation(hT[b][:], hp[b % 2][:, 0, 0:C, :], ACT.Gelu)
                else:
                    for c in range(C):
                        last = nc.scalar.activation(hT[b][:, c, :], hp[b % 2][:, c // 4, c % 4, :], ACT.Relu,
                                                    bias=ba[b][:, c:c + 1])
                last.then_inc(hT_ready, 1)
            each_slot(act, hidden_values)

        @block.vector
        def _(dve):
            for primed in (*freed, hT_ready):
                dve.sem_inc(primed, 1)
            def turned(s, b, use):
                dve.wait_ge(x_turned, s + 1)
                nc.vector.tensor_copy(xT[b][:].rearrange("p k n -> p (k n)"), tp[0][:, 0:D]).then_inc(xT_ready, 1)

            def result(s, b, use):
                dve.wait_ge(y_ready, s + 1)
                if use is not None:
                    dve.wait_ge(stored[b], 16 * use)
                if b2 is None:
                    ins = nc.vector.tensor_copy(yo[b][:], yp[b % 2][:, 0:D])
                else:
                    ins = nc.vector.tensor_tensor(yo[b][:], yp[b % 2][:, 0:D], bb[b][:], ALU.add)
                ins.then_inc(freed[b], 1)
                if gathered:
                    dve.wait_ge(rows_in[b], 16 * (0 if use is None else use) + 16)
                    list_tokens(s + RING, b)

            def list_tokens(s, b):
                nc.vector.tensor_copy(token[b][:], t["b_token"][:, bass.ds(s, 1)]).then_inc(token_ready, 1)

            if gathered:
                for b in range(RING):
                    list_tokens(b, b)
            turned(0, 0, 0)
            turned(1, 1, 0)
            steps = (slots - 2) // RING
            for j in range(RING):
                turned(j + 2, (j + 2) % RING, None)
                result(j, j, None)
            with dve.Fori(1, steps) as i:
                for j in range(RING):
                    turned(i * RING + j + 2, (j + 2) % RING, None)
                    result(i * RING + j, j, i)
            for s in range(steps * RING, slots):
                if s + 2 < slots:
                    turned(s + 2, (s + 2) % RING, None)
                result(s, s % RING, s // RING)

        @block.gpsimd
        def _(pool):
            def store(s, b, use):
                pool.wait_ge(freed[b], 1 + use + 1)
                pool.dma_start(outs[bass.ds(s, 1), :, :].rearrange("s p c -> (s p) c"), yo[b][:]).then_inc(stored[b], 16)

            def gather(s, b):
                pool.wait_ge(token_ready, s + 1)
                pool.sem_inc(token_seen, 1)
                pool.indirect_dma_start(xr[b][:], None, d["tokens2"],
                                        bass.IndirectOffsetOnAxis(token[b][:, 0:1], 0)).then_inc(rows_in[b], 16)

            if gathered:
                for s in range(RING):
                    gather(s, s)
                ahead = slots - RING
                with pool.Fori(0, ahead // RING) as i:
                    for j in range(RING):
                        store(i * RING + j, j, i)
                        gather(i * RING + j + RING, j)
                for s in range(ahead // RING * RING, slots):
                    store(s, s % RING, s // RING)
                    if s + RING < slots:
                        gather(s + RING, s % RING)
            else:
                each_slot(pool, store)
            for b in range(RING):
                pool.wait_ge(stored[b], 16 * (whole + (b < rest)))


def combine(nc, t, tag, base, outs, finish):
    GB = 4
    with ExitStack() as ctx:
        gb = [ctx.enter_context(nc.sbuf_tensor(f"{tag}gb{b}", [P, 2, D], F32)) for b in range(GB)]
        part = [ctx.enter_context(nc.sbuf_tensor(f"{tag}part{b}", [P, D], F32)) for b in range(GB)]
        res = [ctx.enter_context(nc.sbuf_tensor(f"{tag}res{b}", [P, D], F32)) for b in range(GB)]
        got = [ctx.enter_context(nc.semaphore(f"{tag}got{b}")) for b in range(GB)]
        part_ready = ctx.enter_context(nc.semaphore(tag + "part_ready"))
        res_ready = ctx.enter_context(nc.semaphore(tag + "res_ready"))
        sent = [ctx.enter_context(nc.semaphore(f"{tag}sent{b}")) for b in range(GB)]
        block = ctx.enter_context(nc.Block())
        row, gate = t[tag + "row"], t[tag + "gate"]

        @block.gpsimd
        def _(pool):
            for tt in range(NT):
                if tt >= GB:
                    pool.wait_ge(res_ready, tt - GB + 1)
                for k in range(2):
                    pool.indirect_dma_start(gb[tt % GB][:, k, :], None, outs,
                                            bass.IndirectOffsetOnAxis(row[:, k, tt:tt + 1], 0)).then_inc(got[tt % GB], 16)

        @block.vector
        def _(dve):
            for tt in range(NT):
                dve.wait_ge(got[tt % GB], 32 * (tt // GB + 1))
                nc.vector.scalar_tensor_tensor(part[tt % GB][:], gb[tt % GB][:, 0, :], gate[:, 0, tt:tt + 1],
                                               base[:, tt, :], ALU.mult, ALU.add).then_inc(part_ready, 1)
                dve.wait_ge(part_ready, tt + 1)
                if tt >= GB:
                    dve.wait_ge(sent[tt % GB], 16 * (tt // GB))
                nc.vector.scalar_tensor_tensor(res[tt % GB][:], gb[tt % GB][:, 1, :], gate[:, 1, tt:tt + 1],
                                               part[tt % GB][:], ALU.mult, ALU.add).then_inc(res_ready, 1)

        @block.sync
        def _(sp):
            for tt in range(NT):
                sp.wait_ge(res_ready, tt + 1)
                sp.dma_start(finish[:, tt, :], res[tt % GB][:]).then_inc(sent[tt % GB], 16)
            for b in range(GB):
                sp.wait_ge(sent[b], 16 * (NT // GB))


def mix_and_project(nc, d, t):
    NI = 4
    W = SEQ // NI
    TB = W // P
    COLS = B * W
    BANKS = 6
    SHIFT_ORDER = (3, 1, 0, 2)
    names = ["maa_x", "maa_w", "maa_k", "maa_v", "maa_r", "decay", "ln_w", "ln_b", "faaaa"]
    vec = t["vec"]

    with ExitStack() as ctx:
        def sb(name, shape, dt=F32):
            return ctx.enter_context(nc.sbuf_tensor(name, shape, dt))

        def sem(name):
            return ctx.enter_context(nc.semaphore(name))

        maa1, maa2 = sb("maa1", [P, KC, P]), sb("maa2", [P, D])
        dw1, dw2 = sb("dw1", [P, KC, DEC]), sb("dw2", [DEC, D])
        wr, wk, wv = (sb(n, [P, KC, D]) for n in ("wr", "wk", "wv"))
        vec_rows = sb("vec_rows", [len(names) * KC, P])
        xx = [sb(f"xx{i}", [P, KC, B, W]) for i in range(2)]
        xxx = sb("xxx", [P, KC, B, W])
        mix = [sb(f"mix{i}", [P, COLS]) for i in range(2)]
        shifted = [[sb(f"shifted{i}{f}", [P, KC, B, W]) for f in range(4)] for i in range(2)]
        dlow, rate = sb("dlow", [DEC, COLS]), sb("rate", [P, KC, COLS])
        gb = [sb(f"gb{q}", [P, 2, D]) for q in range(B * TB)]
        res = [sb(f"res{q}", [P, D]) for q in range(B * TB)]
        got = [sem(f"got{q}") for q in range(B * TB)]
        sum_step, q_ready = sem("sum_step"), sem("q_ready")
        pw = [ctx.enter_context(nc.psum_tensor(f"pw{i}", [P, 512], F32)) for i in range(BANKS)]
        pv = ctx.enter_context(nc.psum_tensor("pv", [P, 512], F32))
        ld, vec_in, vec_turned, vec_ready, zeroed = sem("ld"), sem("vec_in"), sem("vec_turned"), sem("vec_ready"), sem("q_zeroed")
        diff_ready, xxx_ready, mix_ready, moved, shifted_ready = (
            sem("diff_ready"), sem("xxx_ready"), sem("mix_ready"), sem("moved"), sem("shifted_ready"))
        rk_ready, low_ready, rate_ready, w_ready, v_ready = (
            sem("rk_ready"), sem("low_ready"), sem("rate_ready"), sem("w_ready"), sem("v_ready"))
        done = [sem(f"wide_done{i}") for i in range(BANKS)]
        block = ctx.enter_context(nc.Block())

        jobs = [("turn", 0, b) for b in range(B)]
        for i in range(NI + 1):
            jobs += [("mix", i)] if i < NI else []
            jobs += [(x, i - 1, c) for x in "rk" for c in range(KC)] if i else []
            jobs += [("shift", i, f, c) for f in range(4) for c in range(KC)] if i < NI else []
            jobs += [("turn", i + 1, b) for b in range(B)] if i + 1 < NI else []
            jobs += [("low", i - 1), ("v", i - 1, 0), ("v", i - 1, 1), ("dec", i - 1, 0), ("dec", i - 1, 1)] if i else []
        number = {job: n for n, job in enumerate(jobs)}

        def taken_by(job):
            kind, i = job[0], job[1]
            return {"turn": lambda: (q_ready, B * i + job[2] + 1),
                    "mix": lambda: (mix_ready, i + 1),
                    "shift": lambda: (moved, 8 * i + 2 * job[2] + job[3] + 1),
                    "r": lambda: (rk_ready, 4 * i + job[2] + 1),
                    "k": lambda: (rk_ready, 4 * i + 2 + job[2] + 1),
                    "low": lambda: (low_ready, i + 1),
                    "v": lambda: (v_ready, 2 * i + job[2] + 1),
                    "dec": lambda: (rate_ready, 2 * i + job[2] + 1)}[kind]()

        def bank(job):
            return pw[number[job] % BANKS]

        def arrived(eng, job):
            n = number[job]
            eng.wait_ge(done[n % BANKS], n // BANKS + 1)

        def col(name, c):
            n = names.index(name) * KC + c
            return vec[:, n:n + 1]

        def tile_of(i, q):
            return q // TB * (NT // B) + i * TB + q % TB

        def token_cols(i, back):
            return t["qT"][:, :, :, 1 - back + i * W:1 - back + (i + 1) * W].rearrange("p k b w -> p (k b) w")

        def chunks_of(ap, i, c):
            return ap[:, i * (W // CH):(i + 1) * (W // CH), c].rearrange("p j b x -> p b j x")

        @block.sync
        def _(sp):
            for name, cols in (("maa_w1", maa1), ("W_r", wr), ("W_k", wk), ("W_v", wv), ("decay_w1", dw1)):
                sp.dma_start(cols[:], d[name].rearrange("(k p) n -> p k n", p=P)).then_inc(ld, 16)
            sp.dma_start(maa2[:], d["maa_w2"].rearrange("f l c -> (f l) c")).then_inc(ld, 16)
            sp.dma_start(dw2[:], d["decay_w2"]).then_inc(ld, 16)

        @block.tensor
        def _(pe):
            for n, job in enumerate(jobs):
                kind, i = job[0], job[1]
                if n == B:
                    pe.wait_ge(vec_in, 16 * len(names))
                    nc.tensor.transpose(pv[:, 0:len(names) * KC], vec_rows[:],
                                        t["ident"][0:len(names) * KC, 0:len(names) * KC]).then_inc(vec_turned, 1)
                    pe.wait_ge(ld, 16 * 7)
                if n >= BANKS:
                    pe.wait_ge(*taken_by(jobs[n - BANKS]))
                o, s = bank(job), shifted[i % 2]
                if kind == "turn":
                    for q in range(TB):
                        place = job[2] * TB + q
                        pe.wait_ge(sum_step, 2 * (B * TB * i + place) + 2)
                        for k in range(KC):
                            last = nc.tensor.transpose(o[:, k * W + q * P:k * W + (q + 1) * P],
                                                       res[place][:, k * P:(k + 1) * P], t["ident"][:])
                elif kind == "mix":
                    pe.wait_ge(xxx_ready, i + 1)
                    for c in range(KC):
                        last = nc.tensor.matmul(o[:], maa1[:, c, :], xxx[:, c].rearrange("p b w -> p (b w)"),
                                                start=(c == 0), stop=(c == KC - 1))
                elif kind == "shift":
                    f, c = job[2:]
                    pe.wait_ge(mix_ready, i + 1)
                    last = nc.tensor.matmul(o[:], maa2[MIX * f:MIX * f + MIX, c * P:(c + 1) * P],
                                            mix[i % 2][MIX * f:MIX * f + MIX, :], start=True, stop=True,
                                            tile_position=(MIX * f, 0))
                elif kind in "rk":
                    c = job[2]
                    wt, f = (wr, 3) if kind == "r" else (wk, 1)
                    pe.wait_ge(shifted_ready, 4 * i + SHIFT_ORDER.index(f) + 1)
                    for kk in range(KC):
                        last = nc.tensor.matmul(o[:], wt[:, kk, c * P:(c + 1) * P], s[f][:, kk].rearrange("p b w -> p (b w)"),
                                                start=(kk == 0), stop=(kk == KC - 1))
                elif kind == "low":
                    pe.wait_ge(shifted_ready, 4 * i + SHIFT_ORDER.index(0) + 1)
                    for kk in range(KC):
                        last = nc.tensor.matmul(o[0:DEC, :], dw1[:, kk, :], s[0][:, kk].rearrange("p b w -> p (b w)"),
                                                start=(kk == 0), stop=(kk == KC - 1))
                elif kind == "v":
                    pe.wait_ge(shifted_ready, 4 * i + SHIFT_ORDER.index(2) + 1)
                    for q in range(2):
                        for kk in range(KC):
                            last = nc.tensor.matmul(o[:, q * D:(q + 1) * D], s[2][:, kk, job[2], q * CH:(q + 1) * CH],
                                                    wv[:, kk, :], start=(kk == 0), stop=(kk == KC - 1))
                else:
                    c = job[2]
                    pe.wait_ge(low_ready, i + 1)
                    last = nc.tensor.matmul(o[:], dw2[:, c * P:(c + 1) * P], dlow[:], start=True, stop=True)
                last.then_inc(done[n % BANKS], 1)

        @block.scalar
        def _(act):

            def token_columns(i):
                for b in range(B):
                    arrived(act, ("turn", i, b))
                    nc.scalar.activation(t["qT"][:, :, b, 1 + i * W:1 + (i + 1) * W],
                                         bank(("turn", i, b))[:].rearrange("p (k w) -> p k w", w=W), ACT.Copy,
                                         scale=1.0 / 3.0).then_inc(q_ready, 1)

            token_columns(0)
            act.wait_ge(vec_turned, 1)
            nc.scalar.activation(vec[:], pv[:, 0:len(names) * KC], ACT.Copy).then_inc(vec_ready, 1)
            act.wait_ge(vec_ready, 1)
            for i in range(NI + 1):
                if i < NI:
                    arrived(act, ("mix", i))
                    nc.scalar.activation(mix[i % 2][:], bank(("mix", i))[:], ACT.Tanh).then_inc(mix_ready, 1)
                if i == 0:
                    token_columns(1)
                    continue
                g = i - 1
                for x, store in (("r", t["r_all"]), ("k", t["k_all"])):
                    for c in range(KC):
                        arrived(act, (x, g, c))
                        nc.scalar.activation(chunks_of(store, g, c),
                                             bank((x, g, c))[:].rearrange("p (b j x) -> p b j x", b=B, x=CH),
                                             ACT.Copy).then_inc(rk_ready, 1)
                if i + 1 < NI:
                    token_columns(i + 1)
                arrived(act, ("low", g))
                nc.scalar.activation(dlow[:], bank(("low", g))[0:DEC, :], ACT.Tanh).then_inc(low_ready, 1)
                if g:
                    act.wait_ge(w_ready, 2 * g)
                for c in range(KC):
                    arrived(act, ("dec", g, c))
                    nc.scalar.activation(rate[:, c, :], bank(("dec", g, c))[:], ACT.Exp,
                                         bias=col("decay", c)).then_inc(rate_ready, 1)
                for c in range(KC):
                    act.wait_ge(rate_ready, 2 * g + c + 1)
                    nc.scalar.activation(chunks_of(t["w_all"], g, c),
                                         rate[:, c, :].rearrange("p (b j x) -> p b j x", b=B, x=CH),
                                         ACT.Exp, scale=-1.0).then_inc(w_ready, 1)

        @block.gpsimd
        def _(pool):
            def gather(i):
                for q in range(B * TB):
                    tile = tile_of(i, q)
                    if i:
                        pool.wait_ge(sum_step, 2 * (B * TB * (i - 1) + q) + 2)
                    for k in range(2):
                        pool.indirect_dma_start(gb[q][:, k, :], None, d["outs1"],
                                                bass.IndirectOffsetOnAxis(t["a_row"][:, k, tile:tile + 1], 0)).then_inc(got[q], 16)

            gather(0)
            for n, name in enumerate(names):
                src = d[name].rearrange("h i -> (h i)") if name == "faaaa" else d[name]
                pool.dma_start(vec_rows[n * KC:(n + 1) * KC, :], src.rearrange("(k p) -> k p", p=P)).then_inc(vec_in, 16)
            gather(1)
            for i in range(NI):
                for f in SHIFT_ORDER:
                    pool.wait_ge(moved, 8 * i + 2 * f + 2)
                    if f == 3:
                        pool.wait_ge(moved, 8 * i + 8)
                    s = shifted[i % 2][f][:].rearrange("p k b w -> p (k b) w")
                    nc.gpsimd.tensor_tensor(s, s, token_cols(i, 0), ALU.add).then_inc(shifted_ready, 1)
                if i + 2 < NI:
                    gather(i + 2)

        @block.vector
        def _(dve):
            nc.vector.memset(t["qT"][:, :, :, 0:1], 0.0).then_inc(zeroed, 1)
            dve.wait_ge(zeroed, 1)

            def sums(i):
                for q in range(B * TB):
                    tile, n = tile_of(i, q), B * TB * i + q
                    dve.wait_ge(got[q], 32 * (i + 1))
                    if i:
                        arrived(dve, ("turn", i - 1, q // TB))
                    nc.vector.scalar_tensor_tensor(res[q][:], gb[q][:, 0, :], t["a_gate"][:, 0, tile:tile + 1],
                                                   t["acc"][:, tile, :], ALU.mult, ALU.add).then_inc(sum_step, 1)
                    dve.wait_ge(sum_step, 2 * n + 1)
                    nc.vector.scalar_tensor_tensor(res[q][:], gb[q][:, 1, :], t["a_gate"][:, 1, tile:tile + 1],
                                                   res[q][:], ALU.mult, ALU.add).then_inc(sum_step, 1)

            def differences(i):
                dve.wait_ge(q_ready, B * (i + 1))
                nc.vector.tensor_tensor(xx[i % 2][:].rearrange("p k b w -> p (k b) w"), token_cols(i, 1), token_cols(i, 0),
                                        ALU.subtract).then_inc(diff_ready, 1)
                dve.wait_ge(diff_ready, i + 1)
                if i:
                    arrived(dve, ("mix", i - 1))
                for c in range(KC):
                    last = nc.vector.scalar_tensor_tensor(xxx[:, c], xx[i % 2][:, c], col("maa_x", c),
                                                          t["qT"][:, c, :, 1 + i * W:1 + (i + 1) * W], ALU.mult, ALU.add)
                last.then_inc(xxx_ready, 1)

            def values(g):
                for b in range(B):
                    arrived(dve, ("v", g, b))
                    nc.vector.tensor_copy(t["v_all"][:, g * (W // CH):(g + 1) * (W // CH), b, :],
                                          bank(("v", g, b))[:].rearrange("p (j c) -> p j c", c=D)).then_inc(v_ready, 1)

            sums(0)
            dve.wait_ge(vec_ready, 1)
            differences(0)
            for i in range(NI):
                if i + 1 < NI:
                    sums(i + 1)
                for f in range(4):
                    for c in range(KC):
                        arrived(dve, ("shift", i, f, c))
                        nc.vector.scalar_tensor_tensor(shifted[i % 2][f][:, c].rearrange("p b w -> p (b w)"),
                                                       bank(("shift", i, f, c))[:], col(names[1 + f], c),
                                                       xx[i % 2][:, c].rearrange("p b w -> p (b w)"),
                                                       ALU.add, ALU.mult).then_inc(moved, 1)
                if i + 1 < NI:
                    differences(i + 1)
                if i:
                    values(i - 1)
            values(NI - 1)


def recurrence(nc, d, t):
    NJ = SEQ // CH
    COLS = KC * B * CH
    with ExitStack() as ctx:
        def sb(name, shape, dt=F32):
            return ctx.enter_context(nc.sbuf_tensor(name, shape, dt))

        def two(name, shape):
            return [sb(f"{name}_{i}", shape) for i in range(2)]

        def ps(name, shape, dt=F32):
            return ctx.enter_context(nc.psum_tensor(name, shape, dt))

        def sem(name):
            return ctx.enter_context(nc.semaphore(name))

        wo = sb("wo", [P, KC, D])
        bonus_sel = sb("bonus_sel", [P, KC, HEADS])
        pick = t["pick"]
        r, k, v = two("r", [P, COLS]), two("k", [P, COLS]), two("v", [P, B, D])
        rk, rfull, kfull = two("rk", [P, COLS]), two("rfull", [P, COLS]), two("kfull", [P, COLS])
        rp = [two(f"rp{l}", [P, KC * B, 2, CH // 2]) for l in range(LEVELS)]
        kq = [two(f"kq{l}", [P, COLS]) if l else k for l in range(LEVELS)]
        pre, suf = sb("pre", [P, COLS]), sb("suf", [P, COLS])
        tot = [None] + [two(f"tot{l}", [P, COLS >> l]) for l in range(1, LEVELS + 1)]
        A = sb("A", [P, HEADS, CH])
        kt = sb("kt", [P, KC, P])
        state = sb("state", [P, B, KC, 2 * HD])
        y0, y1, yn = two("y0", [P, D]), two("y1", [P, D]), two("yn", [P, D])
        stats, aggr = sb("stats", [P, HEADS, 6]), two("aggr", [P, HEADS, 2])
        dev, inv, off = two("dev", [P, HEADS]), two("inv", [P, HEADS]), two("off", [P, HEADS])
        ynT = sb("ynT", [P, KC, P])
        eps = sb("eps", [P, 1])

        PAIRS = (LEVELS + 1) // 2
        pa = ps("pa", [P, PAIRS, 2, HEADS * CH // 2])
        py = ps("py", [P, 512])
        pk, pu, pz = ps("pk", [P, 512]), ps("pu", [P, 512]), ps("pz", [P, 2, D])

        wo_in, zeroed, consts, dve_step, pool_step = sem("wo_in"), sem("wkv_zeroed"), sem("wkv_consts"), sem("dve_step"), sem("pool_step")
        local_ready, tot_ready, pre_ready, left_ready, right_ready = (
            sem("local_ready"), sem("tot_ready"), sem("pre_ready"), sem("left_ready"), sem("right_ready"))
        weights_done, weights_seen, picked, k_turned, kt_ready, state_inc, state_ready = (
            sem("weights_done"), sem("weights_seen"), sem("picked"), sem("k_turned"), sem("kt_ready"), sem("state_inc"),
            sem("state_ready"))
        y_done, y_taken, var_ready, dev_ready, off_ready, yn_ready, yn_turned, ynT_ready, o_done, o_taken = (
            sem("y_done"), sem("y_taken"), sem("var_ready"), sem("dev_ready"), sem("off_ready"), sem("yn_ready"),
            sem("yn_turned"), sem("ynT_ready"), sem("o_done"), sem("o_taken"))
        tot_seen, state_zeroed, keys_zeroed = sem("tot_seen"), sem("state_zeroed"), sem("keys_zeroed")
        block = ctx.enter_context(nc.Block())
        vec, LNW, LNB, BON = t["vec"], 6, 7, 8

        def half(ap, m, side):
            return ap.rearrange("p (n s m) -> p n s m", s=2, m=m)[:, :, side, :]

        def even_odd(ap, side):
            return ap.rearrange("p (n s) -> p n s", s=2)[:, :, side]

        def spread(ap, m):
            return ap.unsqueeze(2).to_broadcast([P, COLS // (2 * m), m])

        def chunk(ap, j):
            return ap[:, bass.ds(j, 1)]

        def each_step(eng, step):
            step(0, 0, True, False)
            with eng.Fori(0, (NJ - 2) // 2) as i:
                step(2 * i + 1, 1, False, False)
                step(2 * i + 2, 0, False, False)
            step(NJ - 1, (NJ - 1) % 2, False, True)

        @block.sync
        def _(sp):
            sp.dma_start(wo[:], d["W_o"].rearrange("(k p) n -> p k n", p=P)).then_inc(wo_in, 16)

        @block.tensor
        def _(pe):
            def weigh(j, par, b):
                n = 2 * j + b
                if b == 0:
                    pe.wait_ge(left_ready, j + 1)
                    pe.wait_ge(pre_ready, j + 1)
                for l in range(LEVELS):
                    if l % 2 == 0 and not (isinstance(n, int) and n == 0):
                        pe.wait_ge(picked, (n - 1) * PAIRS + l // 2 + 1)
                    for c in range(KC):
                        first = (c * B + b) * CH
                        last = nc.tensor.matmul(pa[:, l // 2, l % 2, c * CH:(c + 1) * CH], kq[l][par][:, first:first + CH],
                                                rp[l][par][:, c * B + b].rearrange("p h n -> p (h n)"),
                                                start=True, stop=True)
                    if l % 2 or l == LEVELS - 1:
                        last.then_inc(weights_done, 1)

            def turn_keys(j, par, b):
                for c in range(KC):
                    first = (c * B + b) * CH
                    last = nc.tensor.transpose(pk[:, c * P:(c + 1) * P], kfull[par][:, first:first + CH], t["ident"][:])
                last.then_inc(k_turned, 1)

            def outputs(j, par, b):
                n = 2 * j + b
                if b == 0:
                    pe.wait_ge(right_ready, j + 1)
                pe.wait_ge(picked, n * PAIRS + PAIRS)
                if not (isinstance(n, int) and n == 0):
                    pe.wait_ge(y_taken, n)
                if not (isinstance(j, int) and j == 0):
                    pe.wait_ge(state_ready, 2 * j - 1 + b)
                for c in range(KC):
                    first = (c * B + b) * CH
                    nc.tensor.matmul(py[:, c * P:(c + 1) * P], rfull[par][:, first:first + CH], state[:, b, c, :],
                                     start=True, stop=True)
                    for h in range(2):
                        hc = slice((2 * c + h) * HD, (2 * c + h + 1) * HD)
                        nc.tensor.matmul(py[:, hc], A[:, 2 * c + h, :], v[par][:, b, hc],
                                         start=False, stop=True, skip_group_check=True)
                for c in range(KC):
                    first = (c * B + b) * CH
                    last = nc.tensor.matmul(py[:, D:D + HEADS], rk[par][:, first:first + CH], bonus_sel[:, c, :],
                                            start=(c == 0), stop=(c == KC - 1))
                last.then_inc(y_done, 1)
                pe.wait_ge(kt_ready, n + 1)
                if not (isinstance(n, int) and n == 0):
                    pe.wait_ge(state_ready, n)
                for c in range(KC):
                    last = nc.tensor.matmul(pu[:, c * P:(c + 1) * P], kt[:, c, :], v[par][:, b, c * P:(c + 1) * P],
                                            start=True, stop=True)
                last.then_inc(state_inc, 1)

            def project(n, par):
                pe.wait_ge(yn_ready, n + 1)
                if not (isinstance(n, int) and n == 0):
                    pe.wait_ge(o_taken, n)
                for kk in range(KC):
                    last = nc.tensor.transpose(pz[:, 0, kk * P:(kk + 1) * P], yn[par][:, kk * P:(kk + 1) * P], t["ident"][:])
                last.then_inc(yn_turned, 1)
                pe.wait_ge(ynT_ready, n + 1)
                for kk in range(KC):
                    last = nc.tensor.matmul(pz[:, 1, :], ynT[:, kk, :], wo[:, kk, :], start=(kk == 0), stop=(kk == KC - 1))
                last.then_inc(o_done, 1)

            pe.wait_ge(wo_in, 16)
            pe.wait_ge(consts, 1)

            def step(j, par, first, last):
                for b in range(B):
                    weigh(j, par, b)
                    turn_keys(j, par, b)
                    if not (first and b == 0):
                        project(2 * j + b - 1, (b + 1) % 2)
                    outputs(j, par, b)
                if last:
                    project(2 * j + 1, 1)

            each_step(pe, step)

        @block.scalar
        def _(act):
            def local(j, par):
                jj = chunk(t["r_all"], j), chunk(t["k_all"], j), chunk(t["v_all"], j)
                for h in range(2):
                    hs = slice(HD * h, HD * h + HD)
                    nc.scalar.activation(rp[0][par][hs, :, h, :],
                                         jj[0][hs].rearrange("p j k b (n s) -> p (j k b) n s", s=2)[:, :, :, 1], ACT.Copy)
                nc.scalar.activation(r[par][:], jj[0].rearrange("p j k b x -> p (j k b x)"), ACT.Copy)
                nc.scalar.activation(k[par][:], jj[1].rearrange("p j k b x -> p (j k b x)"), ACT.Copy)
                nc.scalar.activation(v[par][:].rearrange("p b c -> p (b c)"), jj[2].rearrange("p j b c -> p (j b c)"),
                                     ACT.Copy).then_inc(local_ready, 1)

            def columns(n):
                act.wait_ge(yn_turned, n + 1)
                for kk in range(KC):
                    last = nc.scalar.activation(ynT[:, kk, :], pz[:, 0, kk * P:(kk + 1) * P], ACT.Identity,
                                                scale=vec[:, LNW * KC + kk:LNW * KC + kk + 1],
                                                bias=vec[:, LNB * KC + kk:LNB * KC + kk + 1])
                last.then_inc(ynT_ready, 1)

            def step(j, par, first, last):
                for b in range(B):
                    n = 2 * j + b
                    act.wait_ge(k_turned, n + 1)
                    nc.scalar.activation(kt[:].rearrange("p k n -> p (k n)"), pk[:, 0:D], ACT.Copy).then_inc(kt_ready, 1)
                    if not (first and b == 0):
                        columns(n - 1)
                    if b == 0 and not last:
                        if not first:
                            act.wait_ge(y_taken, n)
                        local(j + 1, 1 - par)
                    act.wait_ge(var_ready, n + 1)
                    nc.scalar.activation(dev[b][:], aggr[b][:, :, 1], ACT.Sqrt, bias=eps[:, 0:1]).then_inc(dev_ready, 1)
                    act.wait_ge(off_ready, n + 1)
                    for h in range(HEADS):
                        hc = slice(h * HD, (h + 1) * HD)
                        ins = nc.scalar.activation(yn[b][:, hc], y1[b][:, hc], ACT.Identity,
                                                   scale=inv[b][:, h:h + 1], bias=off[b][:, h:h + 1])
                    ins.then_inc(yn_ready, 1)
                if last:
                    columns(2 * j + 1)

            act.wait_ge(state_zeroed, 1)
            for l in range(LEVELS):
                nc.scalar.activation(rp[l][1][:].rearrange("p q h n -> p (q h n)"),
                                     state[:].rearrange("p b k n -> p (b k n)"), ACT.Copy)
            act.wait_ge(zeroed, 1)
            local(0, 0)
            each_step(act, step)

        @block.gpsimd
        def _(pool):
            steps = [0]
            nc.gpsimd.memset(bonus_sel[:], 0.0).then_inc(pool_step, 1)
            steps[0] += 1
            pool.wait_ge(pool_step, steps[0])
            for c in range(KC):
                for h in range(2):
                    hs = slice(HD * h, HD * h + HD)
                    nc.gpsimd.tensor_copy(bonus_sel[hs, c, 2 * c + h:2 * c + h + 1],
                                          vec[hs, BON * KC + c:BON * KC + c + 1]).then_inc(pool_step, 1)
                    steps[0] += 1
                    pool.wait_ge(pool_step, steps[0])
            pool.sem_inc(consts, 1)
            pool.wait_ge(keys_zeroed, 1)

            def left(j, par):
                pool.sem_clear(pool_step)
                done = [0]

                def link(ins):
                    done[0] += 1
                    ins.then_inc(pool_step, 1)
                    pool.wait_ge(pool_step, done[0])

                w = chunk(t["w_all"], j).rearrange("p j k b x -> p (j k b x)")
                pool.wait_ge(local_ready, j + 1)
                nc.gpsimd.tensor_tensor(rk[par][:], r[par][:], k[par][:], ALU.mult)
                link(nc.gpsimd.tensor_copy(half(suf[:], 1, 0), half(w, 1, 1)))
                pool.wait_ge(tot_ready, j + 1)
                for l in range(1, LEVELS):
                    m = 1 << l
                    link(nc.gpsimd.tensor_tensor(half(kq[l][par][:], m, 0), half(k[par][:], m, 0), half(suf[:], m, 0), ALU.mult))
                    link(nc.gpsimd.tensor_tensor(half(suf[:], m, 0), half(suf[:], m, 0),
                                                 spread(even_odd(tot[l][par][:], 1), m), ALU.mult))
                link(nc.gpsimd.tensor_tensor(kfull[par][:], k[par][:], suf[:], ALU.mult))
                pool.sem_inc(left_ready, 1)
                pool.wait_ge(pre_ready, j + 1)
                link(nc.gpsimd.tensor_tensor(rfull[par][:], r[par][:], pre[:], ALU.mult))
                link(nc.gpsimd.memset(half(suf[:], 1, 1), 1.0))
                pool.sem_inc(right_ready, 1)

            nc.gpsimd.memset(half(suf[:], 1, 1), 1.0)
            left(0, 0)

            def step(j, par, first, last):
                if not last:
                    if not first:
                        pool.wait_ge(y_done, 2 * j)
                    pool.sem_inc(tot_seen, 1)
                    left(j + 1, 1 - par)

            each_step(pool, step)

        @block.vector
        def _(dve):
            done = [0]

            def link(ins):
                done[0] += 1
                ins.then_inc(dve_step, 1)
                dve.wait_ge(dve_step, done[0])

            def count(ins):
                done[0] += 1
                ins.then_inc(dve_step, 1)
                return done[0]

            def need(n):
                dve.wait_ge(dve_step, n)

            def whole(j, par, l):
                src = chunk(t["w_all"], j).rearrange("p j k b x -> p (j k b x)") if l == 0 else tot[l][par][:]
                return count(nc.vector.tensor_tensor(tot[l + 1][par][:], even_odd(src, 0), even_odd(src, 1), ALU.mult))

            def start_right(j):
                w = chunk(t["w_all"], j).rearrange("p j k b x -> p (j k b x)")
                if not (isinstance(j, int) and j == 0):
                    dve.wait_ge(right_ready, j)
                nc.vector.memset(half(pre[:], 1, 0), 1.0)
                return count(nc.vector.tensor_copy(half(pre[:], 1, 1), half(w, 1, 0)))

            def receive(par, l, h):
                m, hs = 1 << l, slice(HD * h, HD * h + HD)
                return count(nc.vector.tensor_tensor(rp[l][par][hs, :, h, :].rearrange("p q (n m) -> p q n m", m=m),
                                                     half(r[par][hs], m, 1).rearrange("p (q n) m -> p q n m", q=KC * B),
                                                     half(pre[hs], m, 1).rearrange("p (q n) m -> p q n m", q=KC * B),
                                                     ALU.mult))

            def extend(par, l):
                m = 1 << l
                return count(nc.vector.tensor_tensor(half(pre[:], m, 1), half(pre[:], m, 1),
                                                     spread(even_odd(tot[l][par][:], 0), m), ALU.mult))

            def level(par, l):
                receive(par, l, 0)
                need(receive(par, l, 1))
                need(extend(par, l))

            def choose(n, l):
                if l == 0 and not (isinstance(n, int) and n == 0):
                    dve.wait_ge(y_done, n)
                if l % 2 == 0:
                    dve.wait_ge(weights_done, n * PAIRS + l // 2 + 1)
                    dve.sem_inc(weights_seen, 1)
                m = 1 << l
                return count(nc.vector.copy_predicated(
                    A[:].rearrange("p h (n s m) -> p h n s m", s=2, m=m)[:, :, :, 1, :],
                    pick[:, l, :].bitcast(I32).rearrange("p (n m) -> p n m", m=m).unsqueeze(1).to_broadcast(
                        [P, HEADS, CH // 2 // m, m]),
                    pa[:, l // 2, l % 2].rearrange("p (h n m) -> p h n m", h=HEADS, m=m)))

            def chosen(l, at):
                need(at)
                if l % 2 or l == LEVELS - 1:
                    dve.sem_inc(picked, 1)

            def advance(par, b, c):
                for h in range(2):
                    hs = slice(HD * h, HD * h + HD)
                    own = state[hs, b, c, HD * h:HD * h + HD]
                    last = nc.vector.scalar_tensor_tensor(own, own, tot[LEVELS][par][hs, c * B + b:c * B + b + 1],
                                                          pu[hs, c * P + HD * h:c * P + HD * h + HD], ALU.mult, ALU.add)
                return last

            def moments(n, par, b):
                dve.wait_ge(y_done, n + 1)
                heads = [P, HEADS, HD]
                own = count(nc.vector.tensor_tensor(y0[b][:].rearrange("p (h j) -> p h j", j=HD),
                                                    v[par][:, b, :].rearrange("p (h j) -> p h j", j=HD),
                                                    py[:, D:D + HEADS].unsqueeze(2).to_broadcast(heads), ALU.mult))
                dve.wait_ge(state_inc, n + 1)
                advance(par, b, 0)
                need(own)
                y = count(nc.vector.tensor_tensor(y1[b][:], y0[b][:], py[:, 0:D], ALU.add))
                advance(par, b, 1).then_inc(state_ready, 1)
                need(y)
                dve.sem_inc(y_taken, 1)
                for h in range(HEADS):
                    last = nc.vector.bn_stats(stats[:, h, :], y1[b][:, h * HD:(h + 1) * HD])
                need(count(last))
                for h in range(HEADS):
                    last = nc.vector.bn_aggr(aggr[b][:, h, :], stats[:, h, :])
                last.then_inc(var_ready, 1)

            def offsets(n, b):
                dve.wait_ge(dev_ready, n + 1)
                link(nc.vector.reciprocal(inv[b][:], dev[b][:]))
                nc.vector.scalar_tensor_tensor(off[b][:], aggr[b][:, :, 0], -1.0, inv[b][:], ALU.mult,
                                               ALU.mult).then_inc(off_ready, 1)

            def residual(n, j, b):
                dve.wait_ge(o_done, n + 1)
                at = t["x_tok"][:, bass.ds(b * (NT // B) + j, 1), :].rearrange("p t c -> p (t c)")
                nc.vector.tensor_tensor(at, at, pz[:, 1, :], ALU.add).then_inc(o_taken, 1)

            nc.vector.memset(state[:], 0.0).then_inc(state_zeroed, 1)
            for l in range(1, LEVELS):
                for par in range(2):
                    last = nc.vector.memset(half(kq[l][par][:], 1 << l, 1), 0.0)
            last.then_inc(keys_zeroed, 1)
            for l in range(LEVELS):
                need(whole(0, 0, l))
            dve.sem_inc(tot_ready, 1)
            for l in range(LEVELS):
                nc.vector.memset(rp[l][0][:], 0.0)
            nc.vector.memset(eps[:], LN_EPS)
            nc.vector.memset(A[:], 0.0).then_inc(zeroed, 1)
            dve.wait_ge(zeroed, 1)
            dve.wait_ge(consts, 1)
            need(start_right(0))
            dve.wait_ge(local_ready, 1)
            for l in range(1, LEVELS):
                level(0, l)
            dve.sem_inc(pre_ready, 1)

            def step(j, par, first, last):
                dve.sem_clear(dve_step)
                done[0] = 0
                n, after = 2 * j, 1 - par
                for l in range(LEVELS):
                    at = choose(n, l)
                    if not last:
                        block_done = whole(j + 1, after, l)
                    chosen(l, at)
                    if not last:
                        need(block_done)
                if not last:
                    dve.sem_inc(tot_ready, 1)
                    need(start_right(j + 1))
                    dve.wait_ge(local_ready, j + 2)
                    level(after, 1)
                moments(n, par, 0)
                if not first:
                    residual(n - 1, j - 1, 1)
                offsets(n, 0)
                if not last:
                    level(after, 2)
                n = 2 * j + 1
                for l in range(LEVELS):
                    at = choose(n, l)
                    if not last and l < 6:
                        q = 3 + l // 3
                        if l % 3 == 2:
                            part = extend(after, q)
                        else:
                            part = receive(after, q, l % 3)
                    chosen(l, at)
                    if not last and l < 6 and l % 3:
                        need(part)
                if not last:
                    for l in (5, 6):
                        level(after, l)
                    dve.sem_inc(pre_ready, 1)
                moments(n, par, 1)
                residual(n - 1, j, 0)
                offsets(n, 1)
                if last:
                    residual(n, j, 1)

            each_step(dve, step)


def condition(nc, d, t):
    with ExitStack() as ctx:
        def sb(name, shape, dt=F32):
            return ctx.enter_context(nc.sbuf_tensor("c_" + name, shape, dt))

        def ps(name, shape, dt=F32):
            return ctx.enter_context(nc.psum_tensor("c_" + name, shape, dt))

        def sem(name):
            return ctx.enter_context(nc.semaphore("c_" + name))

        wp, wm = sb("wp", [P, KC, D]), sb("wm", [P, 2 * KC, D])
        wr = sb("wr", [P, KC, E2])
        cond_col, bp_col = sb("cond_col", [P, KC, B]), sb("bp_col", [P, KC])
        u_col, u_rep, u_row = sb("u_col", [P, KC, B]), sb("u_rep", [P, KC, B, P]), sb("u_row", [P, B, D])
        br = sb("br", [P, E2])
        xT, hT = ([sb(f"{n}{i}", [P, KC, GT * P]) for i in range(2)] for n in ("xT", "hT"))
        logits, top, total = sb("logits", [P, NT, E2]), sb("top", [P, NT]), sb("total", [P, NT])
        xp, hp, tp = ps("xp", [P, KC, GT * P]), ps("hp", [P, GT, D]), ps("tp", [P, KC, GT * P])
        rp, up = ps("rp", [P, 512]), ps("up", [P, 512])
        rp_t = rp[:, 0:NT * E2].rearrange("p (t e) -> p t e", e=E2)
        proj_in, weights_in, cols_in, u_sum, u_ready, rep_ready, urow_done, urow_ready = (
            sem("proj_in"), sem("weights_in"), sem("cols_in"), sem("u_sum"), sem("u_ready"), sem("rep_ready"),
            sem("urow_done"), sem("urow_ready"))
        h_stored = sem("h_stored")
        x_turned, xT_ready, h_done, h_ready, h_turned, hT_ready, r_done, step_done, exp_done = (
            sem("x_turned"), sem("xT_ready"), sem("h_done"), sem("h_ready"), sem("h_turned"), sem("hT_ready"),
            sem("r_done"), sem("step_done"), sem("exp_done"))
        block = ctx.enter_context(nc.Block())

        @block.sync
        def _(sp):
            sp.dma_start(wp[:], d["W_proj"].rearrange("(k p) n -> p k n", p=P)).then_inc(proj_in, 16)
            sp.dma_start(wm[:], d["weight_matrix"].rearrange("(k p) n -> p k n", p=P)).then_inc(weights_in, 16)
            sp.dma_start(wr[:], d["Wr"].rearrange("(k p) n -> p k n", p=P)).then_inc(weights_in, 16)
            sp.dma_start(br[:], d["br"].unsqueeze(0).to_broadcast([P, E2])).then_inc(weights_in, 16)
            for g in range(NG):
                sp.wait_ge(h_ready, g + 1)
                sp.dma_start(d["tokens2"].rearrange("(t p) c -> p t c", p=P)[:, g * GT:(g + 1) * GT, :],
                             t["acc"][:, g * GT:(g + 1) * GT, :]).then_inc(h_stored, 16)
            sp.wait_ge(h_stored, 16 * NG)

        @block.gpsimd
        def _(pool):
            with nc.allow_non_contiguous_dma(reason="768 values, once"):
                for b in range(B):
                    pool.dma_start(cond_col[:, :, b], d["cond"][b].rearrange("(k p) -> p k", p=P)).then_inc(cols_in, 16)
                pool.dma_start(bp_col[:], d["b_proj"].rearrange("(k p) -> p k", p=P)).then_inc(cols_in, 16)

        @block.tensor
        def _(pe):
            def turn(out, src, g):
                for tt in range(GT):
                    for k in range(KC):
                        last = nc.tensor.transpose(out[:, k, tt * P:(tt + 1) * P],
                                                   src[:, g * GT + tt, k * P:(k + 1) * P], t["ident"][:])
                return last

            def turn_x(g):
                if g:
                    pe.wait_ge(xT_ready, g)
                turn(xp, t["x_tok"], g).then_inc(x_turned, 1)

            turn_x(0)
            pe.wait_ge(proj_in, 16)
            pe.wait_ge(cols_in, 48)
            for c in range(KC):
                for k in range(KC):
                    last = nc.tensor.matmul(up[:, c * B:(c + 1) * B], wp[:, k, c * P:(c + 1) * P], cond_col[:, k, :],
                                            start=(k == 0), stop=(k == KC - 1))
            last.then_inc(u_sum, 1)
            pe.wait_ge(weights_in, 48)
            for g in range(NG + 1):
                if g:
                    pe.wait_ge(h_ready, g)
                    if g >= 2:
                        pe.wait_ge(hT_ready, g - 1)
                    turn(tp, t["acc"], g - 1).then_inc(h_turned, 1)
                if g < NG:
                    pe.wait_ge(xT_ready, g + 1)
                    for tt in range(GT):
                        for k in range(KC):
                            last = nc.tensor.matmul(hp[:, tt, :], xT[g % 2][:, k, tt * P:(tt + 1) * P], wm[:, KC + k, :],
                                                    start=(k == 0), stop=(k == KC - 1))
                    last.then_inc(h_done, 1)
                if g == 0:
                    pe.wait_ge(rep_ready, 1)
                    for b in range(B):
                        for k in range(KC):
                            last = nc.tensor.matmul(up[:, b * D:(b + 1) * D], u_rep[:, k, b, :], wm[:, k, :],
                                                    start=(k == 0), stop=(k == KC - 1))
                    last.then_inc(urow_done, 1)
                if g + 1 < NG:
                    turn_x(g + 1)
                if g:
                    pe.wait_ge(hT_ready, g)
                    for tt in range(GT):
                        for k in range(KC):
                            last = nc.tensor.matmul(rp_t[:, (g - 1) * GT + tt, :], hT[(g - 1) % 2][:, k, tt * P:(tt + 1) * P],
                                                    wr[:, k, :], start=(k == 0), stop=(k == KC - 1))
                    last.then_inc(r_done, 1)

        @block.scalar
        def _(act):
            def columns(out, src, ready, g):
                for k in range(KC):
                    last = nc.scalar.activation(out[g % 2][:, k, :], src[:, k, :], ACT.Copy)
                last.then_inc(ready, 1)

            act.wait_ge(x_turned, 1)
            columns(xT, xp, xT_ready, 0)
            act.wait_ge(u_sum, 1)
            act.wait_ge(cols_in, 48)
            for c in range(KC):
                last = nc.scalar.activation(u_col[:, c, :], up[:, c * B:(c + 1) * B], ACT.Gelu, bias=bp_col[:, c:c + 1])
            last.then_inc(u_ready, 1)
            act.wait_ge(u_ready, 1)
            for k in range(KC):
                for b in range(B):
                    last = nc.scalar.activation(u_rep[:, k, b, :], u_col[:, k, b:b + 1].to_broadcast([P, P]), ACT.Copy)
            last.then_inc(rep_ready, 1)
            for g in range(NG):
                if g + 1 < NG:
                    act.wait_ge(x_turned, g + 2)
                    if g >= 1:
                        act.wait_ge(h_done, g)
                    columns(xT, xp, xT_ready, g + 1)
                act.wait_ge(h_turned, g + 1)
                if g >= 2:
                    act.wait_ge(r_done, g - 1)
                columns(hT, tp, hT_ready, g)
            act.wait_ge(step_done, 3)
            nc.scalar.activation(logits[:], logits[:], ACT.Exp).then_inc(exp_done, 1)

        @block.vector
        def _(dve):
            dve.wait_ge(urow_done, 1)
            nc.vector.tensor_copy(u_row[:].rearrange("p b c -> p (b c)"), up[:]).then_inc(urow_ready, 1)
            dve.wait_ge(urow_ready, 1)
            for g in range(NG):
                b = g // (NG // B)
                dve.wait_ge(h_done, g + 1)
                nc.vector.tensor_tensor(t["acc"][:, g * GT:(g + 1) * GT, :], hp[:],
                                        u_row[:, b:b + 1, :].to_broadcast([P, GT, D]), ALU.add).then_inc(h_ready, 1)
            wide = [P, NT, E2]
            dve.wait_ge(weights_in, 48)
            dve.wait_ge(r_done, NG)
            nc.vector.tensor_tensor(logits[:], rp_t, br[:].unsqueeze(1).to_broadcast(wide), ALU.add).then_inc(step_done, 1)
            dve.wait_ge(step_done, 1)
            nc.vector.tensor_reduce(top[:], logits[:], AX.X, ALU.max).then_inc(step_done, 1)
            dve.wait_ge(step_done, 2)
            nc.vector.tensor_tensor(logits[:], logits[:], top[:].unsqueeze(2).to_broadcast(wide),
                                    ALU.subtract).then_inc(step_done, 1)
            dve.wait_ge(exp_done, 1)
            nc.vector.tensor_reduce(total[:], logits[:], AX.X, ALU.add).then_inc(step_done, 1)
            dve.wait_ge(step_done, 4)
            nc.vector.reciprocal(total[:], total[:]).then_inc(step_done, 1)
            dve.wait_ge(step_done, 5)
            nc.vector.tensor_tensor(t["score2"][:], logits[:], total[:].unsqueeze(2).to_broadcast(wide),
                                    ALU.mult).then_inc(step_done, 1)
            dve.wait_ge(step_done, 6)
            nc.vector.tensor_copy(t["sel2"][:], t["score2"][:])


def constants(nc, t):
    with nc.semaphore("filled") as filled, nc.Block() as block:
        t["used"].append(filled)
        @block.gpsimd
        def _(pool):
            nc.gpsimd.memset(t["ident"][:], 0.0)
            nc.gpsimd.memset(t["ones"][:], 1.0)
            nc.gpsimd.memset(t["before"][:], 1.0).then_inc(filled, 1)
            nc.gpsimd.iota(t["first1"][:], [[0, NT], [-1, E1]], base=E1, channel_multiplier=0,
                           allow_small_or_imprecise_dtypes=True)
            nc.gpsimd.iota(t["first2"][:], [[0, NT], [-1, E2]], base=E2, channel_multiplier=0,
                           allow_small_or_imprecise_dtypes=True)
            nc.gpsimd.iota(t["slot_no"][:], [[1, S2], [0, E2]], base=0, channel_multiplier=0,
                           allow_small_or_imprecise_dtypes=True)
            nc.gpsimd.iota(t["token_no"][:], [[P, NT]], base=0, channel_multiplier=1,
                           allow_small_or_imprecise_dtypes=True)
            nc.gpsimd.iota(t["row_no"][:], [[1, P]], base=0, channel_multiplier=0,
                           allow_small_or_imprecise_dtypes=True)
            pool.wait_ge(filled, 1)
            nc.gpsimd.affine_select(out=t["ident"][:], in_=t["ident"][:], compare_op=ALU.not_equal, fill=1.0, base=0,
                                    pattern=[[-1, P]], channel_multiplier=1)
            nc.gpsimd.affine_select(out=t["before"][:], in_=t["before"][:], compare_op=ALU.is_ge, fill=0.0, base=-1,
                                    pattern=[[1, P]], channel_multiplier=-1)


def clear(nc, used):
    with nc.Block() as block:
        @block.gpsimd
        def _(pool):
            for sem in used:
                pool.sem_clear(sem)


def program(nc, d, out):
    with ExitStack() as ctx:
        def sb(name, shape, dt=F32):
            return ctx.enter_context(nc.sbuf_tensor(name, shape, dt))

        rows1 = nc.dram_tensor("rows1", [S1, P, D], F32, kind="Internal").ap()
        outs1 = nc.dram_tensor("outs1", [S1, P, D], F32, kind="Internal").ap()
        tokens2 = nc.dram_tensor("tokens2", [N, D], F32, kind="Internal").ap()
        outs2 = nc.dram_tensor("outs2", [S2, P, D], F32, kind="Internal").ap()
        flat = lambda a: a.rearrange("s p c -> (s p) c")
        d["rows1"], d["outs1"], d["tokens2"] = flat(rows1), flat(outs1), tokens2
        out_tiles = out.rearrange("b (t p) c -> p (b t) c", p=P)
        t = {
            "used": [],
            "ident": sb("ident", [P, P]), "ones": sb("ones", [P, P]), "before": sb("before", [P, P]),
            "first1": sb("first1", [P, NT, E1]), "first2": sb("first2", [P, NT, E2]),
            "slot_no": sb("slot_no", [P, S2, E2]),
            "score1": sb("score1", [P, NT, E1]), "sel1": sb("sel1", [P, NT, E1]),
            "score2": sb("score2", [P, NT, E2]), "sel2": sb("sel2", [P, NT, E2]),
            "a_gate": sb("a_gate", [P, 2, NT]), "a_row": sb("a_row", [P, 2, NT], U32), "a_owner": sb("a_owner", [P, S1], I32),
            "b_gate": sb("b_gate", [P, 2, NT]), "b_row": sb("b_row", [P, 2, NT], U32), "b_owner": sb("b_owner", [P, S2], I32),
            "token_no": sb("token_no", [P, NT]), "row_no": sb("row_no", [P, P]), "b_token": sb("b_token", [P, S2 + RING], U32),
            "x_tok": sb("x_tok", [P, NT, D]), "acc": sb("acc", [P, NT, D]),
            "pick": sb("pick", [P, LEVELS, CH // 2]),
            "vec": sb("vec", [P, 9 * KC]),
        }

        def dump(src):
            with nc.semaphore("dumped") as s, nc.Block() as block:
                @block.sync
                def _(sp):
                    sp.dma_start(out_tiles, src).then_inc(s, 16)
                    sp.wait_ge(s, 16)

        constants(nc, t)
        with (nc.sbuf_tensor("xT", [P, KC, N], F32) as xT, nc.sbuf_tensor("w1", [P, KC, HS], F32) as w1,
              nc.sbuf_tensor("w3", [P, KC, HS], F32) as w3, nc.sbuf_tensor("w2", [P, HS // P, D], F32) as w2,
              nc.sbuf_tensor("zero", [P, D], F32) as zero, nc.semaphore("weights_in") as weights_in,
              nc.semaphore("rows_cleared") as rows_cleared):
            t["xT"], t["w1"], t["w3"], t["w2"], t["zero"] = xT, w1, w3, w2, zero
            t["weights_in"], t["rows_cleared"] = weights_in, rows_cleared
            t["used"] += [weights_in, rows_cleared]
            router_front(nc, d, t)
            route(nc, t, E1, S1, t["sel1"], t["score1"], t["first1"], "a_")
            shared_expert(nc, d, t)
        if STOP == "front":
            return dump(t["acc"][:])
        expert_slots(nc, d, t, "a_", E1, H1, S1, rows1, outs1, d["W1e"], None, d["W2e"], None)
        chunked = [P, SEQ // CH, KC, B, CH]
        with (nc.sbuf_tensor("r_all", chunked, F32) as r_all, nc.sbuf_tensor("k_all", chunked, F32) as k_all,
              nc.sbuf_tensor("w_all", chunked, F32) as w_all):
            t["r_all"], t["k_all"], t["w_all"] = r_all[:], k_all[:], w_all[:]
            t["v_all"] = t["acc"][:].rearrange("p (j b) c -> p j b c", b=B)
            with nc.sbuf_tensor("qT", [P, KC, B, 1 + SEQ], F32) as qT:
                t["qT"] = qT
                mix_and_project(nc, d, t)
            recurrence(nc, d, t)
        if STOP == "wkv":
            return dump(t["x_tok"][:])
        clear(nc, t["used"])
        condition(nc, d, t)
        if STOP == "cond":
            return dump(t["acc"][:])
        route(nc, t, E2, S2, t["sel2"], t["score2"], t["first2"], "b_")
        expert_slots(nc, d, t, "b_", E2, H2, S2, None, outs2, d["W1"], d["b1"], d["W2"], d["b2"])
        combine(nc, t, "b_", t["x_tok"], flat(outs2), out_tiles)


_NAMES = {
    "x": "x", "cond": "cond_1024", "router_W": "L0_cond_router_W", "router_bias": "L0_cond_router_bias",
    "w1": "L0_cond_w1", "w3": "L0_cond_w3", "w2": "L0_cond_w2", "W1e": "L0_cond_W1e", "W2e": "L0_cond_W2e",
    "maa_x": "L0_attn_time_maa_x", "maa_w": "L0_attn_time_maa_w", "maa_k": "L0_attn_time_maa_k",
    "maa_v": "L0_attn_time_maa_v", "maa_r": "L0_attn_time_maa_r", "maa_w1": "L0_attn_time_maa_w1",
    "maa_w2": "L0_attn_time_maa_w2", "decay": "L0_attn_time_decay", "decay_w1": "L0_attn_time_decay_w1",
    "decay_w2": "L0_attn_time_decay_w2", "faaaa": "L0_attn_time_faaaa", "W_r": "L0_attn_W_r", "W_k": "L0_attn_W_k",
    "W_v": "L0_attn_W_v", "W_o": "L0_attn_W_o", "ln_w": "L0_attn_ln_w", "ln_b": "L0_attn_ln_b",
    "weight_matrix": "L0_cond2_weight_matrix", "W_proj": "L0_cond2_W_proj", "b_proj": "L0_cond2_b_proj",
    "Wr": "L0_ffn_Wr", "br": "L0_ffn_br", "W1": "L0_ffn_W1", "b1": "L0_ffn_b1", "W2": "L0_ffn_W2", "b2": "L0_ffn_b2",
}


def kernel(**inputs):
    import numpy as np
    import concourse.bacc as bacc
    from concourse.bass_utils import run_bass_kernel_spmd

    nc = bacc.Bacc("TRN2", target_bir_lowering=False, num_devices=1)
    arrays, dram = {}, {}
    for short, name in _NAMES.items():
        a = np.ascontiguousarray(inputs[name])
        arrays[f"in_{short}"] = a
        dram[short] = nc.dram_tensor(f"in_{short}", a.shape, mybir.dt.from_np(a.dtype), kind="ExternalInput").ap()
    out = nc.dram_tensor("out_0", (B, SEQ, D), F32, kind="ExternalOutput").ap()
    program(nc, dram, out)
    r = run_bass_kernel_spmd(nc, [arrays], core_ids=[0])
    return r.results[0]["out_0"]
```

```python
from contextlib import ExitStack

import concourse.bass as bass
from concourse import mybir

F32 = mybir.dt.float32
I32 = mybir.dt.int32
U32 = mybir.dt.uint32
ALU = mybir.AluOpType
ACT = mybir.ActivationFunctionType
AX = mybir.AxisListType

P = 128
B, SEQ, D = 2, 1024, 256
N = B * SEQ
NT = N // P
KC = D // P
GT = 4
NG = NT // GT
HS = 512
E1, H1 = 8, 256
E2, H2 = 16, 1024
RING1, RING2 = 8, 4
HEADS, HD = 4, 64
MIX, DEC = 32, 64
CH = 128
LEVELS = 7
LN_EPS = 0.00064


def slots_for(experts):
    return 2 * N // P + experts - 1


S1, S2 = slots_for(E1), slots_for(E2)


def router_front(nc, d, t):
    with ExitStack() as ctx:
        def sb(name, shape, dt=F32):
            return ctx.enter_context(nc.sbuf_tensor(name, shape, dt))

        def ps(name, shape, dt=F32):
            return ctx.enter_context(nc.psum_tensor(name, shape, dt))

        def sem(name):
            t["used"].append(ctx.enter_context(nc.semaphore(name)))
            return t["used"][-1]

        rw = sb("rw", [P, 2 * KC, E1])
        cond_col, cond_rep = sb("cond_col", [P, KC, B]), sb("cond_rep", [P, KC, B, P])
        bias_rep = sb("bias_rep", [P, E1])
        cond_part, logits = sb("cond_part", [P, B, E1]), sb("logits", [P, NT, E1])
        tp = [ps(f"tp{i}", [P, KC, GT * P]) for i in range(2)]
        rp, cp = ps("rp", [P, 512]), ps("cp", [P, 512])
        rp_t = rp[:, 0:NT * E1].rearrange("p (t e) -> p t e", e=E1)
        cp_b = cp[:, 0:B * E1].rearrange("p (b e) -> p b e", e=E1)
        x_in = [sem(f"x_in{g}") for g in range(NG)]
        zeroed = sem("zeroed")
        rw_in, cond_in, cond_ready, x_turned, xT_ready, c_done, c_taken, logits_done, summed, scores_ready = (
            sem("rw_in"), sem("cond_in"), sem("cond_ready"), sem("x_turned"), sem("xT_ready"), sem("c_done"),
            sem("c_taken"), sem("logits_done"), sem("summed"), sem("scores_ready"))
        block = ctx.enter_context(nc.Block())
        x_rows = d["x"].rearrange("b (t p) c -> p (b t) c", p=P)

        @block.sync
        def _(sp):
            for g in range(NG):
                sp.dma_start(t["x_tok"][:, g * GT:(g + 1) * GT, :], x_rows[:, g * GT:(g + 1) * GT, :]).then_inc(x_in[g], 16)
                if g:
                    continue
                sp.dma_start(rw[:], d["router_W"].rearrange("(k p) n -> p k n", p=P)).then_inc(rw_in, 16)
                sp.dma_start(bias_rep[:], d["router_bias"].unsqueeze(0).to_broadcast([P, E1])).then_inc(rw_in, 16)
                with nc.allow_non_contiguous_dma(reason="512 condition values, once"):
                    for b in range(B):
                        sp.dma_start(cond_col[:, :, b], d["cond"][b].rearrange("(k p) -> p k", p=P)).then_inc(cond_in, 16)
            for name in ("w1", "w3", "w2"):
                sp.dma_start(t[name][:], d[name].rearrange("(k p) n -> p k n", p=P)).then_inc(t["weights_in"], 16)
            sp.wait_ge(zeroed, 1)
            sp.dma_start(d["rows1"].rearrange("(s p) c -> p s c", p=P),
                         t["zero"][:].unsqueeze(1).to_broadcast([P, S1, D])).then_inc(t["rows_cleared"], 16)

        @block.gpsimd
        def _(pool):
            nc.gpsimd.memset(t["zero"][:], 0.0).then_inc(zeroed, 1)

        @block.tensor
        def _(pe):
            def turn(g):
                pe.wait_ge(x_in[g], 16)
                if g >= 2:
                    pe.wait_ge(xT_ready, g - 1)
                for tt in range(GT):
                    for k in range(KC):
                        last = nc.tensor.transpose(tp[g % 2][:, k, tt * P:(tt + 1) * P],
                                                   t["x_tok"][:, g * GT + tt, k * P:(k + 1) * P], t["ident"][:])
                last.then_inc(x_turned, 1)

            def logits_of(g):
                pe.wait_ge(xT_ready, g + 1)
                for tt in range(g * GT, (g + 1) * GT):
                    for k in range(KC):
                        last = nc.tensor.matmul(rp_t[:, tt, :], t["xT"][:, k, tt * P:(tt + 1) * P], rw[:, k, :],
                                                start=(k == 0), stop=(k == KC - 1))
                return last

            turn(0)
            turn(1)
            pe.wait_ge(rw_in, 32)
            for g in range(2, NG):
                logits_of(g - 2)
                turn(g)
            logits_of(NG - 2)
            pe.wait_ge(cond_ready, 1)
            for b in range(B):
                for k in range(KC):
                    last = nc.tensor.matmul(cp_b[:, b, :], cond_rep[:, k, b, :], rw[:, KC + k, :],
                                            start=(k == 0), stop=(k == KC - 1))
            last.then_inc(c_done, 1)
            logits_of(NG - 1).then_inc(logits_done, 1)

        @block.scalar
        def _(act):
            for g in range(NG):
                if g == 2:
                    act.wait_ge(cond_in, 32)
                    for k in range(KC):
                        for b in range(B):
                            last = nc.scalar.activation(cond_rep[:, k, b, :],
                                                        cond_col[:, k, b:b + 1].to_broadcast([P, P]), ACT.Copy)
                    last.then_inc(cond_ready, 1)
                act.wait_ge(x_turned, g + 1)
                for k in range(KC):
                    last = nc.scalar.activation(t["xT"][:, k, g * GT * P:(g + 1) * GT * P], tp[g % 2][:, k, :], ACT.Copy)
                last.then_inc(xT_ready, 1)
            act.wait_ge(summed, 1)
            nc.scalar.activation(t["score1"][:], logits[:], ACT.Sigmoid).then_inc(scores_ready, 1)

        @block.vector
        def _(dve):
            dve.wait_ge(c_done, 1)
            nc.vector.tensor_copy(cond_part[:], cp_b).then_inc(c_taken, 1)
            dve.wait_ge(c_taken, 1)
            dve.wait_ge(logits_done, 1)
            for b in range(B):
                own = slice(b * NT // B, (b + 1) * NT // B)
                last = nc.vector.tensor_tensor(logits[:, own, :], rp_t[:, own, :],
                                               cond_part[:, b:b + 1, :].to_broadcast([P, NT // B, E1]), ALU.add)
            last.then_inc(summed, 1)
            dve.wait_ge(scores_ready, 1)
            dve.wait_ge(rw_in, 32)
            nc.vector.tensor_tensor(t["sel1"][:], t["score1"][:], bias_rep[:].unsqueeze(1).to_broadcast([P, NT, E1]),
                                    ALU.add)


def shared_expert(nc, d, t, prefetch):
    with ExitStack() as ctx:
        def sb(name, shape, dt=F32):
            return ctx.enter_context(nc.sbuf_tensor(name, shape, dt))

        def ps(name, shape, dt=F32):
            return ctx.enter_context(nc.psum_tensor(name, shape, dt))

        def sem(name):
            t["used"].append(ctx.enter_context(nc.semaphore(name)))
            return t["used"][-1]

        C = HS // P
        w1, w3, w2 = t["w1"], t["w3"], t["w2"]
        sig, gate = sb("sig", [P, 2, GT * P]), sb("gate", [P, 2, GT * P])
        hT = sb("hT", [P, C, GT * P])
        gsum, gpos, gate_step = sb("gsum", [P, NT]), sb("gpos", [P, NT]), sem("gate_step")
        hp, gp, yp = ps("hp", [P, 2, GT * P]), ps("gp", [P, 2, GT * P]), ps("yp", [P, GT, 512])
        mask_step, rows_out = sem("mask_step"), t["rows_out"]
        h_ready, sig_ready, gate_ready, hT_ready, y_ready, y_out = (
            sem("h_ready"), sem("sig_ready"), sem("gate_ready"), sem("hT_ready"), sem("y_ready"), sem("y_out"))
        block = ctx.enter_context(nc.Block())

        @block.sync
        def _(sp):
            prefetch(sp)

        @block.gpsimd
        def _(pool):
            pool.wait_ge(t["rows_cleared"], 16)
            for tt in range(NT):
                for k in range(2):
                    pool.indirect_dma_start(d["rows1"], bass.IndirectOffsetOnAxis(t["a_row"][:, k, tt:tt + 1], 0),
                                            t["x_tok"][:, tt, :], None).then_inc(rows_out, 16)
            nc.gpsimd.memset(t["pick"][:], 1.0).then_inc(mask_step, 1)
            for l in range(LEVELS):
                m = 1 << l
                view = t["pick"][:, l, :].rearrange("p (n m) -> p n m", m=m)
                for q, (mult, pat, base) in enumerate(((1, -2 * m, 0), (-1, 2 * m, m - 1))):
                    pool.wait_ge(mask_step, 2 * l + q + 1)
                    nc.gpsimd.affine_select(out=view, in_=view, compare_op=ALU.is_ge, fill=0.0, base=base,
                                            pattern=[[pat, CH // 2 // m], [0, m]],
                                            channel_multiplier=mult).then_inc(mask_step, 1)
            pool.wait_ge(rows_out, 32 * NT)

        @block.tensor
        def _(pe):
            pe.wait_ge(t["weights_in"], 48)
            with pe.Fori(0, NG) as g:
                for c in range(C):
                    pe.wait_ge(hT_ready, 1 + g * C + (c - 1 if c >= 2 else 0))
                    for w, o in ((w1, hp), (w3, gp)):
                        for k in range(KC):
                            last = nc.tensor.matmul(o[:, c % 2, :], w[:, k, c * P:(c + 1) * P],
                                                    t["xT"][:, k, bass.ds(g * (GT * P), GT * P)],
                                                    start=(k == 0), stop=(k == KC - 1))
                    last.then_inc(h_ready, 1)
                pe.wait_ge(y_out, 1 + g)
                for c in range(C):
                    pe.wait_ge(hT_ready, 1 + g * C + c + 1)
                    for tt in range(GT):
                        last = nc.tensor.matmul(yp[:, tt, 0:D], hT[:, c, tt * P:(tt + 1) * P], w2[:, c, :],
                                                start=(c == 0), stop=(c == C - 1))
                last.then_inc(y_ready, 1)

        @block.scalar
        def _(act):
            with act.Fori(0, NG) as g:
                for c in range(C):
                    act.wait_ge(h_ready, g * C + c + 1)
                    act.wait_ge(hT_ready, 1 + g * C + (c - 1 if c >= 2 else 0))
                    nc.scalar.activation(sig[:, c % 2, :], hp[:, c % 2, :], ACT.Sigmoid).then_inc(sig_ready, 1)

        @block.vector
        def _(dve):
            for primed in (hT_ready, y_out, y_ready):
                dve.sem_inc(primed, 1)
            g, steps = t["a_gate"], [0]

            def link(ins):
                steps[0] += 1
                ins.then_inc(gate_step, 1)
                dve.wait_ge(gate_step, steps[0])

            link(nc.vector.tensor_tensor(gsum[:], g[:, 0, :], g[:, 1, :], ALU.add))
            link(nc.vector.tensor_scalar(gpos[:], gsum[:], 1e-9, None, ALU.is_gt))
            link(nc.vector.tensor_scalar(gsum[:], gsum[:], 1e-9, None, ALU.add))
            link(nc.vector.reciprocal(gsum[:], gsum[:]))
            link(nc.vector.tensor_tensor(gsum[:], gsum[:], gpos[:], ALU.mult))
            link(nc.vector.tensor_scalar(gpos[:], gpos[:], -0.5, 0.5, ALU.mult, ALU.add))
            link(nc.vector.tensor_tensor(g[:], g[:], gsum[:].unsqueeze(1).to_broadcast([P, 2, NT]), ALU.mult))
            link(nc.vector.tensor_tensor(g[:], g[:], gpos[:].unsqueeze(1).to_broadcast([P, 2, NT]), ALU.add))
            with dve.Fori(0, NG) as g:
                for c in range(C):
                    dve.wait_ge(sig_ready, g * C + c + 1)
                    nc.vector.tensor_tensor(gate[:, c % 2, :], sig[:, c % 2, :], hp[:, c % 2, :],
                                            ALU.mult).then_inc(gate_ready, 1)
                    dve.wait_ge(gate_ready, g * C + c + 1)
                    if c == 0:
                        dve.wait_ge(y_ready, 1 + g)
                    nc.vector.tensor_tensor(hT[:, c, :], gate[:, c % 2, :], gp[:, c % 2, :],
                                            ALU.mult).then_inc(hT_ready, 1)
                dve.wait_ge(y_ready, 1 + g + 1)
                nc.vector.tensor_copy(t["acc"][:, bass.ds(g * GT, GT), :], yp[:, :, 0:D]).then_inc(y_out, 1)


def route(nc, t, experts, slots, sel, val, first, tag, prefetch=None):
    with ExitStack() as ctx:
        def sb(name, shape, dt=F32):
            return ctx.enter_context(nc.sbuf_tensor(tag + name, shape, dt))

        cand, onehot = sb("cand", [P, NT, experts]), sb("onehot", [P, 2, NT, experts])
        best, order = sb("best", [P, NT]), sb("order", [P, NT])
        both, rank = sb("both", [P, NT, experts]), sb("rank", [P, NT, experts])
        run = sb("run", [P, 2, NT, experts])
        count_i = sb("count_i", [P, experts], I32)
        tiles = sb("tiles", [P, experts])
        ends = sb("ends", [P, 2, experts])
        prod, picked = sb("prod", [P, NT, experts]), sb("picked", [P, NT])
        over = sb("over", [P, slots, experts])
        ends_f = sb("ends_f", [P, slots])
        cp = ctx.enter_context(nc.psum_tensor(tag + "cp", [P, 2, 512], F32))
        if tag == "b_":
            QUARTER = 2 * NT // 4
            place, place_i, place_slot = sb("place", [P, NT]), sb("place_i", [P, NT], I32), sb("place_slot", [P, NT])
            in_row, in_slot = sb("in_row", [P, 2 * NT, P]), sb("in_slot", [P, 2 * NT, slots])
            tk = ctx.enter_context(nc.psum_tensor(tag + "tk", [P, 512], F32))
            row_ready, table_done = (ctx.enter_context(nc.semaphore(tag + n)) for n in ("row_ready", "table_done"))
        counts_ready, both_ready, owner_ready, step_done = (
            ctx.enter_context(nc.semaphore(tag + n)) for n in ("counts_ready", "both_ready", "owner_ready", "step_done"))
        t["used"] += [counts_ready, both_ready, owner_ready, step_done]
        block = ctx.enter_context(nc.Block())
        if prefetch is not None:
            @block.sync
            def _(sp):
                sp.wait_ge(owner_ready, 1)
                prefetch(sp)

        width = NT * experts
        full = [P, NT, experts]

        @block.tensor
        def _(pe):
            pe.wait_ge(both_ready, 1)
            flat = both[:].rearrange("p t e -> p (t e)")
            nc.tensor.matmul(cp[:, 0, 0:width], t["before"][:], flat, start=True, stop=True)
            nc.tensor.matmul(cp[:, 1, 0:width], t["ones"][:], flat, start=True, stop=True).then_inc(counts_ready, 1)
            if tag == "b_":
                for q in range(2 * NT):
                    if q % QUARTER == 0:
                        pe.wait_ge(row_ready, q // QUARTER + 1)
                    last = nc.tensor.matmul(tk[:, 0:slots], in_row[:, q, :], in_slot[:, q, :], start=(q == 0),
                                            stop=(q == 2 * NT - 1))
                last.then_inc(table_done, 1)

        @block.vector
        def _(dve):
            steps = [0]

            def link(ins):
                steps[0] += 1
                ins.then_inc(step_done, 1)
                dve.wait_ge(step_done, steps[0])

            for k in range(2):
                link(nc.vector.tensor_reduce(best[:], sel[:], AX.X, ALU.max))
                link(nc.vector.tensor_tensor(cand[:], sel[:], best[:].unsqueeze(2).to_broadcast(full), ALU.is_equal))
                link(nc.vector.tensor_tensor(cand[:], cand[:], first[:], ALU.mult))
                link(nc.vector.tensor_reduce(order[:], cand[:], AX.X, ALU.max))
                link(nc.vector.tensor_tensor(onehot[:, k], cand[:], order[:].unsqueeze(2).to_broadcast(full),
                                             ALU.is_equal))
                if k == 0:
                    link(nc.vector.scalar_tensor_tensor(sel[:], onehot[:, 0], -3.0e38, sel[:], ALU.mult, ALU.add))
            nc.vector.tensor_tensor(both[:], onehot[:, 0], onehot[:, 1], ALU.add).then_inc(both_ready, 1)
            for k in range(2):
                link(nc.vector.tensor_tensor(prod[:], onehot[:, k], val[:], ALU.mult))
                link(nc.vector.tensor_reduce(t[tag + "gate"][:, k, :], prod[:], AX.X, ALU.add))
            dve.wait_ge(counts_ready, 1)
            total = cp[:, 1, 0:width].rearrange("p (t e) -> p t e", e=experts)
            link(nc.vector.tensor_copy(run[:, 0], total))
            now, d = 0, 1
            while d < NT:
                steps[0] += 1
                nc.vector.tensor_copy(run[:, 1 - now, 0:d], run[:, now, 0:d]).then_inc(step_done, 1)
                link(nc.vector.tensor_tensor(run[:, 1 - now, d:NT], run[:, now, d:NT], run[:, now, 0:NT - d], ALU.add))
                now, d = 1 - now, 2 * d
            link(nc.vector.tensor_scalar(count_i[:], run[:, now, NT - 1], float(P - 1), None, ALU.add))
            link(nc.vector.tensor_scalar(count_i[:], count_i[:], 7, None, ALU.arith_shift_right))
            link(nc.vector.tensor_copy(tiles[:], count_i[:]))
            link(nc.vector.tensor_copy(ends[:, 0], tiles[:]))
            at, d = 0, 1
            while d < experts:
                steps[0] += 1
                nc.vector.tensor_copy(ends[:, 1 - at, 0:d], ends[:, at, 0:d]).then_inc(step_done, 1)
                link(nc.vector.tensor_tensor(ends[:, 1 - at, d:experts], ends[:, at, d:experts],
                                             ends[:, at, 0:experts - d], ALU.add))
                at, d = 1 - at, 2 * d
            link(nc.vector.tensor_tensor(rank[:], run[:, now], total, ALU.subtract))
            link(nc.vector.tensor_tensor(rank[:], rank[:],
                                         cp[:, 0, 0:width].rearrange("p (t e) -> p t e", e=experts), ALU.add))
            link(nc.vector.tensor_tensor(tiles[:], ends[:, at], tiles[:], ALU.subtract))
            link(nc.vector.tensor_scalar(tiles[:], tiles[:], float(P), None, ALU.mult))
            link(nc.vector.tensor_tensor(rank[:], rank[:], tiles[:].unsqueeze(1).to_broadcast(full), ALU.add))
            link(nc.vector.tensor_tensor(over[:], ends[:, at].unsqueeze(1).to_broadcast([P, slots, experts]),
                                         t["slot_no"][:, 0:slots, 0:experts], ALU.is_le))
            link(nc.vector.tensor_reduce(ends_f[:], over[:], AX.X, ALU.add))
            nc.vector.tensor_scalar(t[tag + "owner"][:], ends_f[:], float(experts - 1), None,
                                    ALU.min).then_inc(owner_ready, 1)
            for k in range(2):
                link(nc.vector.tensor_tensor(prod[:], onehot[:, k], rank[:], ALU.mult))
                link(nc.vector.tensor_reduce(picked[:], prod[:], AX.X, ALU.add))
                link(nc.vector.tensor_copy(t[tag + "row"][:, k, :], picked[:]))
                if tag == "b_":
                    own = slice(k * NT, (k + 1) * NT)
                    link(nc.vector.tensor_copy(place_i[:], picked[:]))
                    link(nc.vector.tensor_scalar(place_i[:], place_i[:], 7, None, ALU.arith_shift_right))
                    link(nc.vector.tensor_copy(place_slot[:], place_i[:]))
                    link(nc.vector.scalar_tensor_tensor(place[:], place_slot[:], -float(P), picked[:], ALU.mult, ALU.add))
                    link(nc.vector.tensor_tensor(in_slot[:, own, :], place_slot[:].unsqueeze(2).to_broadcast([P, NT, slots]),
                                                 t["slot_no"][:, 0:slots, 0].unsqueeze(1).to_broadcast([P, NT, slots]),
                                                 ALU.is_equal))
                    link(nc.vector.tensor_tensor(in_slot[:, own, :], in_slot[:, own, :],
                                                 t["token_no"][:].unsqueeze(2).to_broadcast([P, NT, slots]), ALU.mult))
                    for q in range(2):
                        part = slice(q * QUARTER, (q + 1) * QUARTER)
                        last = nc.vector.tensor_tensor(in_row[:, k * NT + q * QUARTER:k * NT + (q + 1) * QUARTER, :],
                                                       place[:, part].unsqueeze(2).to_broadcast([P, QUARTER, P]),
                                                       t["row_no"][:].unsqueeze(1).to_broadcast([P, QUARTER, P]),
                                                       ALU.is_equal)
                        last.then_inc(row_ready, 1)
                        dve.wait_ge(row_ready, 2 * k + q + 1)
            if tag == "b_":
                link(nc.vector.memset(t["b_token"][:], 0))
                dve.wait_ge(table_done, 1)
                link(nc.vector.tensor_copy(t["b_token"][:, 0:slots], tk[:, 0:slots]))


def slot_buffers(nc, ctx, tag, RING, hidden, biased):
    def sb(name, shape):
        return ctx.enter_context(nc.sbuf_tensor(tag + name, shape, F32))

    C = hidden // P
    return {
        "ring": RING,
        "wa": [sb(f"wa{b}", [P, KC, hidden]) for b in range(RING)],
        "wb": [sb(f"wb{b}", [P, C, D]) for b in range(RING)],
        "ba": [sb(f"ba{b}", [P, C]) for b in range(RING)] if biased else None,
        "bb": [sb(f"bb{b}", [P, D]) for b in range(RING)] if biased else None,
        "loaded": [ctx.enter_context(nc.semaphore(f"{tag}loaded{b}")) for b in range(RING)],
    }


def load_weights(nc, sp, t, bufs, tag, s, b, W1, b1, W2, b2):
    loaded = bufs["loaded"][b]
    e = sp.value_load(t[tag + "owner"][0:1, bass.ds(s, 1)], min_val=0, max_val=W1.shape[0] - 1)
    sp.dma_start(bufs["wa"][b][:], W1[bass.ds(e, 1), :, :].rearrange("e (k p) n -> p (e k) n", p=P)).then_inc(loaded, 16)
    sp.dma_start(bufs["wb"][b][:], W2[bass.ds(e, 1), :, :].rearrange("e (p c) n -> p (e c) n", p=P)).then_inc(loaded, 16)
    if b1 is not None:
        sp.dma_start(bufs["ba"][b][:], b1[bass.ds(e, 1), :].rearrange("e (p c) -> p (e c)", p=P)).then_inc(loaded, 16)
        sp.dma_start(bufs["bb"][b][:], b2[bass.ds(e, 1), :].to_broadcast([P, D])).then_inc(loaded, 16)


def expert_slots(nc, d, t, bufs, tag, experts, hidden, slots, rows, outs, W1, b1, W2, b2):
    C, RING = hidden // P, bufs["ring"]
    with ExitStack() as ctx:
        def sb(name, shape, dt=F32):
            return ctx.enter_context(nc.sbuf_tensor(tag + name, shape, dt))

        def ps(name, shape, dt=F32):
            return ctx.enter_context(nc.psum_tensor(tag + name, shape, dt))

        def ring(name):
            return [ctx.enter_context(nc.semaphore(f"{tag}{name}{b}")) for b in range(RING)]

        def sem(name):
            return ctx.enter_context(nc.semaphore(tag + name))

        wa, wb, ba, bb, loaded = (bufs[n] for n in ("wa", "wb", "ba", "bb", "loaded"))
        xr = [sb(f"xr{b}", [P, D]) for b in range(RING)]
        xT = [sb(f"xT{b}", [P, KC, P]) for b in range(RING)]
        hT = [sb(f"hT{b}", [P, C, P]) for b in range(RING)]
        yo = [sb(f"yo{b}", [P, D]) for b in range(RING)]
        HB = 2 if C > 4 else 1
        tp = [ps(f"tp{b}", [P, 512]) for b in range(1)]
        hp = [ps(f"hp{b}", [P, HB, 4, P]) for b in range(2)]
        yp = [ps(f"yp{b}", [P, 512]) for b in range(2)]
        freed, stored = ring("freed"), ring("stored")
        x_turned, xT_ready, h_ready, hT_ready, y_ready = (
            sem("x_turned"), sem("xT_ready"), sem("h_ready"), sem("hT_ready"), sem("y_ready"))
        gathered = rows is None
        rows_in = ring("rows_in")
        if gathered:
            token_ready, token_seen = sem("token_ready"), sem("token_seen")
            token = [sb(f"token{b}", [P, 1], U32) for b in range(RING)]
        loads = 4 if b1 is not None else 2
        block = ctx.enter_context(nc.Block())
        whole, rest = slots // RING, slots % RING

        def each_slot(eng, slot, rounds=1):
            with eng.Fori(0, whole // rounds) as i:
                for r in range(rounds):
                    for j in range(RING):
                        slot(i * (rounds * RING) + r * RING + j, j, i * rounds + r)
            for s in range(whole // rounds * rounds * RING, slots):
                slot(s, s % RING, s // RING)

        @block.sync
        def _(sp):
            def fetch_rows(s, b):
                if not gathered:
                    sp.dma_start(xr[b][:], rows[bass.ds(s, 1), :, :].rearrange("s p c -> (s p) c")).then_inc(rows_in[b], 16)

            def load(s, b, use):
                sp.wait_ge(freed[b], 1 + use)
                fetch_rows(s, b)
                load_weights(nc, sp, t, bufs, tag, s, b, W1, b1, W2, b2)

            for b in range(RING):
                fetch_rows(b, b)
            sp.wait_ge(rows_in[0], 16)
            load_weights(nc, sp, t, bufs, tag, RING - 1, RING - 1, W1, b1, W2, b2)
            with sp.Fori(1, whole) as i:
                for j in range(RING):
                    load(i * RING + j, j, i)
            for j in range(rest):
                load(whole * RING + j, j, whole)

        @block.tensor
        def _(pe):
            def turn(s, b, use):
                pe.wait_ge(rows_in[b], use * 16 + 16)
                pe.wait_ge(xT_ready, s)
                for k in range(KC):
                    last = nc.tensor.transpose(tp[0][:, k * P:(k + 1) * P], xr[b][:, k * P:(k + 1) * P], t["ident"][:])
                last.then_inc(x_turned, 1)

            def up(s, b, use, q):
                pe.wait_ge(loaded[b], use * (16 * loads) + 16 * loads)
                pe.wait_ge(xT_ready, s + 1)
                if q is not None:
                    pe.wait_ge(hT_ready, 1 + q)
                for c in range(C):
                    for k in range(KC):
                        last = nc.tensor.matmul(hp[b % 2][:, c // 4, c % 4, :], wa[b][:, k, c:hidden:C], xT[b][:, k, :],
                                                start=(k == 0), stop=(k == KC - 1))
                last.then_inc(h_ready, 1)

            def down(s, b, use):
                pe.wait_ge(hT_ready, 1 + s + 1)
                pe.wait_ge(freed[(b - 2) % RING], 1 + use + (1 if b >= 2 else 0))
                for c in range(C):
                    last = nc.tensor.matmul(yp[b % 2][:, 0:D], hT[b][:, c, :], wb[b][:, c, :],
                                            start=(c == 0), stop=(c == C - 1))
                last.then_inc(y_ready, 1)

            turn(0, 0, 0)
            up(0, 0, 0, None)
            turn(1, 1, 0)
            steps = (slots - 2) // RING
            with pe.Fori(0, steps) as i:
                for j in range(RING):
                    s, b = i * RING + j + 1, (j + 1) % RING
                    up(s, b, i + (j + 1) // RING, i * RING + j)
                    turn(i * RING + j + 2, (j + 2) % RING, i + (j + 2) // RING)
                    down(i * RING + j, j, i)
            for s in range(steps * RING + 1, slots):
                up(s, s % RING, s // RING, s - 1)
                if s + 1 < slots:
                    turn(s + 1, (s + 1) % RING, (s + 1) // RING)
                down(s - 1, (s - 1) % RING, (s - 1) // RING)
            down(slots - 1, (slots - 1) % RING, (slots - 1) // RING)

        @block.scalar
        def _(act):
            def hidden_values(s, b, use):
                act.wait_ge(h_ready, s + 1)
                act.wait_ge(freed[b], 1 + use)
                if b1 is None:
                    last = nc.scalar.activation(hT[b][:], hp[b % 2][:, 0, 0:C, :], ACT.Gelu)
                else:
                    for c in range(C):
                        last = nc.scalar.activation(hT[b][:, c, :], hp[b % 2][:, c // 4, c % 4, :], ACT.Relu,
                                                    bias=ba[b][:, c:c + 1])
                last.then_inc(hT_ready, 1)
            each_slot(act, hidden_values, 12 // RING)

        @block.vector
        def _(dve):
            for primed in (*freed, hT_ready):
                dve.sem_inc(primed, 1)
            def turned(s, b, use):
                dve.wait_ge(x_turned, s + 1)
                nc.vector.tensor_copy(xT[b][:].rearrange("p k n -> p (k n)"), tp[0][:, 0:D]).then_inc(xT_ready, 1)

            def result(s, b, use):
                dve.wait_ge(y_ready, s + 1)
                if use is not None:
                    dve.wait_ge(stored[b], 16 * use)
                if b2 is None:
                    ins = nc.vector.tensor_copy(yo[b][:], yp[b % 2][:, 0:D])
                else:
                    ins = nc.vector.tensor_tensor(yo[b][:], yp[b % 2][:, 0:D], bb[b][:], ALU.add)
                ins.then_inc(freed[b], 1)
                if gathered:
                    dve.wait_ge(rows_in[b], 16 * (0 if use is None else use) + 16)
                    list_tokens(s + RING, b)

            def list_tokens(s, b):
                nc.vector.tensor_copy(token[b][:], t["b_token"][:, bass.ds(s, 1)]).then_inc(token_ready, 1)

            if gathered:
                for b in range(RING):
                    list_tokens(b, b)
            turned(0, 0, 0)
            turned(1, 1, 0)
            steps = (slots - 2) // RING
            for j in range(RING):
                turned(j + 2, (j + 2) % RING, None)
                result(j, j, None)
            with dve.Fori(1, steps) as i:
                for j in range(RING):
                    turned(i * RING + j + 2, (j + 2) % RING, None)
                    result(i * RING + j, j, i)
            for s in range(steps * RING, slots):
                if s + 2 < slots:
                    turned(s + 2, (s + 2) % RING, None)
                result(s, s % RING, s // RING)

        @block.gpsimd
        def _(pool):
            def store(s, b, use):
                pool.wait_ge(freed[b], 1 + use + 1)
                pool.dma_start(outs[bass.ds(s, 1), :, :].rearrange("s p c -> (s p) c"), yo[b][:]).then_inc(stored[b], 16)

            def gather(s, b):
                pool.wait_ge(token_ready, s + 1)
                pool.sem_inc(token_seen, 1)
                pool.indirect_dma_start(xr[b][:], None, d["tokens2"],
                                        bass.IndirectOffsetOnAxis(token[b][:, 0:1], 0)).then_inc(rows_in[b], 16)

            if gathered:
                for s in range(RING):
                    gather(s, s)
                ahead = slots - RING
                with pool.Fori(0, ahead // RING) as i:
                    for j in range(RING):
                        store(i * RING + j, j, i)
                        gather(i * RING + j + RING, j)
                for s in range(ahead // RING * RING, slots):
                    store(s, s % RING, s // RING)
                    if s + RING < slots:
                        gather(s + RING, s % RING)
            else:
                each_slot(pool, store)
            for b in range(RING):
                pool.wait_ge(stored[b], 16 * (whole + (b < rest)))


def combine(nc, t, tag, base, outs, finish):
    GB = 4
    with ExitStack() as ctx:
        gb = [ctx.enter_context(nc.sbuf_tensor(f"{tag}gb{b}", [P, 2, D], F32)) for b in range(GB)]
        part = [ctx.enter_context(nc.sbuf_tensor(f"{tag}part{b}", [P, D], F32)) for b in range(GB)]
        res = [ctx.enter_context(nc.sbuf_tensor(f"{tag}res{b}", [P, D], F32)) for b in range(GB)]
        got = [ctx.enter_context(nc.semaphore(f"{tag}got{b}")) for b in range(GB)]
        part_ready = ctx.enter_context(nc.semaphore(tag + "part_ready"))
        res_ready = ctx.enter_context(nc.semaphore(tag + "res_ready"))
        sent = [ctx.enter_context(nc.semaphore(f"{tag}sent{b}")) for b in range(GB)]
        block = ctx.enter_context(nc.Block())
        row, gate = t[tag + "row"], t[tag + "gate"]

        @block.gpsimd
        def _(pool):
            for tt in range(NT):
                if tt >= GB:
                    pool.wait_ge(res_ready, tt - GB + 1)
                for k in range(2):
                    pool.indirect_dma_start(gb[tt % GB][:, k, :], None, outs,
                                            bass.IndirectOffsetOnAxis(row[:, k, tt:tt + 1], 0)).then_inc(got[tt % GB], 16)

        @block.vector
        def _(dve):
            for tt in range(NT):
                dve.wait_ge(got[tt % GB], 32 * (tt // GB + 1))
                nc.vector.scalar_tensor_tensor(part[tt % GB][:], gb[tt % GB][:, 0, :], gate[:, 0, tt:tt + 1],
                                               base[:, tt, :], ALU.mult, ALU.add).then_inc(part_ready, 1)
                dve.wait_ge(part_ready, tt + 1)
                if tt >= GB:
                    dve.wait_ge(sent[tt % GB], 16 * (tt // GB))
                nc.vector.scalar_tensor_tensor(res[tt % GB][:], gb[tt % GB][:, 1, :], gate[:, 1, tt:tt + 1],
                                               part[tt % GB][:], ALU.mult, ALU.add).then_inc(res_ready, 1)

        @block.sync
        def _(sp):
            for tt in range(NT):
                sp.wait_ge(res_ready, tt + 1)
                sp.dma_start(finish[:, tt, :], res[tt % GB][:]).then_inc(sent[tt % GB], 16)
            for b in range(GB):
                sp.wait_ge(sent[b], 16 * (NT // GB))


def mix_and_project(nc, d, t):
    NI = 4
    W = SEQ // NI
    TB = W // P
    COLS = B * W
    BANKS = 6
    SHIFT_ORDER = (3, 1, 0, 2)
    names = ["maa_x", "maa_w", "maa_k", "maa_v", "maa_r", "decay", "ln_w", "ln_b", "faaaa"]
    vec = t["vec"]

    with ExitStack() as ctx:
        def sb(name, shape, dt=F32):
            return ctx.enter_context(nc.sbuf_tensor(name, shape, dt))

        def sem(name):
            return ctx.enter_context(nc.semaphore(name))

        maa1, maa2 = sb("maa1", [P, KC, P]), sb("maa2", [P, D])
        dw1, dw2 = sb("dw1", [P, KC, DEC]), sb("dw2", [DEC, D])
        wr, wk, wv = (sb(n, [P, KC, D]) for n in ("wr", "wk", "wv"))
        vec_rows = sb("vec_rows", [len(names) * KC, P])
        xx = [sb(f"xx{i}", [P, KC, B, W]) for i in range(2)]
        xxx = sb("xxx", [P, KC, B, W])
        mix = [sb(f"mix{i}", [P, COLS]) for i in range(2)]
        shifted = [[sb(f"shifted{i}{f}", [P, KC, B, W]) for f in range(4)] for i in range(2)]
        dlow, rate = sb("dlow", [DEC, COLS]), sb("rate", [P, KC, COLS])
        gb = [sb(f"gb{q}", [P, 2, D]) for q in range(B * TB)]
        res = [sb(f"res{q}", [P, D]) for q in range(B * TB)]
        got = [sem(f"got{q}") for q in range(B * TB)]
        sum_step, q_ready = sem("sum_step"), sem("q_ready")
        pw = [ctx.enter_context(nc.psum_tensor(f"pw{i}", [P, 512], F32)) for i in range(BANKS)]
        pv = ctx.enter_context(nc.psum_tensor("pv", [P, 512], F32))
        ld, vec_in, vec_turned, vec_ready, zeroed = sem("ld"), sem("vec_in"), sem("vec_turned"), sem("vec_ready"), sem("q_zeroed")
        diff_ready, xxx_ready, mix_ready, moved, shifted_ready = (
            sem("diff_ready"), sem("xxx_ready"), sem("mix_ready"), sem("moved"), sem("shifted_ready"))
        rk_ready, low_ready, rate_ready, w_ready, v_ready = (
            sem("rk_ready"), sem("low_ready"), sem("rate_ready"), sem("w_ready"), sem("v_ready"))
        done = [sem(f"wide_done{i}") for i in range(BANKS)]
        block = ctx.enter_context(nc.Block())

        jobs = [("turn", 0, b) for b in range(B)]
        for i in range(NI + 1):
            jobs += [("mix", i)] if i < NI else []
            jobs += [(x, i - 1, c) for x in "rk" for c in range(KC)] if i else []
            jobs += [("shift", i, f, c) for f in range(4) for c in range(KC)] if i < NI else []
            jobs += [("turn", i + 1, b) for b in range(B)] if i + 1 < NI else []
            jobs += [("low", i - 1), ("v", i - 1, 0), ("v", i - 1, 1), ("dec", i - 1, 0), ("dec", i - 1, 1)] if i else []
        number = {job: n for n, job in enumerate(jobs)}

        def taken_by(job):
            kind, i = job[0], job[1]
            return {"turn": lambda: (q_ready, B * i + job[2] + 1),
                    "mix": lambda: (mix_ready, i + 1),
                    "shift": lambda: (moved, 8 * i + 2 * job[2] + job[3] + 1),
                    "r": lambda: (rk_ready, 4 * i + job[2] + 1),
                    "k": lambda: (rk_ready, 4 * i + 2 + job[2] + 1),
                    "low": lambda: (low_ready, i + 1),
                    "v": lambda: (v_ready, 2 * i + job[2] + 1),
                    "dec": lambda: (rate_ready, 2 * i + job[2] + 1)}[kind]()

        def bank(job):
            return pw[number[job] % BANKS]

        def arrived(eng, job):
            n = number[job]
            eng.wait_ge(done[n % BANKS], n // BANKS + 1)

        def col(name, c):
            n = names.index(name) * KC + c
            return vec[:, n:n + 1]

        def tile_of(i, q):
            return q // TB * (NT // B) + i * TB + q % TB

        def token_cols(i, back):
            return t["qT"][:, :, :, 1 - back + i * W:1 - back + (i + 1) * W].rearrange("p k b w -> p (k b) w")

        def chunks_of(ap, i, c):
            return ap[:, i * (W // CH):(i + 1) * (W // CH), c].rearrange("p j b x -> p b j x")

        @block.sync
        def _(sp):
            for name, cols in (("maa_w1", maa1), ("W_r", wr), ("W_k", wk), ("W_v", wv), ("decay_w1", dw1)):
                sp.dma_start(cols[:], d[name].rearrange("(k p) n -> p k n", p=P)).then_inc(ld, 16)
            sp.dma_start(maa2[:], d["maa_w2"].rearrange("f l c -> (f l) c")).then_inc(ld, 16)
            sp.dma_start(dw2[:], d["decay_w2"]).then_inc(ld, 16)

        @block.tensor
        def _(pe):
            for n, job in enumerate(jobs):
                kind, i = job[0], job[1]
                if n == B:
                    pe.wait_ge(vec_in, 16 * len(names))
                    nc.tensor.transpose(pv[:, 0:len(names) * KC], vec_rows[:],
                                        t["ident"][0:len(names) * KC, 0:len(names) * KC]).then_inc(vec_turned, 1)
                    pe.wait_ge(ld, 16 * 7)
                if n >= BANKS:
                    pe.wait_ge(*taken_by(jobs[n - BANKS]))
                o, s = bank(job), shifted[i % 2]
                if kind == "turn":
                    for q in range(TB):
                        place = job[2] * TB + q
                        pe.wait_ge(sum_step, 2 * (B * TB * i + place) + 2)
                        for k in range(KC):
                            last = nc.tensor.transpose(o[:, k * W + q * P:k * W + (q + 1) * P],
                                                       res[place][:, k * P:(k + 1) * P], t["ident"][:])
                elif kind == "mix":
                    pe.wait_ge(xxx_ready, i + 1)
                    for c in range(KC):
                        last = nc.tensor.matmul(o[:], maa1[:, c, :], xxx[:, c].rearrange("p b w -> p (b w)"),
                                                start=(c == 0), stop=(c == KC - 1))
                elif kind == "shift":
                    f, c = job[2:]
                    pe.wait_ge(mix_ready, i + 1)
                    last = nc.tensor.matmul(o[:], maa2[MIX * f:MIX * f + MIX, c * P:(c + 1) * P],
                                            mix[i % 2][MIX * f:MIX * f + MIX, :], start=True, stop=True,
                                            tile_position=(MIX * f, 0))
                elif kind in "rk":
                    c = job[2]
                    wt, f = (wr, 3) if kind == "r" else (wk, 1)
                    pe.wait_ge(shifted_ready, 4 * i + SHIFT_ORDER.index(f) + 1)
                    for kk in range(KC):
                        last = nc.tensor.matmul(o[:], wt[:, kk, c * P:(c + 1) * P], s[f][:, kk].rearrange("p b w -> p (b w)"),
                                                start=(kk == 0), stop=(kk == KC - 1))
                elif kind == "low":
                    pe.wait_ge(shifted_ready, 4 * i + SHIFT_ORDER.index(0) + 1)
                    for kk in range(KC):
                        last = nc.tensor.matmul(o[0:DEC, :], dw1[:, kk, :], s[0][:, kk].rearrange("p b w -> p (b w)"),
                                                start=(kk == 0), stop=(kk == KC - 1))
                elif kind == "v":
                    pe.wait_ge(shifted_ready, 4 * i + SHIFT_ORDER.index(2) + 1)
                    for q in range(2):
                        for kk in range(KC):
                            last = nc.tensor.matmul(o[:, q * D:(q + 1) * D], s[2][:, kk, job[2], q * CH:(q + 1) * CH],
                                                    wv[:, kk, :], start=(kk == 0), stop=(kk == KC - 1))
                else:
                    c = job[2]
                    pe.wait_ge(low_ready, i + 1)
                    last = nc.tensor.matmul(o[:], dw2[:, c * P:(c + 1) * P], dlow[:], start=True, stop=True)
                last.then_inc(done[n % BANKS], 1)

        @block.scalar
        def _(act):

            def token_columns(i):
                for b in range(B):
                    arrived(act, ("turn", i, b))
                    nc.scalar.activation(t["qT"][:, :, b, 1 + i * W:1 + (i + 1) * W],
                                         bank(("turn", i, b))[:].rearrange("p (k w) -> p k w", w=W), ACT.Copy,
                                         scale=1.0 / 3.0).then_inc(q_ready, 1)

            token_columns(0)
            act.wait_ge(vec_turned, 1)
            nc.scalar.activation(vec[:], pv[:, 0:len(names) * KC], ACT.Copy).then_inc(vec_ready, 1)
            act.wait_ge(vec_ready, 1)
            for i in range(NI + 1):
                if i < NI:
                    arrived(act, ("mix", i))
                    nc.scalar.activation(mix[i % 2][:], bank(("mix", i))[:], ACT.Tanh).then_inc(mix_ready, 1)
                if i == 0:
                    token_columns(1)
                    continue
                g = i - 1
                for x, store in (("r", t["r_all"]), ("k", t["k_all"])):
                    for c in range(KC):
                        arrived(act, (x, g, c))
                        nc.scalar.activation(chunks_of(store, g, c),
                                             bank((x, g, c))[:].rearrange("p (b j x) -> p b j x", b=B, x=CH),
                                             ACT.Copy).then_inc(rk_ready, 1)
                if i + 1 < NI:
                    token_columns(i + 1)
                arrived(act, ("low", g))
                nc.scalar.activation(dlow[:], bank(("low", g))[0:DEC, :], ACT.Tanh).then_inc(low_ready, 1)
                if g:
                    act.wait_ge(w_ready, 2 * g)
                for c in range(KC):
                    arrived(act, ("dec", g, c))
                    nc.scalar.activation(rate[:, c, :], bank(("dec", g, c))[:], ACT.Exp,
                                         bias=col("decay", c)).then_inc(rate_ready, 1)
                for c in range(KC):
                    act.wait_ge(rate_ready, 2 * g + c + 1)
                    nc.scalar.activation(chunks_of(t["w_all"], g, c),
                                         rate[:, c, :].rearrange("p (b j x) -> p b j x", b=B, x=CH),
                                         ACT.Exp, scale=-1.0).then_inc(w_ready, 1)

        @block.gpsimd
        def _(pool):
            def gather(i):
                for q in range(B * TB):
                    tile = tile_of(i, q)
                    if i:
                        pool.wait_ge(sum_step, 2 * (B * TB * (i - 1) + q) + 2)
                    for k in range(2):
                        pool.indirect_dma_start(gb[q][:, k, :], None, d["outs1"],
                                                bass.IndirectOffsetOnAxis(t["a_row"][:, k, tile:tile + 1], 0)).then_inc(got[q], 16)

            gather(0)
            for n, name in enumerate(names):
                src = d[name].rearrange("h i -> (h i)") if name == "faaaa" else d[name]
                pool.dma_start(vec_rows[n * KC:(n + 1) * KC, :], src.rearrange("(k p) -> k p", p=P)).then_inc(vec_in, 16)
            gather(1)
            for i in range(NI):
                for f in SHIFT_ORDER:
                    pool.wait_ge(moved, 8 * i + 2 * f + 2)
                    if f == 3:
                        pool.wait_ge(moved, 8 * i + 8)
                    s = shifted[i % 2][f][:].rearrange("p k b w -> p (k b) w")
                    nc.gpsimd.tensor_tensor(s, s, token_cols(i, 0), ALU.add).then_inc(shifted_ready, 1)
                if i + 2 < NI:
                    gather(i + 2)

        @block.vector
        def _(dve):
            nc.vector.memset(t["qT"][:, :, :, 0:1], 0.0).then_inc(zeroed, 1)
            dve.wait_ge(zeroed, 1)

            def sums(i):
                for q in range(B * TB):
                    tile, n = tile_of(i, q), B * TB * i + q
                    dve.wait_ge(got[q], 32 * (i + 1))
                    if i:
                        arrived(dve, ("turn", i - 1, q // TB))
                    nc.vector.scalar_tensor_tensor(res[q][:], gb[q][:, 0, :], t["a_gate"][:, 0, tile:tile + 1],
                                                   t["acc"][:, tile, :], ALU.mult, ALU.add).then_inc(sum_step, 1)
                    dve.wait_ge(sum_step, 2 * n + 1)
                    nc.vector.scalar_tensor_tensor(res[q][:], gb[q][:, 1, :], t["a_gate"][:, 1, tile:tile + 1],
                                                   res[q][:], ALU.mult, ALU.add).then_inc(sum_step, 1)

            def differences(i):
                dve.wait_ge(q_ready, B * (i + 1))
                nc.vector.tensor_tensor(xx[i % 2][:].rearrange("p k b w -> p (k b) w"), token_cols(i, 1), token_cols(i, 0),
                                        ALU.subtract).then_inc(diff_ready, 1)
                dve.wait_ge(diff_ready, i + 1)
                if i:
                    arrived(dve, ("mix", i - 1))
                for c in range(KC):
                    last = nc.vector.scalar_tensor_tensor(xxx[:, c], xx[i % 2][:, c], col("maa_x", c),
                                                          t["qT"][:, c, :, 1 + i * W:1 + (i + 1) * W], ALU.mult, ALU.add)
                last.then_inc(xxx_ready, 1)

            def values(g):
                for b in range(B):
                    arrived(dve, ("v", g, b))
                    nc.vector.tensor_copy(t["v_all"][:, g * (W // CH):(g + 1) * (W // CH), b, :],
                                          bank(("v", g, b))[:].rearrange("p (j c) -> p j c", c=D)).then_inc(v_ready, 1)

            sums(0)
            dve.wait_ge(vec_ready, 1)
            differences(0)
            for i in range(NI):
                if i + 1 < NI:
                    sums(i + 1)
                for f in range(4):
                    for c in range(KC):
                        arrived(dve, ("shift", i, f, c))
                        nc.vector.scalar_tensor_tensor(shifted[i % 2][f][:, c].rearrange("p b w -> p (b w)"),
                                                       bank(("shift", i, f, c))[:], col(names[1 + f], c),
                                                       xx[i % 2][:, c].rearrange("p b w -> p (b w)"),
                                                       ALU.add, ALU.mult).then_inc(moved, 1)
                if i + 1 < NI:
                    differences(i + 1)
                if i:
                    values(i - 1)
            values(NI - 1)


def recurrence(nc, d, t):
    NJ = SEQ // CH
    COLS = KC * B * CH
    with ExitStack() as ctx:
        def sb(name, shape, dt=F32):
            return ctx.enter_context(nc.sbuf_tensor(name, shape, dt))

        def two(name, shape):
            return [sb(f"{name}_{i}", shape) for i in range(2)]

        def ps(name, shape, dt=F32):
            return ctx.enter_context(nc.psum_tensor(name, shape, dt))

        def sem(name):
            return ctx.enter_context(nc.semaphore(name))

        wo = sb("wo", [P, KC, D])
        bonus_sel = sb("bonus_sel", [P, KC, HEADS])
        pick = t["pick"]
        r, k, v = two("r", [P, COLS]), two("k", [P, COLS]), two("v", [P, B, D])
        rk, rfull, kfull = two("rk", [P, COLS]), two("rfull", [P, COLS]), two("kfull", [P, COLS])
        rp = [two(f"rp{l}", [P, KC * B, 2, CH // 2]) for l in range(LEVELS)]
        rd = [sb(f"rd{l}", [P, COLS // 2]) if l else None for l in range(LEVELS)]
        kq = [two(f"kq{l}", [P, COLS]) if l else k for l in range(LEVELS)]
        pre, suf = sb("pre", [P, COLS]), sb("suf", [P, COLS])
        tot = [None] + [two(f"tot{l}", [P, COLS >> l]) for l in range(1, LEVELS)] + [[sb("tot_new", [P, COLS // CH])] * 2]
        decay = two("decay", [P, COLS // CH])
        A = two("A", [P, HEADS, CH])
        kt = sb("kt", [P, KC, P])
        state = sb("state", [P, B, KC, 2 * HD])
        y0, y1, yn = two("y0", [P, D]), two("y1", [P, D]), two("yn", [P, D])
        stats, aggr = sb("stats", [P, HEADS, 6]), two("aggr", [P, HEADS, 2])
        dev, inv, off = two("dev", [P, HEADS]), two("inv", [P, HEADS]), two("off", [P, HEADS])
        ynT = sb("ynT", [P, KC, P])
        eps = sb("eps", [P, 1])

        PAIRS = (LEVELS + 1) // 2
        pa = ps("pa", [P, PAIRS, 2, HEADS * CH // 2])
        py = ps("py", [P, 512])
        pk, pu, pz = ps("pk", [P, 512]), ps("pu", [P, 512]), ps("pz", [P, 2, D])

        wo_in, zeroed, consts, dve_step, pool_step = sem("wo_in"), sem("wkv_zeroed"), sem("wkv_consts"), sem("dve_step"), sem("pool_step")
        local_ready, tot_ready, pre_ready, left_ready, right_ready = (
            sem("local_ready"), sem("tot_ready"), sem("pre_ready"), sem("left_ready"), sem("right_ready"))
        weights_done, weights_seen, picked, k_turned, kt_ready, state_inc, state_ready = (
            sem("weights_done"), sem("weights_seen"), sem("picked"), sem("k_turned"), sem("kt_ready"), sem("state_inc"),
            sem("state_ready"))
        y_done, y_taken, var_ready, dev_ready, off_ready, yn_ready, yn_turned, ynT_ready, o_done, o_taken = (
            sem("y_done"), sem("y_taken"), sem("var_ready"), sem("dev_ready"), sem("off_ready"), sem("yn_ready"),
            sem("yn_turned"), sem("ynT_ready"), sem("o_done"), sem("o_taken"))
        dense_ready, spread_ready, v_local = sem("dense_ready"), sem("spread_ready"), sem("v_local")
        wait_seen, state_zeroed, keys_zeroed = sem("wait_seen"), sem("state_zeroed"), sem("keys_zeroed")
        block = ctx.enter_context(nc.Block())
        vec, LNW, LNB, BON = t["vec"], 6, 7, 8

        def half(ap, m, side):
            return ap.rearrange("p (n s m) -> p n s m", s=2, m=m)[:, :, side, :]

        def even_odd(ap, side):
            return ap.rearrange("p (n s) -> p n s", s=2)[:, :, side]

        def spread(ap, m):
            return ap.unsqueeze(2).to_broadcast([P, COLS // (2 * m), m])

        def chunk(ap, j):
            return ap[:, bass.ds(j, 1)]

        def each_step(eng, step):
            step(0, 0, True, False)
            with eng.Fori(0, (NJ - 2) // 2) as i:
                step(2 * i + 1, 1, False, False)
                step(2 * i + 2, 0, False, False)
            step(NJ - 1, (NJ - 1) % 2, False, True)

        @block.sync
        def _(sp):
            sp.dma_start(wo[:], d["W_o"].rearrange("(k p) n -> p k n", p=P)).then_inc(wo_in, 16)
            cw, done = t["cw"], t["cw"]["loads_in"]
            for name, src in (("wp", "W_proj"), ("wm", "weight_matrix"), ("wr", "Wr")):
                sp.dma_start(cw[name][:], d[src].rearrange("(k p) n -> p k n", p=P)).then_inc(done, 16)
            sp.dma_start(cw["br"][:], d["br"].unsqueeze(0).to_broadcast([P, E2])).then_inc(done, 16)
            with nc.allow_non_contiguous_dma(reason="768 values, once"):
                for b in range(B):
                    sp.dma_start(cw["cond_col"][:, :, b], d["cond"][b].rearrange("(k p) -> p k", p=P)).then_inc(done, 16)
                sp.dma_start(cw["bp_col"][:], d["b_proj"].rearrange("(k p) -> p k", p=P)).then_inc(done, 16)

        @block.tensor
        def _(pe):
            def weigh(j, par, b):
                n = 2 * j + b
                for l in range(LEVELS):
                    if b == 0 and l == 0:
                        pe.wait_ge(local_ready, j + 1)
                    if b == 0 and l:
                        pe.wait_ge(left_ready, LEVELS * j + l)
                        pe.wait_ge(spread_ready, (LEVELS - 1) * j + l)
                    if l % 2 == 0 and not (isinstance(n, int) and n == 0):
                        pe.wait_ge(picked, (n - 1) * PAIRS + l // 2 + 1)
                    for c in range(KC):
                        first = (c * B + b) * CH
                        last = nc.tensor.matmul(pa[:, l // 2, l % 2, c * CH:(c + 1) * CH], kq[l][par][:, first:first + CH],
                                                rp[l][par][:, c * B + b].rearrange("p h n -> p (h n)"),
                                                start=True, stop=True)
                    if l % 2 or l == LEVELS - 1:
                        last.then_inc(weights_done, 1)

            def turn_keys(j, par, b):
                if b == 0:
                    pe.wait_ge(left_ready, LEVELS * j + LEVELS)
                for c in range(KC):
                    first = (c * B + b) * CH
                    last = nc.tensor.transpose(pk[:, c * P:(c + 1) * P], kfull[par][:, first:first + CH], t["ident"][:])
                last.then_inc(k_turned, 1)

            def outputs(j, par, b):
                n = 2 * j + b
                if b == 0:
                    pe.wait_ge(right_ready, j + 1)
                    pe.wait_ge(v_local, j + 1)
                pe.wait_ge(picked, n * PAIRS + PAIRS)
                if not (isinstance(n, int) and n == 0):
                    pe.wait_ge(y_taken, n)
                    pe.wait_ge(state_ready, n)
                for c in range(KC):
                    first = (c * B + b) * CH
                    nc.tensor.matmul(py[:, c * P:(c + 1) * P], rfull[par][:, first:first + CH], state[:, b, c, :],
                                     start=True, stop=True)
                    for h in range(2):
                        hc = slice((2 * c + h) * HD, (2 * c + h + 1) * HD)
                        nc.tensor.matmul(py[:, hc], A[b][:, 2 * c + h, :], v[par][:, b, hc],
                                         start=False, stop=True, skip_group_check=True)
                for c in range(KC):
                    first = (c * B + b) * CH
                    last = nc.tensor.matmul(py[:, D:D + HEADS], rk[par][:, first:first + CH], bonus_sel[:, c, :],
                                            start=(c == 0), stop=(c == KC - 1))
                last.then_inc(y_done, 1)
                pe.wait_ge(kt_ready, n + 1)
                for c in range(KC):
                    last = nc.tensor.matmul(pu[:, c * P:(c + 1) * P], kt[:, c, :], v[par][:, b, c * P:(c + 1) * P],
                                            start=True, stop=True)
                last.then_inc(state_inc, 1)

            def project(n, par):
                pe.wait_ge(yn_ready, n + 1)
                if not (isinstance(n, int) and n == 0):
                    pe.wait_ge(o_taken, n)
                for kk in range(KC):
                    last = nc.tensor.transpose(pz[:, 0, kk * P:(kk + 1) * P], yn[par][:, kk * P:(kk + 1) * P], t["ident"][:])
                last.then_inc(yn_turned, 1)
                pe.wait_ge(ynT_ready, n + 1)
                for kk in range(KC):
                    last = nc.tensor.matmul(pz[:, 1, :], ynT[:, kk, :], wo[:, kk, :], start=(kk == 0), stop=(kk == KC - 1))
                last.then_inc(o_done, 1)

            pe.wait_ge(wo_in, 16)
            pe.wait_ge(consts, 1)

            def step(j, par, first, last):
                for b in range(B):
                    if not first:
                        project(2 * j + b - 2, b)
                    turn_keys(j, par, b)
                    if b == 0:
                        weigh(j, par, 1)
                    elif not last:
                        weigh(j + 1, 1 - par, 0)
                    outputs(j, par, b)
                if last:
                    for b in range(B):
                        project(2 * j + b, b)

            weigh(0, 0, 0)

            each_step(pe, step)

        @block.scalar
        def _(act):
            def local(j, par):
                jj = chunk(t["r_all"], j), chunk(t["k_all"], j)
                for h in range(2):
                    hs = slice(HD * h, HD * h + HD)
                    nc.scalar.activation(rp[0][par][hs, :, h, :],
                                         jj[0][hs].rearrange("p j k b (n s) -> p (j k b) n s", s=2)[:, :, :, 1], ACT.Copy)
                nc.scalar.activation(r[par][:], jj[0].rearrange("p j k b x -> p (j k b x)"), ACT.Copy)
                nc.scalar.activation(k[par][:], jj[1].rearrange("p j k b x -> p (j k b x)"),
                                     ACT.Copy).then_inc(local_ready, 1)

            def local_values(j, par):
                nc.scalar.activation(v[par][:].rearrange("p b c -> p (b c)"),
                                     chunk(t["v_all"], j).rearrange("p j b c -> p (j b c)"),
                                     ACT.Copy).then_inc(v_local, 1)

            def put_apart(j, par, l):
                act.wait_ge(dense_ready, (LEVELS - 1) * j + l)
                for h in range(2):
                    hs = slice(HD * h, HD * h + HD)
                    last = nc.scalar.activation(rp[l][par][hs, :, h, :], rd[l][hs].rearrange("p (q n) -> p q n", q=KC * B),
                                                ACT.Copy)
                last.then_inc(spread_ready, 1)

            def columns(n):
                act.wait_ge(yn_turned, n + 1)
                for kk in range(KC):
                    last = nc.scalar.activation(ynT[:, kk, :], pz[:, 0, kk * P:(kk + 1) * P], ACT.Identity,
                                                scale=vec[:, LNW * KC + kk:LNW * KC + kk + 1],
                                                bias=vec[:, LNB * KC + kk:LNB * KC + kk + 1])
                last.then_inc(ynT_ready, 1)

            def normed(n, b):
                act.wait_ge(var_ready, n + 1)
                nc.scalar.activation(dev[b][:], aggr[b][:, :, 1], ACT.Sqrt, bias=eps[:, 0:1]).then_inc(dev_ready, 1)
                act.wait_ge(off_ready, n + 1)
                for h in range(HEADS):
                    hc = slice(h * HD, (h + 1) * HD)
                    ins = nc.scalar.activation(yn[b][:, hc], y1[b][:, hc], ACT.Identity,
                                               scale=inv[b][:, h:h + 1], bias=off[b][:, h:h + 1])
                ins.then_inc(yn_ready, 1)

            def step(j, par, first, last):
                for b in range(B):
                    n, before = 2 * j + b, 1 - b
                    if b == 0 and not last:
                        if not first:
                            act.wait_ge(y_done, n - 1)
                        local(j + 1, 1 - par)
                    if not first:
                        columns(n - 2)
                    act.wait_ge(k_turned, n + 1)
                    nc.scalar.activation(kt[:].rearrange("p k n -> p (k n)"), pk[:, 0:D], ACT.Copy).then_inc(kt_ready, 1)
                    if b == 1 and not last:
                        for l in (2, 3):
                            put_apart(j + 1, 1 - par, l)
                    if not (first and b == 0):
                        normed(n - 1, before)
                    if b == 0 and not last:
                        if not first:
                            act.wait_ge(y_taken, n)
                        local_values(j + 1, 1 - par)
                        put_apart(j + 1, 1 - par, 1)
                    if b == 1 and not last:
                        for l in range(4, LEVELS):
                            put_apart(j + 1, 1 - par, l)
                if last:
                    columns(2 * j)
                    normed(2 * j + 1, 1)
                    columns(2 * j + 1)

            act.wait_ge(state_zeroed, 1)
            for l in range(LEVELS):
                nc.scalar.activation(rp[l][1][:].rearrange("p q h n -> p (q h n)"),
                                     state[:].rearrange("p b k n -> p (b k n)"), ACT.Copy)
            act.wait_ge(zeroed, 1)
            local(0, 0)
            local_values(0, 0)
            for l in range(1, LEVELS):
                put_apart(0, 0, l)
            each_step(act, step)

        @block.gpsimd
        def _(pool):
            steps = [0]
            nc.gpsimd.memset(bonus_sel[:], 0.0).then_inc(pool_step, 1)
            steps[0] += 1
            pool.wait_ge(pool_step, steps[0])
            for c in range(KC):
                for h in range(2):
                    hs = slice(HD * h, HD * h + HD)
                    nc.gpsimd.tensor_copy(bonus_sel[hs, c, 2 * c + h:2 * c + h + 1],
                                          vec[hs, BON * KC + c:BON * KC + c + 1]).then_inc(pool_step, 1)
                    steps[0] += 1
                    pool.wait_ge(pool_step, steps[0])
            pool.sem_inc(consts, 1)
            pool.wait_ge(keys_zeroed, 1)

            def left(j, par):
                pool.sem_clear(pool_step)
                done = [0]

                def link(ins):
                    done[0] += 1
                    ins.then_inc(pool_step, 1)
                    pool.wait_ge(pool_step, done[0])

                w = chunk(t["w_all"], j).rearrange("p j k b x -> p (j k b x)")
                pool.wait_ge(local_ready, j + 1)
                link(nc.gpsimd.tensor_copy(half(suf[:], 1, 0), half(w, 1, 1)))
                pool.wait_ge(tot_ready, j + 1)
                for l in range(1, LEVELS):
                    m = 1 << l
                    link(nc.gpsimd.tensor_tensor(half(kq[l][par][:], m, 0), half(k[par][:], m, 0), half(suf[:], m, 0), ALU.mult))
                    pool.sem_inc(left_ready, 1)
                    link(nc.gpsimd.tensor_tensor(half(suf[:], m, 0), half(suf[:], m, 0),
                                                 spread(even_odd(tot[l][par][:], 1), m), ALU.mult))
                if not (isinstance(j, int) and j < 2):
                    pool.wait_ge(y_done, 2 * (j - 1))
                    pool.sem_inc(wait_seen, 1)
                link(nc.gpsimd.tensor_tensor(kfull[par][:], k[par][:], suf[:], ALU.mult))
                pool.sem_inc(left_ready, 1)
                pool.wait_ge(pre_ready, j + 1)
                nc.gpsimd.tensor_tensor(rk[par][:], r[par][:], k[par][:], ALU.mult)
                link(nc.gpsimd.tensor_tensor(rfull[par][:], r[par][:], pre[:], ALU.mult))
                link(nc.gpsimd.memset(half(suf[:], 1, 1), 1.0))
                pool.sem_inc(right_ready, 1)

            nc.gpsimd.memset(half(suf[:], 1, 1), 1.0)
            left(0, 0)

            def step(j, par, first, last):
                if not last:
                    if not first:
                        pool.wait_ge(y_done, 2 * j - 1)
                    pool.sem_inc(wait_seen, 1)
                    left(j + 1, 1 - par)

            each_step(pool, step)

        @block.vector
        def _(dve):
            done = [0]

            def link(ins):
                done[0] += 1
                ins.then_inc(dve_step, 1)
                dve.wait_ge(dve_step, done[0])

            def count(ins):
                done[0] += 1
                ins.then_inc(dve_step, 1)
                return done[0]

            def need(n):
                dve.wait_ge(dve_step, n)

            def whole(j, par, l):
                src = chunk(t["w_all"], j).rearrange("p j k b x -> p (j k b x)") if l == 0 else tot[l][par][:]
                return count(nc.vector.tensor_tensor(tot[l + 1][par][:], even_odd(src, 0), even_odd(src, 1), ALU.mult))

            def start_right(j):
                w = chunk(t["w_all"], j).rearrange("p j k b x -> p (j k b x)")
                if not (isinstance(j, int) and j == 0):
                    dve.wait_ge(right_ready, j)
                nc.vector.memset(half(pre[:], 1, 0), 1.0)
                return count(nc.vector.tensor_copy(half(pre[:], 1, 1), half(w, 1, 0)))

            def receive(par, l):
                m = 1 << l
                return count(nc.vector.tensor_tensor(rd[l][:].rearrange("p (n m) -> p n m", m=m), half(r[par][:], m, 1),
                                                     half(pre[:], m, 1), ALU.mult))

            def extend(par, l):
                m = 1 << l
                return count(nc.vector.tensor_tensor(half(pre[:], m, 1), half(pre[:], m, 1),
                                                     spread(even_odd(tot[l][par][:], 0), m), ALU.mult))

            def level(par, l):
                need(receive(par, l))
                dve.sem_inc(dense_ready, 1)
                need(extend(par, l))

            def choose(n, b, l):
                if l == 0 and not (isinstance(n, int) and n < 2):
                    dve.wait_ge(y_done, n - 1)
                if l % 2 == 0:
                    dve.wait_ge(weights_done, n * PAIRS + l // 2 + 1)
                    dve.sem_inc(weights_seen, 1)
                m = 1 << l
                return count(nc.vector.copy_predicated(
                    A[b][:].rearrange("p h (n s m) -> p h n s m", s=2, m=m)[:, :, :, 1, :],
                    pick[:, l, :].bitcast(I32).rearrange("p (n m) -> p n m", m=m).unsqueeze(1).to_broadcast(
                        [P, HEADS, CH // 2 // m, m]),
                    pa[:, l // 2, l % 2].rearrange("p (h n m) -> p h n m", h=HEADS, m=m)))

            def chosen(l, at):
                need(at)
                if l % 2 or l == LEVELS - 1:
                    dve.sem_inc(picked, 1)

            def advance(par, b, c):
                for h in range(2):
                    hs = slice(HD * h, HD * h + HD)
                    own = state[hs, b, c, HD * h:HD * h + HD]
                    last = nc.vector.scalar_tensor_tensor(own, own, decay[par][hs, c * B + b:c * B + b + 1],
                                                          pu[hs, c * P + HD * h:c * P + HD * h + HD], ALU.mult, ALU.add)
                return last

            def moments(n, par, b):
                dve.wait_ge(y_done, n + 1)
                heads = [P, HEADS, HD]
                own = count(nc.vector.tensor_tensor(y0[b][:].rearrange("p (h j) -> p h j", j=HD),
                                                    v[par][:, b, :].rearrange("p (h j) -> p h j", j=HD),
                                                    py[:, D:D + HEADS].unsqueeze(2).to_broadcast(heads), ALU.mult))
                dve.wait_ge(state_inc, n + 1)
                advance(par, b, 0)
                need(own)
                y = count(nc.vector.tensor_tensor(y1[b][:], y0[b][:], py[:, 0:D], ALU.add))
                advance(par, b, 1).then_inc(state_ready, 1)
                need(y)
                dve.sem_inc(y_taken, 1)
                for h in range(HEADS):
                    last = nc.vector.bn_stats(stats[:, h, :], y1[b][:, h * HD:(h + 1) * HD])
                need(count(last))
                for h in range(HEADS):
                    last = nc.vector.bn_aggr(aggr[b][:, h, :], stats[:, h, :])
                last.then_inc(var_ready, 1)

            def offsets(n, b):
                dve.wait_ge(dev_ready, n + 1)
                link(nc.vector.reciprocal(inv[b][:], dev[b][:]))
                nc.vector.scalar_tensor_tensor(off[b][:], aggr[b][:, :, 0], -1.0, inv[b][:], ALU.mult,
                                               ALU.mult).then_inc(off_ready, 1)

            def residual(n, j, b):
                dve.wait_ge(o_done, n + 1)
                at = t["x_tok"][:, bass.ds(b * (NT // B) + j, 1), :].rearrange("p t c -> p (t c)")
                nc.vector.tensor_tensor(at, at, pz[:, 1, :], ALU.add).then_inc(o_taken, 1)

            nc.vector.memset(state[:], 0.0).then_inc(state_zeroed, 1)
            for l in range(1, LEVELS):
                for par in range(2):
                    last = nc.vector.memset(half(kq[l][par][:], 1 << l, 1), 0.0)
            last.then_inc(keys_zeroed, 1)
            for l in range(LEVELS):
                need(whole(0, 0, l))
            dve.sem_inc(tot_ready, 1)
            need(count(nc.vector.tensor_copy(decay[0][:], tot[LEVELS][0][:])))
            for l in range(LEVELS):
                nc.vector.memset(rp[l][0][:], 0.0)
            nc.vector.memset(eps[:], LN_EPS)
            nc.vector.memset(A[1][:], 0.0)
            nc.vector.memset(A[0][:], 0.0).then_inc(zeroed, 1)
            dve.wait_ge(zeroed, 1)
            dve.wait_ge(consts, 1)
            def residual_and_offsets(n, j, b, first):
                if not first:
                    residual(n - 1, j if b else j - 1, 1 - b)
                offsets(n, b)

            need(start_right(0))
            dve.wait_ge(local_ready, 1)
            for l in range(1, LEVELS):
                level(0, l)
            dve.sem_inc(pre_ready, 1)

            def step(j, par, first, last):
                dve.sem_clear(dve_step)
                done[0] = 0
                n, after = 2 * j, 1 - par
                for l in range(LEVELS):
                    at = choose(n, 0, l)
                    if not last:
                        block_done = whole(j + 1, after, l)
                    chosen(l, at)
                    if not last:
                        need(block_done)
                if not last:
                    dve.sem_inc(tot_ready, 1)
                if not first:
                    moments(n - 1, after, 1)
                    residual_and_offsets(n - 1, j - 1, 1, first=False)
                if not last:
                    need(count(nc.vector.tensor_copy(decay[after][:], tot[LEVELS][after][:])))
                    need(start_right(j + 1))
                    dve.wait_ge(local_ready, j + 2)
                    dve.wait_ge(spread_ready, (LEVELS - 1) * (j + 1))
                    level(after, 1)
                n = 2 * j + 1
                for l in range(LEVELS):
                    at = choose(n, 1, l)
                    if not last and l < 4:
                        part = extend(after, 2 + l // 2) if l % 2 else receive(after, 2 + l // 2)
                    chosen(l, at)
                    if not last and l < 4:
                        need(part)
                        if l % 2 == 0:
                            dve.sem_inc(dense_ready, 1)
                moments(n - 1, par, 0)
                residual_and_offsets(n - 1, j, 0, first=first)
                if not last:
                    for l in range(4, LEVELS):
                        level(after, l)
                    dve.sem_inc(pre_ready, 1)
                if last:
                    moments(n, par, 1)
                    residual_and_offsets(n, j, 1, first=False)
                    residual(n, j, 1)

            each_step(dve, step)


def condition(nc, d, t):
    with ExitStack() as ctx:
        def sb(name, shape, dt=F32):
            return ctx.enter_context(nc.sbuf_tensor("c_" + name, shape, dt))

        def ps(name, shape, dt=F32):
            return ctx.enter_context(nc.psum_tensor("c_" + name, shape, dt))

        def sem(name):
            return ctx.enter_context(nc.semaphore("c_" + name))

        wp, wm, wr, br, cond_col, bp_col, loads_in = (
            t["cw"][n] for n in ("wp", "wm", "wr", "br", "cond_col", "bp_col", "loads_in"))
        u_col, u_rep, u_row = sb("u_col", [P, KC, B]), sb("u_rep", [P, KC, B, P]), sb("u_row", [P, B, D])
        xT, hT = ([sb(f"{n}{i}", [P, KC, GT * P]) for i in range(2)] for n in ("xT", "hT"))
        logits, top, total = sb("logits", [P, NT, E2]), sb("top", [P, NT]), sb("total", [P, NT])
        xp, hp, tp = ps("xp", [P, KC, GT * P]), ps("hp", [P, GT, D]), ps("tp", [P, KC, GT * P])
        rp, up = ps("rp", [P, 512]), ps("up", [P, 512])
        rp_t = rp[:, 0:NT * E2].rearrange("p (t e) -> p t e", e=E2)
        u_sum, u_ready, rep_ready, urow_done, urow_ready = (
            sem("u_sum"), sem("u_ready"), sem("rep_ready"), sem("urow_done"), sem("urow_ready"))
        h_stored = sem("h_stored")
        x_turned, xT_ready, h_done, h_ready, h_turned, hT_ready, r_done, step_done, exp_done = (
            sem("x_turned"), sem("xT_ready"), sem("h_done"), sem("h_ready"), sem("h_turned"), sem("hT_ready"),
            sem("r_done"), sem("step_done"), sem("exp_done"))
        block = ctx.enter_context(nc.Block())

        @block.sync
        def _(sp):
            for g in range(NG):
                sp.wait_ge(h_ready, g + 1)
                sp.dma_start(d["tokens2"].rearrange("(t p) c -> p t c", p=P)[:, g * GT:(g + 1) * GT, :],
                             t["acc"][:, g * GT:(g + 1) * GT, :]).then_inc(h_stored, 16)
            sp.wait_ge(h_stored, 16 * NG)

        @block.tensor
        def _(pe):
            def turn(out, src, g):
                for tt in range(GT):
                    for k in range(KC):
                        last = nc.tensor.transpose(out[:, k, tt * P:(tt + 1) * P],
                                                   src[:, g * GT + tt, k * P:(k + 1) * P], t["ident"][:])
                return last

            def turn_x(g):
                if g:
                    pe.wait_ge(xT_ready, g)
                turn(xp, t["x_tok"], g).then_inc(x_turned, 1)

            turn_x(0)
            pe.wait_ge(loads_in, 16 * 7)
            for c in range(KC):
                for k in range(KC):
                    last = nc.tensor.matmul(up[:, c * B:(c + 1) * B], wp[:, k, c * P:(c + 1) * P], cond_col[:, k, :],
                                            start=(k == 0), stop=(k == KC - 1))
            last.then_inc(u_sum, 1)
            for g in range(NG + 1):
                if g:
                    pe.wait_ge(h_ready, g)
                    if g >= 2:
                        pe.wait_ge(hT_ready, g - 1)
                    turn(tp, t["acc"], g - 1).then_inc(h_turned, 1)
                if g < NG:
                    pe.wait_ge(xT_ready, g + 1)
                    for tt in range(GT):
                        for k in range(KC):
                            last = nc.tensor.matmul(hp[:, tt, :], xT[g % 2][:, k, tt * P:(tt + 1) * P], wm[:, KC + k, :],
                                                    start=(k == 0), stop=(k == KC - 1))
                    last.then_inc(h_done, 1)
                if g == 0:
                    pe.wait_ge(rep_ready, 1)
                    for b in range(B):
                        for k in range(KC):
                            last = nc.tensor.matmul(up[:, b * D:(b + 1) * D], u_rep[:, k, b, :], wm[:, k, :],
                                                    start=(k == 0), stop=(k == KC - 1))
                    last.then_inc(urow_done, 1)
                if g + 1 < NG:
                    turn_x(g + 1)
                if g:
                    pe.wait_ge(hT_ready, g)
                    for tt in range(GT):
                        for k in range(KC):
                            last = nc.tensor.matmul(rp_t[:, (g - 1) * GT + tt, :], hT[(g - 1) % 2][:, k, tt * P:(tt + 1) * P],
                                                    wr[:, k, :], start=(k == 0), stop=(k == KC - 1))
                    last.then_inc(r_done, 1)

        @block.scalar
        def _(act):
            def columns(out, src, ready, g):
                for k in range(KC):
                    last = nc.scalar.activation(out[g % 2][:, k, :], src[:, k, :], ACT.Copy)
                last.then_inc(ready, 1)

            act.wait_ge(x_turned, 1)
            columns(xT, xp, xT_ready, 0)
            act.wait_ge(u_sum, 1)
            act.wait_ge(loads_in, 16 * 7)
            for c in range(KC):
                last = nc.scalar.activation(u_col[:, c, :], up[:, c * B:(c + 1) * B], ACT.Gelu, bias=bp_col[:, c:c + 1])
            last.then_inc(u_ready, 1)
            act.wait_ge(u_ready, 1)
            for k in range(KC):
                for b in range(B):
                    last = nc.scalar.activation(u_rep[:, k, b, :], u_col[:, k, b:b + 1].to_broadcast([P, P]), ACT.Copy)
            last.then_inc(rep_ready, 1)
            for g in range(NG):
                if g + 1 < NG:
                    act.wait_ge(x_turned, g + 2)
                    if g >= 1:
                        act.wait_ge(h_done, g)
                    columns(xT, xp, xT_ready, g + 1)
                act.wait_ge(h_turned, g + 1)
                if g >= 2:
                    act.wait_ge(r_done, g - 1)
                columns(hT, tp, hT_ready, g)
            act.wait_ge(step_done, 3)
            nc.scalar.activation(logits[:], logits[:], ACT.Exp).then_inc(exp_done, 1)

        @block.vector
        def _(dve):
            dve.wait_ge(urow_done, 1)
            nc.vector.tensor_copy(u_row[:].rearrange("p b c -> p (b c)"), up[:]).then_inc(urow_ready, 1)
            dve.wait_ge(urow_ready, 1)
            for g in range(NG):
                b = g // (NG // B)
                dve.wait_ge(h_done, g + 1)
                nc.vector.tensor_tensor(t["acc"][:, g * GT:(g + 1) * GT, :], hp[:],
                                        u_row[:, b:b + 1, :].to_broadcast([P, GT, D]), ALU.add).then_inc(h_ready, 1)
            wide = [P, NT, E2]
            dve.wait_ge(loads_in, 16 * 7)
            dve.wait_ge(r_done, NG)
            nc.vector.tensor_tensor(logits[:], rp_t, br[:].unsqueeze(1).to_broadcast(wide), ALU.add).then_inc(step_done, 1)
            dve.wait_ge(step_done, 1)
            nc.vector.tensor_reduce(top[:], logits[:], AX.X, ALU.max).then_inc(step_done, 1)
            dve.wait_ge(step_done, 2)
            nc.vector.tensor_tensor(logits[:], logits[:], top[:].unsqueeze(2).to_broadcast(wide),
                                    ALU.subtract).then_inc(step_done, 1)
            dve.wait_ge(exp_done, 1)
            nc.vector.tensor_reduce(total[:], logits[:], AX.X, ALU.add).then_inc(step_done, 1)
            dve.wait_ge(step_done, 4)
            nc.vector.reciprocal(total[:], total[:]).then_inc(step_done, 1)
            dve.wait_ge(step_done, 5)
            nc.vector.tensor_tensor(t["score2"][:], logits[:], total[:].unsqueeze(2).to_broadcast(wide),
                                    ALU.mult).then_inc(step_done, 1)
            dve.wait_ge(step_done, 6)
            nc.vector.tensor_copy(t["sel2"][:], t["score2"][:])


def constants(nc, t):
    with nc.semaphore("filled") as filled, nc.Block() as block:
        t["used"].append(filled)
        @block.gpsimd
        def _(pool):
            nc.gpsimd.memset(t["ident"][:], 0.0)
            nc.gpsimd.memset(t["ones"][:], 1.0)
            nc.gpsimd.memset(t["before"][:], 1.0).then_inc(filled, 1)
            nc.gpsimd.iota(t["first1"][:], [[0, NT], [-1, E1]], base=E1, channel_multiplier=0,
                           allow_small_or_imprecise_dtypes=True)
            nc.gpsimd.iota(t["first2"][:], [[0, NT], [-1, E2]], base=E2, channel_multiplier=0,
                           allow_small_or_imprecise_dtypes=True)
            nc.gpsimd.iota(t["slot_no"][:], [[1, S2], [0, E2]], base=0, channel_multiplier=0,
                           allow_small_or_imprecise_dtypes=True)
            nc.gpsimd.iota(t["token_no"][:], [[P, NT]], base=0, channel_multiplier=1,
                           allow_small_or_imprecise_dtypes=True)
            nc.gpsimd.iota(t["row_no"][:], [[1, P]], base=0, channel_multiplier=0,
                           allow_small_or_imprecise_dtypes=True)
            pool.wait_ge(filled, 1)
            nc.gpsimd.affine_select(out=t["ident"][:], in_=t["ident"][:], compare_op=ALU.not_equal, fill=1.0, base=0,
                                    pattern=[[-1, P]], channel_multiplier=1)
            nc.gpsimd.affine_select(out=t["before"][:], in_=t["before"][:], compare_op=ALU.is_ge, fill=0.0, base=-1,
                                    pattern=[[1, P]], channel_multiplier=-1)


def clear(nc, used):
    with nc.Block() as block:
        @block.gpsimd
        def _(pool):
            for sem in used:
                pool.sem_clear(sem)


def program(nc, d, out):
    with ExitStack() as ctx:
        def sb(name, shape, dt=F32):
            return ctx.enter_context(nc.sbuf_tensor(name, shape, dt))

        rows1 = nc.dram_tensor("rows1", [S1, P, D], F32, kind="Internal").ap()
        outs1 = nc.dram_tensor("outs1", [S1, P, D], F32, kind="Internal").ap()
        tokens2 = nc.dram_tensor("tokens2", [N, D], F32, kind="Internal").ap()
        outs2 = nc.dram_tensor("outs2", [S2, P, D], F32, kind="Internal").ap()
        flat = lambda a: a.rearrange("s p c -> (s p) c")
        d["rows1"], d["outs1"], d["tokens2"] = flat(rows1), flat(outs1), tokens2
        out_tiles = out.rearrange("b (t p) c -> p (b t) c", p=P)
        t = {
            "used": [],
            "rows_out": ctx.enter_context(nc.semaphore("rows_out")),
            "ident": sb("ident", [P, P]), "ones": sb("ones", [P, P]), "before": sb("before", [P, P]),
            "first1": sb("first1", [P, NT, E1]), "first2": sb("first2", [P, NT, E2]),
            "slot_no": sb("slot_no", [P, S2, E2]),
            "score1": sb("score1", [P, NT, E1]), "sel1": sb("sel1", [P, NT, E1]),
            "score2": sb("score2", [P, NT, E2]), "sel2": sb("sel2", [P, NT, E2]),
            "a_gate": sb("a_gate", [P, 2, NT]), "a_row": sb("a_row", [P, 2, NT], U32), "a_owner": sb("a_owner", [P, S1], I32),
            "b_gate": sb("b_gate", [P, 2, NT]), "b_row": sb("b_row", [P, 2, NT], U32), "b_owner": sb("b_owner", [P, S2], I32),
            "token_no": sb("token_no", [P, NT]), "row_no": sb("row_no", [P, P]), "b_token": sb("b_token", [P, S2 + RING2], U32),
            "x_tok": sb("x_tok", [P, NT, D]), "acc": sb("acc", [P, NT, D]),
            "pick": sb("pick", [P, LEVELS, CH // 2]),
            "vec": sb("vec", [P, 9 * KC]),
        }

        constants(nc, t)
        with (nc.sbuf_tensor("xT", [P, KC, N], F32) as xT, nc.sbuf_tensor("w1", [P, KC, HS], F32) as w1,
              nc.sbuf_tensor("w3", [P, KC, HS], F32) as w3, nc.sbuf_tensor("w2", [P, HS // P, D], F32) as w2,
              nc.sbuf_tensor("zero", [P, D], F32) as zero, nc.semaphore("weights_in") as weights_in,
              nc.semaphore("rows_cleared") as rows_cleared):
            t["xT"], t["w1"], t["w3"], t["w2"], t["zero"] = xT, w1, w3, w2, zero
            t["weights_in"], t["rows_cleared"] = weights_in, rows_cleared
            t["used"] += [weights_in, rows_cleared]
            router_front(nc, d, t)
            with ExitStack() as slot_ctx:
                bufs = slot_buffers(nc, slot_ctx, "a_", RING1, H1, False)
                route(nc, t, E1, S1, t["sel1"], t["score1"], t["first1"], "a_")
                shared_expert(nc, d, t,
                              lambda sp: [load_weights(nc, sp, t, bufs, "a_", b, b, d["W1e"], None, d["W2e"], None)
                                          for b in range(RING1 - 1)])
                expert_slots(nc, d, t, bufs, "a_", E1, H1, S1, rows1, outs1, d["W1e"], None, d["W2e"], None)
        with ExitStack() as cond_ctx:
            t["cw"] = {n: cond_ctx.enter_context(nc.sbuf_tensor("cw_" + n, shape, F32)) for n, shape in (
                ("wp", [P, KC, D]), ("wm", [P, 2 * KC, D]), ("wr", [P, KC, E2]), ("br", [P, E2]),
                ("cond_col", [P, KC, B]), ("bp_col", [P, KC]))}
            t["cw"]["loads_in"] = cond_ctx.enter_context(nc.semaphore("cw_loads_in"))
            chunked = [P, SEQ // CH, KC, B, CH]
            with (nc.sbuf_tensor("r_all", chunked, F32) as r_all, nc.sbuf_tensor("k_all", chunked, F32) as k_all,
                  nc.sbuf_tensor("w_all", chunked, F32) as w_all):
                t["r_all"], t["k_all"], t["w_all"] = r_all[:], k_all[:], w_all[:]
                t["v_all"] = t["acc"][:].rearrange("p (j b) c -> p j b c", b=B)
                with nc.sbuf_tensor("qT", [P, KC, B, 1 + SEQ], F32) as qT:
                    t["qT"] = qT
                    mix_and_project(nc, d, t)
                recurrence(nc, d, t)
            clear(nc, t["used"])
            condition(nc, d, t)
        with ExitStack() as slot_ctx:
            bufs = slot_buffers(nc, slot_ctx, "b_", RING2, H2, True)
            route(nc, t, E2, S2, t["sel2"], t["score2"], t["first2"], "b_",
                  lambda sp: [load_weights(nc, sp, t, bufs, "b_", b, b, d["W1"], d["b1"], d["W2"], d["b2"])
                              for b in range(RING2 - 1)])
            expert_slots(nc, d, t, bufs, "b_", E2, H2, S2, None, outs2, d["W1"], d["b1"], d["W2"], d["b2"])
        combine(nc, t, "b_", t["x_tok"], flat(outs2), out_tiles)


_NAMES = {
    "x": "x", "cond": "cond_1024", "router_W": "L0_cond_router_W", "router_bias": "L0_cond_router_bias",
    "w1": "L0_cond_w1", "w3": "L0_cond_w3", "w2": "L0_cond_w2", "W1e": "L0_cond_W1e", "W2e": "L0_cond_W2e",
    "maa_x": "L0_attn_time_maa_x", "maa_w": "L0_attn_time_maa_w", "maa_k": "L0_attn_time_maa_k",
    "maa_v": "L0_attn_time_maa_v", "maa_r": "L0_attn_time_maa_r", "maa_w1": "L0_attn_time_maa_w1",
    "maa_w2": "L0_attn_time_maa_w2", "decay": "L0_attn_time_decay", "decay_w1": "L0_attn_time_decay_w1",
    "decay_w2": "L0_attn_time_decay_w2", "faaaa": "L0_attn_time_faaaa", "W_r": "L0_attn_W_r", "W_k": "L0_attn_W_k",
    "W_v": "L0_attn_W_v", "W_o": "L0_attn_W_o", "ln_w": "L0_attn_ln_w", "ln_b": "L0_attn_ln_b",
    "weight_matrix": "L0_cond2_weight_matrix", "W_proj": "L0_cond2_W_proj", "b_proj": "L0_cond2_b_proj",
    "Wr": "L0_ffn_Wr", "br": "L0_ffn_br", "W1": "L0_ffn_W1", "b1": "L0_ffn_b1", "W2": "L0_ffn_W2", "b2": "L0_ffn_b2",
}


def kernel(**inputs):
    import numpy as np
    import concourse.bacc as bacc
    from concourse.bass_utils import run_bass_kernel_spmd

    nc = bacc.Bacc("TRN2", target_bir_lowering=False, num_devices=1)
    arrays, dram = {}, {}
    for short, name in _NAMES.items():
        a = np.ascontiguousarray(inputs[name])
        arrays[f"in_{short}"] = a
        dram[short] = nc.dram_tensor(f"in_{short}", a.shape, mybir.dt.from_np(a.dtype), kind="ExternalInput").ap()
    out = nc.dram_tensor("out_0", (B, SEQ, D), F32, kind="ExternalOutput").ap()
    program(nc, dram, out)
    r = run_bass_kernel_spmd(nc, [arrays], core_ids=[0])
    return r.results[0]["out_0"]
```
